# Optimizing a Trainium2 kernel written in Bass

```python
import numpy as np
import jax
import jax.numpy as jnp

def _softmax(x, axis=-1):
    return jax.nn.softmax(x, axis=axis)

def _gelu(x):
    return jax.nn.gelu(x, approximate=True)

def _silu(x):
    return jax.nn.silu(x)

def _sigmoid(x):
    return jax.nn.sigmoid(x)

def _layernorm(x, axis=-1, eps=1e-05):
    m = jnp.mean(x, axis=axis, keepdims=True)
    v = jnp.var(x, axis=axis, keepdims=True)
    return (x - m) / jnp.sqrt(v + eps)

def _scatter_add(tgt, idx, src, axis=0):
    return tgt.at[idx].add(src)

def _segment_sum(src, seg, n):
    return jax.ops.segment_sum(src, seg, n)
kernel_name = 'mk_hybrid_d2_jaxref_r4_427feb'

def setup_inputs(seed: int=0):
    np.random.seed(seed)
    _w = jnp.asarray

    def _L0_attn_a_setup():
        import jax, jax.numpy as jnp
        import numpy as np
        B, S, D, H = (4, 1024, 256, 8)
        HD = D // H
        key = jax.random.key(seed)
        k1, k2, k3 = jax.random.split(key, 3)
        x = jax.random.normal(k1, (B, S, D), dtype=jnp.float32)
        w_qkv = jax.random.normal(k2, (D, 3 * D), dtype=jnp.float32) * (1.0 / np.sqrt(D))
        w_out = jax.random.normal(k3, (D, D), dtype=jnp.float32) * (1.0 / np.sqrt(D))
        return {'x': x, 'w_qkv': w_qkv, 'w_out': w_out}
    _L0_attn_a_in = _L0_attn_a_setup()

    def _L0_attn_b_setup():
        import jax, jax.numpy as jnp
        import numpy as np
        T, B, D = (256, 32, 256)
        N_STATE, BLOCK = (256, 8)
        NB = N_STATE // BLOCK

        def _xavier(key, shape):
            fan_out, fan_in = shape
            a = (6.0 / (fan_in + fan_out)) ** 0.5
            return jax.random.uniform(key, shape, jnp.float32, -a, a)
        key = jax.random.key(seed)
        kx, kk, kv, kq = jax.random.split(key, 4)
        return {'x': jax.random.normal(kx, (T, B, D), jnp.float32), 'W_k': _xavier(kk, (N_STATE, D)), 'W_v': _xavier(kv, (N_STATE, D)), 'W_q': _xavier(kq, (N_STATE, D))}
    _L0_attn_b_in = _L0_attn_b_setup()

    def _L0_ffn_setup():
        import jax, jax.numpy as jnp
        import numpy as np
        D_MODEL = 256
        H_SHARED = 512
        H_ROUTED = 256
        N_EXPERTS = 8
        TOP_K = 2
        key = jax.random.key(seed)
        ks = jax.random.split(key, 8)
        B, T = (2, 512)
        sc_d = 1.0 / np.sqrt(D_MODEL)
        sc_hs = 1.0 / np.sqrt(H_SHARED)
        sc_hr = 1.0 / np.sqrt(H_ROUTED)
        return {'x': jax.random.normal(ks[0], (B, T, D_MODEL), dtype=jnp.float32), 'router_w': jax.random.normal(ks[1], (N_EXPERTS, D_MODEL), dtype=jnp.float32) * sc_d, 'router_bias': jnp.zeros((N_EXPERTS,), dtype=jnp.float32), 'sw1': jax.random.normal(ks[2], (D_MODEL, H_SHARED), dtype=jnp.float32) * sc_d, 'sw3': jax.random.normal(ks[3], (D_MODEL, H_SHARED), dtype=jnp.float32) * sc_d, 'sw2': jax.random.normal(ks[4], (H_SHARED, D_MODEL), dtype=jnp.float32) * sc_hs, 'ew1': jax.random.normal(ks[5], (N_EXPERTS, D_MODEL, H_ROUTED), dtype=jnp.float32) * sc_d, 'ew2': jax.random.normal(ks[6], (N_EXPERTS, H_ROUTED, D_MODEL), dtype=jnp.float32) * sc_hr}
    _L0_ffn_in = _L0_ffn_setup()

    def _L1_attn_a_setup():
        import jax, jax.numpy as jnp
        import numpy as np
        NUM_HEADS = 16
        key = jax.random.key(seed)
        ks = jax.random.split(key, 5)
        B, S, H = (2, 512, 256)
        scale = 0.02
        return {'x': jax.random.normal(ks[0], (B, S, H), dtype=jnp.float32), 'w_qkv': jax.random.normal(ks[1], (H, 3 * H), dtype=jnp.float32) * scale, 'b_qkv': jax.random.normal(ks[2], (3 * H,), dtype=jnp.float32) * scale, 'w_out': jax.random.normal(ks[3], (H, H), dtype=jnp.float32) * scale, 'b_out': jax.random.normal(ks[4], (H,), dtype=jnp.float32) * scale}
    _L1_attn_a_in = _L1_attn_a_setup()

    def _L1_attn_b_setup():
        import jax, jax.numpy as jnp
        import numpy as np
        import math
        DIM = 256
        HEADS = 16
        HEAD_DIM = DIM // HEADS
        SEQ = 512
        WINDOW = 4
        SPARSITY = 0.1
        ROPE_BASE = 10000.0

        def _dendritic(x, kernel):
            w = kernel.shape[0]
            s = x.shape[1]
            padded = jnp.pad(x, ((0, 0), (w - 1, 0), (0, 0)))
            out = kernel[0] * padded[:, 0:s]
            for i in range(1, w):
                out = out + kernel[i] * padded[:, i:i + s]
            return out

        def _oscillatory(x, pos, gamma_freq, theta_freq, phase):
            p = pos[None, :, None].astype(x.dtype)
            two_pi = 2.0 * jnp.pi
            gamma_phase = two_pi * gamma_freq[None, None, :] * p / 100.0 + phase[None, None, :]
            theta_phase = two_pi * theta_freq[None, None, :] * p / 100.0
            gain = 0.5 + 0.3 * jnp.cos(gamma_phase) + 0.2 * jnp.cos(theta_phase)
            return x * gain

        def _rope(x, cos, sin):
            b, h, s, hd = x.shape
            xp = x.reshape(b, h, s, hd // 2, 2)
            xe, xo = (xp[..., 0], xp[..., 1])
            c = cos[None, None, :, :]
            sn = sin[None, None, :, :]
            out_e = xe * c - xo * sn
            out_o = xe * sn + xo * c
            return jnp.stack([out_e, out_o], axis=-1).reshape(b, h, s, hd)

        def _forward(x, qkv_w, proj_w, proj_b, kernel_q, kernel_k, kernel_v, gamma_freq, theta_freq, phase):
            b, s, d = x.shape
            pos = jnp.arange(s)
            qkv = x @ qkv_w.T
            q, k, v = jnp.split(qkv, 3, axis=-1)
            q = _dendritic(q, kernel_q)
            k = _dendritic(k, kernel_k)
            v = _dendritic(v, kernel_v)
            q = _oscillatory(q, pos, gamma_freq, theta_freq, phase)
            k = _oscillatory(k, pos, gamma_freq, theta_freq, phase)
            q = q.reshape(b, s, HEADS, HEAD_DIM).transpose(0, 2, 1, 3)
            k = k.reshape(b, s, HEADS, HEAD_DIM).transpose(0, 2, 1, 3)
            v = v.reshape(b, s, HEADS, HEAD_DIM).transpose(0, 2, 1, 3)
            inv_freq = 1.0 / ROPE_BASE ** (jnp.arange(0, HEAD_DIM, 2, dtype=jnp.float32) / HEAD_DIM)
            freqs = pos.astype(jnp.float32)[:, None] * inv_freq[None, :]
            cosf, sinf = (jnp.cos(freqs), jnp.sin(freqs))
            q = _rope(q, cosf, sinf)
            k = _rope(k, cosf, sinf)
            scale = HEAD_DIM ** (-0.5)
            scores = jnp.einsum('bhqd,bhkd->bhqk', q, k) * scale
            minv = jnp.finfo(scores.dtype).min
            causal = jnp.tril(jnp.ones((s, s), dtype=bool))[None, None]
            scores = jnp.where(causal, scores, minv)
            topk = max(1, int(s * SPARSITY))
            kth = jax.lax.top_k(scores, topk)[0][..., -1:]
            sparse = jnp.where(scores >= kth, scores, minv)
            probs = jax.nn.softmax(sparse, axis=-1)
            out = jnp.einsum('bhqk,bhkd->bhqd', probs, v)
            out = out.transpose(0, 2, 1, 3).reshape(b, s, d)
            return out @ proj_w.T + proj_b
        key = jax.random.key(seed)
        ks = jax.random.split(key, 8)
        init = 0.02
        return {'x': jax.random.normal(ks[0], (1, SEQ, DIM), dtype=jnp.float32), 'qkv_w': jax.random.normal(ks[1], (3 * DIM, DIM), dtype=jnp.float32) * init, 'proj_w': jax.random.normal(ks[2], (DIM, DIM), dtype=jnp.float32) * init, 'proj_b': jax.random.normal(ks[3], (DIM,), dtype=jnp.float32) * init, 'kernel_q': jnp.exp(-jnp.linspace(0.0, 3.0, WINDOW)), 'kernel_k': jnp.exp(-jnp.linspace(0.0, 3.0, WINDOW)), 'kernel_v': jnp.exp(-jnp.linspace(0.0, 3.0, WINDOW)), 'gamma_freq': jnp.ones((DIM,), dtype=jnp.float32) * 60.0, 'theta_freq': jnp.ones((1,), dtype=jnp.float32) * 6.0, 'phase': jnp.zeros((DIM,), dtype=jnp.float32)}
    _L1_attn_b_in = _L1_attn_b_setup()

    def _L1_ffn_setup():
        import jax, jax.numpy as jnp
        import numpy as np
        D, H, NE, K, ED = (256, 16, 8, 2, 1024)
        B, S = (4, 256)
        EPS = 1e-06

        def rmsnorm(x, w):
            ms = jnp.mean(jnp.square(x.astype(jnp.float32)), axis=-1, keepdims=True)
            return x * jax.lax.rsqrt(ms + EPS).astype(x.dtype) * w

        def attn(x, qkv_w, o_w):
            b, s, d = x.shape
            hd = d // H
            qkv = (x @ qkv_w.T).reshape(b, s, 3, H, hd).transpose(2, 0, 3, 1, 4)
            q, k, v = (qkv[0], qkv[1], qkv[2])
            a = jnp.einsum('bhqd,bhkd->bhqk', q, k) * hd ** (-0.5)
            mask = jnp.triu(jnp.ones((s, s), dtype=bool), 1)
            a = jax.nn.softmax(jnp.where(mask, -1000000000.0, a), axis=-1)
            out = jnp.einsum('bhqk,bhkd->bhqd', a, v).transpose(0, 2, 1, 3).reshape(b, s, d)
            return out @ o_w.T

        def moe(x, gate_w, up_w, down_w):
            b, s, d = x.shape
            xf = x.reshape(b * s, d)
            gp = jax.nn.softmax(xf @ gate_w.T, axis=-1)
            ew, _ = jax.lax.top_k(gp, K)
            ew = ew / (jnp.sum(ew, axis=-1, keepdims=True) + 1e-09)
            ef = jax.nn.silu(xf @ up_w.T) @ down_w.T
            out = ef * jnp.sum(ew, axis=-1, keepdims=True)
            return out.reshape(b, s, d)
        key = jax.random.key(seed)
        ks = jax.random.split(key, 8)
        sd = 1.0 / np.sqrt(D)
        se = 1.0 / np.sqrt(ED)
        return {'x': jax.random.normal(ks[0], (B, S, D), dtype=jnp.float32), 'n1_w': jnp.ones((D,), jnp.float32), 'qkv_w': jax.random.normal(ks[1], (3 * D, D), jnp.float32) * sd, 'o_w': jax.random.normal(ks[2], (D, D), jnp.float32) * sd, 'n2_w': jnp.ones((D,), jnp.float32), 'gate_w': jax.random.normal(ks[3], (NE, D), jnp.float32) * sd, 'up_w': jax.random.normal(ks[4], (ED, D), jnp.float32) * sd, 'down_w': jax.random.normal(ks[5], (D, ED), jnp.float32) * se}
    _L1_ffn_in = _L1_ffn_setup()
    _d = {'L0_attn_a_x': _L0_attn_a_in['x'], 'L0_attn_a_w_qkv': _L0_attn_a_in['w_qkv'], 'L0_attn_a_w_out': _L0_attn_a_in['w_out'], 'L0_attn_b_W_k': _L0_attn_b_in['W_k'], 'L0_attn_b_W_v': _L0_attn_b_in['W_v'], 'L0_attn_b_W_q': _L0_attn_b_in['W_q'], 'L0_ffn_router_w': _L0_ffn_in['router_w'], 'L0_ffn_router_bias': _L0_ffn_in['router_bias'], 'L0_ffn_sw1': _L0_ffn_in['sw1'], 'L0_ffn_sw3': _L0_ffn_in['sw3'], 'L0_ffn_sw2': _L0_ffn_in['sw2'], 'L0_ffn_ew1': _L0_ffn_in['ew1'], 'L0_ffn_ew2': _L0_ffn_in['ew2'], 'L1_attn_a_w_qkv': _L1_attn_a_in['w_qkv'], 'L1_attn_a_b_qkv': _L1_attn_a_in['b_qkv'], 'L1_attn_a_w_out': _L1_attn_a_in['w_out'], 'L1_attn_a_b_out': _L1_attn_a_in['b_out'], 'L1_attn_b_qkv_w': _L1_attn_b_in['qkv_w'], 'L1_attn_b_proj_w': _L1_attn_b_in['proj_w'], 'L1_attn_b_proj_b': _L1_attn_b_in['proj_b'], 'L1_attn_b_kernel_q': _L1_attn_b_in['kernel_q'], 'L1_attn_b_kernel_k': _L1_attn_b_in['kernel_k'], 'L1_attn_b_kernel_v': _L1_attn_b_in['kernel_v'], 'L1_attn_b_gamma_freq': _L1_attn_b_in['gamma_freq'], 'L1_attn_b_theta_freq': _L1_attn_b_in['theta_freq'], 'L1_attn_b_phase': _L1_attn_b_in['phase'], 'L1_ffn_n1_w': _L1_ffn_in['n1_w'], 'L1_ffn_qkv_w': _L1_ffn_in['qkv_w'], 'L1_ffn_o_w': _L1_ffn_in['o_w'], 'L1_ffn_n2_w': _L1_ffn_in['n2_w'], 'L1_ffn_gate_w': _L1_ffn_in['gate_w'], 'L1_ffn_up_w': _L1_ffn_in['up_w'], 'L1_ffn_down_w': _L1_ffn_in['down_w']}
    _x0 = _d['L0_attn_a_x']
    _d['L0_attn_a_x'] = jax.random.normal(jax.random.fold_in(jax.random.key(seed), 1), (4, 1024, 256), dtype=_x0.dtype)
    del _x0
    return _d

def reference(L0_attn_a_x, L0_attn_a_w_qkv, L0_attn_a_w_out, L0_attn_b_W_k, L0_attn_b_W_v, L0_attn_b_W_q, L0_ffn_router_w, L0_ffn_router_bias, L0_ffn_sw1, L0_ffn_sw3, L0_ffn_sw2, L0_ffn_ew1, L0_ffn_ew2, L1_attn_a_w_qkv, L1_attn_a_b_qkv, L1_attn_a_w_out, L1_attn_a_b_out, L1_attn_b_qkv_w, L1_attn_b_proj_w, L1_attn_b_proj_b, L1_attn_b_kernel_q, L1_attn_b_kernel_k, L1_attn_b_kernel_v, L1_attn_b_gamma_freq, L1_attn_b_theta_freq, L1_attn_b_phase, L1_ffn_n1_w, L1_ffn_qkv_w, L1_ffn_o_w, L1_ffn_n2_w, L1_ffn_gate_w, L1_ffn_up_w, L1_ffn_down_w):

    def _L0_attn_a_ref(x, w_qkv, w_out):
        import jax, jax.numpy as jnp
        import numpy as np
        B, S, D, H = (4, 1024, 256, 8)
        HD = D // H
        b, s, d = x.shape
        qkv = x @ w_qkv
        q, k, v = jnp.split(qkv, 3, axis=-1)
        q = q.reshape(b, s, H, HD)
        k = k.reshape(b, s, H, HD)
        v = v.reshape(b, s, H, HD)
        fq = jnp.fft.fft(q, axis=-1)
        fk = jnp.fft.fft(k, axis=-1)
        fv = jnp.fft.fft(v, axis=-1)
        kv = fk * fv
        kv = jnp.cumsum(kv, axis=1)
        vals = jnp.fft.ifft(kv * jnp.conj(fq), axis=-1).real.astype(x.dtype)
        vals = vals.reshape(b, s, d)
        return vals @ w_out

    def _L0_attn_b_ref(x, W_k, W_v, W_q):
        import jax, jax.numpy as jnp
        import numpy as np
        T, B, D = (256, 32, 256)
        N_STATE, BLOCK = (256, 8)
        NB = N_STATE // BLOCK

        def _xavier(key, shape):
            fan_out, fan_in = shape
            a = (6.0 / (fan_in + fan_out)) ** 0.5
            return jax.random.uniform(key, shape, jnp.float32, -a, a)
        T_, B_, D_ = x.shape
        n = W_k.shape[0]
        b = BLOCK
        nb = n // b
        k = jnp.einsum('tbd,nd->tbn', x, W_k).reshape(T_, B_, nb, b)
        v = jnp.einsum('tbd,nd->tbn', x, W_v).reshape(T_, B_, nb, b)
        q = jnp.einsum('tbd,nd->tbn', x, W_q).reshape(T_, B_, nb, b)

        def step(S, kvq):
            k_t, v_t, q_t = kvq
            k_norm = k_t / (jnp.linalg.norm(k_t, axis=-1, keepdims=True) + 1e-06)
            retrieved = jnp.einsum('bnij,bnj->bni', S, k_norm)
            delta = v_t - retrieved
            S_new = jnp.tanh(S + jnp.einsum('bni,bnj->bnij', delta, k_norm))
            Sq = jnp.einsum('bnij,bnj->bni', S_new, q_t).reshape(B_, n)
            out = Sq * jax.nn.silu(Sq)
            return (S_new, out)
        S0 = jnp.zeros((B_, nb, b, b), x.dtype)
        _, outputs = jax.lax.scan(step, S0, (k, v, q))
        return outputs

    def _L0_ffn_ref(x, router_w, router_bias, sw1, sw3, sw2, ew1, ew2):
        import jax, jax.numpy as jnp
        import numpy as np
        D_MODEL = 256
        H_SHARED = 512
        H_ROUTED = 256
        N_EXPERTS = 8
        TOP_K = 2
        B, T, C = x.shape
        xf = x.reshape(-1, C)
        shared_out = jax.nn.silu(xf @ sw1) * (xf @ sw3) @ sw2
        s = jax.nn.sigmoid((xf @ router_w.T).astype(jnp.float32))
        sel_scores = s + router_bias.astype(jnp.float32)
        _, topk_idx = jax.lax.top_k(sel_scores, TOP_K)
        s_sel = jnp.take_along_axis(s, topk_idx, axis=1)
        denom = s_sel.sum(axis=1, keepdims=True)
        gates = jnp.where(denom > 1e-09, s_sel / (denom + 1e-09), 1.0 / TOP_K).astype(x.dtype)
        one_hot = jax.nn.one_hot(topk_idx, N_EXPERTS, dtype=x.dtype)
        comb = jnp.einsum('nke,nk->ne', one_hot, gates)
        h = jax.nn.gelu(jnp.einsum('nd,edh->neh', xf, ew1), approximate=False)
        y = jnp.einsum('neh,ehd->ned', h, ew2)
        routed_out = jnp.einsum('ned,ne->nd', y, comb)
        return (shared_out + routed_out).reshape(B, T, C)

    def _L1_attn_a_ref(x, w_qkv, b_qkv, w_out, b_out):
        import jax, jax.numpy as jnp
        import numpy as np
        NUM_HEADS = 16
        B, S, H = x.shape
        nh = NUM_HEADS
        hd = H // nh
        attn_scale = 1.0 / np.sqrt(hd).astype(np.float32)
        qkv = x @ w_qkv + b_qkv
        q, k, v = jnp.split(qkv, 3, axis=-1)
        to_heads = lambda t: t.reshape(B, S, nh, hd).transpose(0, 2, 1, 3)
        q, k, v = (to_heads(q), to_heads(k), to_heads(v))
        scores = jnp.einsum('bhid,bhjd->bhij', q, k) * attn_scale
        i = jnp.arange(S)[:, None]
        j = jnp.arange(S)[None, :]
        scores = jnp.where(j >= i, scores, -jnp.inf)
        attn = jax.nn.softmax(scores, axis=-1)
        out = jnp.einsum('bhij,bhjd->bhid', attn, v)
        out = out.transpose(0, 2, 1, 3).reshape(B, S, H)
        return out @ w_out + b_out

    def _L1_attn_b_ref(x, qkv_w, proj_w, proj_b, kernel_q, kernel_k, kernel_v, gamma_freq, theta_freq, phase):
        import jax, jax.numpy as jnp
        import numpy as np
        import math
        DIM = 256
        HEADS = 16
        HEAD_DIM = DIM // HEADS
        SEQ = 512
        WINDOW = 4
        SPARSITY = 0.1
        ROPE_BASE = 10000.0

        def _dendritic(x, kernel):
            w = kernel.shape[0]
            s = x.shape[1]
            padded = jnp.pad(x, ((0, 0), (w - 1, 0), (0, 0)))
            out = kernel[0] * padded[:, 0:s]
            for i in range(1, w):
                out = out + kernel[i] * padded[:, i:i + s]
            return out

        def _oscillatory(x, pos, gamma_freq, theta_freq, phase):
            p = pos[None, :, None].astype(x.dtype)
            two_pi = 2.0 * jnp.pi
            gamma_phase = two_pi * gamma_freq[None, None, :] * p / 100.0 + phase[None, None, :]
            theta_phase = two_pi * theta_freq[None, None, :] * p / 100.0
            gain = 0.5 + 0.3 * jnp.cos(gamma_phase) + 0.2 * jnp.cos(theta_phase)
            return x * gain

        def _rope(x, cos, sin):
            b, h, s, hd = x.shape
            xp = x.reshape(b, h, s, hd // 2, 2)
            xe, xo = (xp[..., 0], xp[..., 1])
            c = cos[None, None, :, :]
            sn = sin[None, None, :, :]
            out_e = xe * c - xo * sn
            out_o = xe * sn + xo * c
            return jnp.stack([out_e, out_o], axis=-1).reshape(b, h, s, hd)

        def _forward(x, qkv_w, proj_w, proj_b, kernel_q, kernel_k, kernel_v, gamma_freq, theta_freq, phase):
            b, s, d = x.shape
            pos = jnp.arange(s)
            qkv = x @ qkv_w.T
            q, k, v = jnp.split(qkv, 3, axis=-1)
            q = _dendritic(q, kernel_q)
            k = _dendritic(k, kernel_k)
            v = _dendritic(v, kernel_v)
            q = _oscillatory(q, pos, gamma_freq, theta_freq, phase)
            k = _oscillatory(k, pos, gamma_freq, theta_freq, phase)
            q = q.reshape(b, s, HEADS, HEAD_DIM).transpose(0, 2, 1, 3)
            k = k.reshape(b, s, HEADS, HEAD_DIM).transpose(0, 2, 1, 3)
            v = v.reshape(b, s, HEADS, HEAD_DIM).transpose(0, 2, 1, 3)
            inv_freq = 1.0 / ROPE_BASE ** (jnp.arange(0, HEAD_DIM, 2, dtype=jnp.float32) / HEAD_DIM)
            freqs = pos.astype(jnp.float32)[:, None] * inv_freq[None, :]
            cosf, sinf = (jnp.cos(freqs), jnp.sin(freqs))
            q = _rope(q, cosf, sinf)
            k = _rope(k, cosf, sinf)
            scale = HEAD_DIM ** (-0.5)
            scores = jnp.einsum('bhqd,bhkd->bhqk', q, k) * scale
            minv = jnp.finfo(scores.dtype).min
            causal = jnp.tril(jnp.ones((s, s), dtype=bool))[None, None]
            scores = jnp.where(causal, scores, minv)
            topk = max(1, int(s * SPARSITY))
            kth = jax.lax.top_k(scores, topk)[0][..., -1:]
            sparse = jnp.where(scores >= kth, scores, minv)
            probs = jax.nn.softmax(sparse, axis=-1)
            out = jnp.einsum('bhqk,bhkd->bhqd', probs, v)
            out = out.transpose(0, 2, 1, 3).reshape(b, s, d)
            return out @ proj_w.T + proj_b
        return _forward(x, qkv_w, proj_w, proj_b, kernel_q, kernel_k, kernel_v, gamma_freq, theta_freq, phase)

    def _L1_ffn_ref(x, n1_w, qkv_w, o_w, n2_w, gate_w, up_w, down_w):
        import jax, jax.numpy as jnp
        import numpy as np
        D, H, NE, K, ED = (256, 16, 8, 2, 1024)
        B, S = (4, 256)
        EPS = 1e-06

        def rmsnorm(x, w):
            ms = jnp.mean(jnp.square(x.astype(jnp.float32)), axis=-1, keepdims=True)
            return x * jax.lax.rsqrt(ms + EPS).astype(x.dtype) * w

        def attn(x, qkv_w, o_w):
            b, s, d = x.shape
            hd = d // H
            qkv = (x @ qkv_w.T).reshape(b, s, 3, H, hd).transpose(2, 0, 3, 1, 4)
            q, k, v = (qkv[0], qkv[1], qkv[2])
            a = jnp.einsum('bhqd,bhkd->bhqk', q, k) * hd ** (-0.5)
            mask = jnp.triu(jnp.ones((s, s), dtype=bool), 1)
            a = jax.nn.softmax(jnp.where(mask, -1000000000.0, a), axis=-1)
            out = jnp.einsum('bhqk,bhkd->bhqd', a, v).transpose(0, 2, 1, 3).reshape(b, s, d)
            return out @ o_w.T

        def moe(x, gate_w, up_w, down_w):
            b, s, d = x.shape
            xf = x.reshape(b * s, d)
            gp = jax.nn.softmax(xf @ gate_w.T, axis=-1)
            ew, _ = jax.lax.top_k(gp, K)
            ew = ew / (jnp.sum(ew, axis=-1, keepdims=True) + 1e-09)
            ef = jax.nn.silu(xf @ up_w.T) @ down_w.T
            out = ef * jnp.sum(ew, axis=-1, keepdims=True)
            return out.reshape(b, s, d)
        x = x + attn(rmsnorm(x, n1_w), qkv_w, o_w)
        x = x + moe(rmsnorm(x, n2_w), gate_w, up_w, down_w)
        return x
    x = L0_attn_a_x
    x = x + _L0_attn_a_ref(_layernorm(x, axis=-1), L0_attn_a_w_qkv, L0_attn_a_w_out)
    x = x + _L0_ffn_ref(_layernorm(x, axis=-1), L0_ffn_router_w, L0_ffn_router_bias, L0_ffn_sw1, L0_ffn_sw3, L0_ffn_sw2, L0_ffn_ew1, L0_ffn_ew2)
    x = x + _L0_attn_b_ref(_layernorm(x, axis=-1), L0_attn_b_W_k, L0_attn_b_W_v, L0_attn_b_W_q)
    x = x + _L0_ffn_ref(_layernorm(x, axis=-1), L0_ffn_router_w, L0_ffn_router_bias, L0_ffn_sw1, L0_ffn_sw3, L0_ffn_sw2, L0_ffn_ew1, L0_ffn_ew2)
    x = x + _L1_attn_a_ref(_layernorm(x, axis=-1), L1_attn_a_w_qkv, L1_attn_a_b_qkv, L1_attn_a_w_out, L1_attn_a_b_out)
    x = x + _L1_ffn_ref(_layernorm(x, axis=-1), L1_ffn_n1_w, L1_ffn_qkv_w, L1_ffn_o_w, L1_ffn_n2_w, L1_ffn_gate_w, L1_ffn_up_w, L1_ffn_down_w)
    x = x + _L1_attn_b_ref(_layernorm(x, axis=-1), L1_attn_b_qkv_w, L1_attn_b_proj_w, L1_attn_b_proj_b, L1_attn_b_kernel_q, L1_attn_b_kernel_k, L1_attn_b_kernel_v, L1_attn_b_gamma_freq, L1_attn_b_theta_freq, L1_attn_b_phase)
    x = x + _L1_ffn_ref(_layernorm(x, axis=-1), L1_ffn_n1_w, L1_ffn_qkv_w, L1_ffn_o_w, L1_ffn_n2_w, L1_ffn_gate_w, L1_ffn_up_w, L1_ffn_down_w)
    return x

_drawn_inputs = setup_inputs


def setup_inputs(seed=0):
    import zlib

    import numpy as np

    out = dict(_drawn_inputs(seed))
    spreads = {'L0_ffn_router_bias': (0.0, 0.8),
     'L1_attn_b_gamma_freq': (60.0, 0.6),
     'L1_attn_b_phase': (0.0, 0.8),
     'L1_ffn_n1_w': (1.0, 0.6),
     'L1_ffn_n2_w': (1.0, 0.6)}
    factors = {'L0_attn_b_W_k': 8.0,
     'L0_attn_b_W_v': 8.0,
     'L0_attn_b_W_q': 8.0,
     'L0_ffn_router_w': 8.0,
     'L0_ffn_sw1': 8.0,
     'L0_ffn_sw3': 8.0,
     'L0_ffn_sw2': 8.0,
     'L0_ffn_ew1': 8.0,
     'L0_ffn_ew2': 8.0,
     'L1_attn_a_w_qkv': 39.886,
     'L1_attn_a_b_qkv': 64.0,
     'L1_attn_a_w_out': 39.64,
     'L1_attn_a_b_out': 64.0,
     'L1_attn_b_qkv_w': 8.0,
     'L1_attn_b_proj_w': 8.0,
     'L1_attn_b_proj_b': 64.0,
     'L1_attn_b_kernel_q': 8.0,
     'L1_attn_b_kernel_k': 8.0,
     'L1_attn_b_kernel_v': 8.0,
     'L1_ffn_qkv_w': 8.0,
     'L1_ffn_o_w': 8.0,
     'L1_ffn_gate_w': 64.0,
     'L1_ffn_up_w': 8.0,
     'L1_ffn_down_w': 8.0}
    for name, (base, spread) in spreads.items():
        noise = np.random.default_rng([zlib.crc32(name.encode()), seed]).standard_normal(out[name].shape)
        drawn = base * np.exp(spread * noise) if base else spread * noise
        out[name] = jnp.asarray(drawn.astype(out[name].dtype))
    for name, factor in factors.items():
        out[name] = (out[name] * factor).astype(out[name].dtype)
    return out
```

```python
import concourse.bass as bass
from concourse import mybir
from contextlib import ExitStack
from math import pi

F32 = mybir.dt.float32
BF16 = mybir.dt.bfloat16
U32 = mybir.dt.uint32
ALU = mybir.AluOpType
ACT = mybir.ActivationFunctionType
AX = mybir.AxisListType

P = 128
B, S, D = 4, 1024, 256
NT = B * S // P
TB = S // P
DC = D // P
NEG = -1.0e30
GONE = -3.0e38
NH, HD = 16, 16
HC = P // HD
TOPK = max(1, int(S * 0.1))
ONE = 1
LN_EPS, RMS_EPS = 1e-5, 1e-6

Q_PART = (0, 0, 1, 1, 0, 2)
K_PART = (0, 1, 0, 1, 2, 0)
QK_ROWS = len(Q_PART) * HD


class Core:

    def __init__(self, nc, ctx):
        self.nc = nc
        self.numbers = sorted(nc.free_semaphores)
        self.turn = 0

        def sb(name, shape, dt=F32):
            return ctx.enter_context(nc.sbuf_tensor(name, shape, dt))

        self.x = sb("x", [P, NT, D])
        self.ident = sb("ident", [P, P])
        self.ident_bf = sb("ident_bf", [P, P], BF16)
        self.above = sb("above", [P, P], BF16)
        self.below = sb("below", [P, P], BF16)
        self.ones = sb("ones", [1, P])
        self.mean_var = sb("mean_var", [P, NT, 2])
        self.rstd = sb("rstd", [P, NT])


class Stage:

    def __init__(self, core, name):
        self.core, self.nc, self.name = core, core.nc, name
        self.ctx = ExitStack()
        self.sems = []

    def __enter__(self):
        self.ctx.__enter__()
        return self

    def __exit__(self, *a):
        done = self.ctx.__exit__(*a)
        if self.sems and a[0] is None:
            self.nc.clear_and_free_semaphores(self.sems)
        return done

    def sb(self, name, shape, dt=F32):
        return self.ctx.enter_context(self.nc.sbuf_tensor(f"{self.name}_{name}", shape, dt))

    def ps(self, name, shape, dt=F32):
        return self.ctx.enter_context(self.nc.psum_tensor(f"{self.name}_{name}", shape, dt))

    def sem(self, name):
        number = self.core.numbers[self.core.turn % len(self.core.numbers)]
        self.core.turn += 1
        self.sems.append(self.nc.alloc_semaphore(f"{self.name}_{name}", num=number))
        return self.sems[-1]

    def block(self):
        return self.ctx.enter_context(self.nc.Block())



def load_and_constants(core, x_dram):
    nc = core.nc
    with Stage(core, "start") as st:
        x_loaded, zeroed, ready = st.sem("x_loaded"), st.sem("zeroed"), st.sem("ready")
        block = st.block()

        @block.sync
        def _(sp):
            xv = x_dram.rearrange("(t p) d -> p t d", p=P)
            for b in range(B):
                sp.dma_start(core.x[:, b * TB:(b + 1) * TB, :], xv[:, b * TB:(b + 1) * TB, :]).then_inc(x_loaded, 16)
            sp.wait_ge(x_loaded, 16 * B)

        @block.gpsimd
        def _(pool):
            for t in (core.ident, core.ident_bf, core.above, core.below):
                nc.gpsimd.memset(t[:], 0.0).then_inc(zeroed, 1)
            nc.gpsimd.memset(core.ones[:], 1.0)
            pool.wait_ge(zeroed, 4)
            for t in (core.ident, core.ident_bf):
                nc.gpsimd.affine_select(out=t[:], in_=t[:], compare_op=ALU.not_equal, fill=1.0,
                                        base=0, pattern=[[-1, P]], channel_multiplier=1).then_inc(ready, 1)
            nc.gpsimd.affine_select(out=core.above[:], in_=core.above[:], compare_op=ALU.is_ge, fill=NEG,
                                    base=0, pattern=[[-1, P]], channel_multiplier=1).then_inc(ready, 1)
            nc.gpsimd.affine_select(out=core.below[:], in_=core.below[:], compare_op=ALU.is_ge, fill=NEG,
                                    base=0, pattern=[[1, P]], channel_multiplier=-1).then_inc(ready, 1)
            pool.wait_ge(ready, 4)


def store(core, out_dram):
    with Stage(core, "end") as st:
        stored = st.sem("stored")
        block = st.block()

        @block.sync
        def _(sp):
            ov = out_dram.rearrange("(t p) d -> p t d", p=P)
            for b in range(B):
                sp.dma_start(ov[:, b * TB:(b + 1) * TB, :], core.x[:, b * TB:(b + 1) * TB, :]).then_inc(stored, 16)
            sp.wait_ge(stored, 16 * B)



def layernorm_statistics(core, name):
    nc = core.nc
    with Stage(core, name) as st:
        parts = st.sb("parts", [P, NT, 6])
        std = st.sb("std", [P, NT])
        var_ready, std_ready = st.sem("var_ready"), st.sem("std_ready")
        eps = st.sb("eps", [P, 1])
        block = st.block()

        @block.vector
        def _(dve):
            nc.vector.memset(eps[:], LN_EPS)
            for t in range(NT):
                nc.vector.bn_stats(parts[:, t, :], core.x[:, t, :])
            dve.drain()
            for t in range(NT):
                last = nc.vector.bn_aggr(core.mean_var[:, t, :], parts[:, t, :])
            last.then_inc(var_ready, 1)
            dve.wait_ge(std_ready, 1)
            nc.vector.reciprocal(core.rstd[:], std[:])

        @block.scalar
        def _(act):
            act.wait_ge(var_ready, 1)
            nc.scalar.activation(std[:], core.mean_var[:, :, 1], ACT.Sqrt, bias=eps[:]).then_inc(std_ready, 1)


def layernorm_rows(core, name, xn):
    nc = core.nc
    with Stage(core, name) as st:
        block = st.block()

        @block.vector
        def _(dve):
            for t in range(NT):
                nc.vector.tensor_scalar(xn[:, t, :], core.x[:, t, :], core.mean_var[:, t, 0:1],
                                        core.rstd[:, t:t + 1], ALU.subtract, ALU.mult)


def rms_statistics(core, name, xn, rinv):
    nc = core.nc
    with Stage(core, name) as st:
        sums = st.sb("sums", [P, NT])
        std = st.sb("std", [P, NT])
        junk = st.sb("junk", [P, D])
        eps = st.sb("eps", [P, 1])
        sums_ready, std_ready = st.sem("sums_ready"), st.sem("std_ready")
        block = st.block()

        @block.vector
        def _(dve):
            nc.vector.memset(eps[:], RMS_EPS)
            for t in range(NT):
                last = nc.vector.tensor_tensor_reduce(
                    out=junk[:], in0=xn[:, t, :], in1=xn[:, t, :], scale=1.0, scalar=0.0,
                    op0=ALU.mult, op1=ALU.add, accum_out=sums[:, t:t + 1])
                dve.drain()
            dve.drain().then_inc(sums_ready, 1)
            dve.wait_ge(std_ready, 1)
            nc.vector.reciprocal(rinv[:], std[:])

        @block.scalar
        def _(act):
            act.wait_ge(sums_ready, 1)
            nc.scalar.activation(std[:], sums[:], ACT.Sqrt, bias=eps[:], scale=1.0 / D).then_inc(std_ready, 1)



def holographic(core, wt_dram, wout_dram, dft_dram):
    nc = core.nc
    NJ = 3 * DC
    with Stage(core, "holo") as st:
        wt = st.sb("wt", [P, NJ, D])
        wout = st.sb("wout", [P, DC, D])
        dft = st.sb("dft", [P, 4, P])
        wf = st.sb("wf", [P, DC, NJ, 2, P])
        wg = st.sb("wg", [P, DC, 2, D])
        xrow = st.sb("xrow", [P, 4, D])
        xt = st.sb("xt", [P, DC, S])
        kre, kim = st.sb("kre", [P, S]), st.sb("kim", [P, S])
        t1, t2, t3, t4 = (st.sb(f"t{i}", [P, S]) for i in range(1, 5))
        kvr, kvi = st.sb("kvr", [P, S]), st.sb("kvi", [P, S])
        ar, ai = st.sb("ar", [P, DC, S]), st.sb("ai", [P, DC, S])
        ps = st.ps("ps", [P, 4, 2, 512])

        w_in, fold_full, fold_free = st.sem("w_in"), st.sem("fold_full"), st.sem("fold_free")
        row_full = st.sem("row_full")
        tr_full, xt_full = st.sem("tr_full"), st.sem("xt_full")
        pr_full, k_full = st.sem("pr_full"), st.sem("k_full")
        v_used, q_used = st.sem("v_used"), st.sem("q_used")
        prod_full, a_full = st.sem("prod_full"), st.sem("a_full")
        y_full, y_used = st.sem("y_full"), st.sem("y_used")
        block = st.block()
        NF = NJ * DC

        @block.sync
        def _(sp):
            sp.dma_start(wt[:], wt_dram.rearrange("(j p) d -> p j d", p=P)).then_inc(w_in, 16)
            sp.dma_start(wout[:], wout_dram.rearrange("(c p) d -> p c d", p=P)).then_inc(w_in, 16)
            sp.dma_start(dft[:], dft_dram.rearrange("a p n -> p a n")).then_inc(w_in, 16)

        @block.tensor
        def _(pe):
            pe.sem_inc(tr_full, ONE)
            pe.sem_inc(y_full, ONE)
            pe.wait_ge(w_in, 48)
            for j in range(NJ):
                for c in range(DC):
                    n = j * DC + c
                    if n >= 4:
                        pe.wait_ge(fold_free, n - 3)
                    for part in range(2):
                        last = nc.tensor.matmul(ps[:, n % 4, 0, part * P:part * P + P],
                                                wt[:, j, c * P:(c + 1) * P], dft[:, part, :], start=True, stop=True)
                    last.then_inc(fold_full, 1)
            for c in range(DC):
                for part in range(2):
                    n = NF + c * 2 + part
                    pe.wait_ge(fold_free, n - 3)
                    nc.tensor.matmul(ps[:, n % 4, 0, 0:D], dft[:, 2 + part, :], wout[:, c, :],
                                     start=True, stop=True).then_inc(fold_full, 1)
            pe.wait_ge(fold_free, NF + 2 * DC)
            with pe.Fori(0, B) as b:
                pe.wait_ge(y_used, ONE + b * TB)
                for t in range(TB):
                    pe.wait_ge(row_full, b * TB + t + 1)
                    for c in range(DC):
                        last = nc.tensor.transpose(ps[:, t // 2, 0, (c * 2 + t % 2) * P:(c * 2 + t % 2 + 1) * P],
                                                   xrow[:, t % 4, c * P:(c + 1) * P], core.ident[:])
                    if t % 2:
                        last.then_inc(tr_full, 1)
                pe.wait_ge(xt_full, (b + 1) * (TB // 2))

                def project(which, c, part, slot):
                    for half in range(2):
                        for d in range(DC):
                            last = nc.tensor.matmul(ps[:, slot, half, :], wf[:, d, which * DC + c, part, :],
                                                    xt[:, d, half * 512:(half + 1) * 512],
                                                    start=(d == 0), stop=(d == DC - 1))
                    last.then_inc(pr_full, 1)

                for c in range(DC):
                    if c:
                        pe.wait_ge(q_used, b * DC + c)
                    for part in range(2):
                        project(1, c, part, part)
                    if c:
                        pe.wait_ge(v_used, b * DC + c)
                    for part in range(2):
                        project(2, c, part, 2 + part)
                    pe.wait_ge(k_full, b * DC + c + 1)
                    for part in range(2):
                        project(0, c, part, part)
                pe.wait_ge(a_full, (b + 1) * DC)
                for t in range(TB):
                    slot, bank = t % 4, t // 4
                    for n in range(2 * DC):
                        c, part = n // 2, n % 2
                        a = (ar, ai)[part]
                        last = nc.tensor.matmul(ps[:, slot, bank, 0:D], a[:, c, t * P:(t + 1) * P], wg[:, c, part, :],
                                                start=(n == 0), stop=(n == 2 * DC - 1))
                    last.then_inc(y_full, 1)

        @block.scalar
        def _(act):
            for n in range(NF):
                act.wait_ge(fold_full, n + 1)
                nc.scalar.activation(wf[:, n % DC, n // DC, :, :],
                                     ps[:, n % 4, 0, 0:2 * P].rearrange("p (a f) -> p a f", a=2),
                                     ACT.Copy).then_inc(fold_free, 1)
            for n in range(NF, NF + 2 * DC):
                act.wait_ge(fold_full, n + 1)
                nc.scalar.activation(wg[:, (n - NF) // 2, (n - NF) % 2, :], ps[:, n % 4, 0, 0:D],
                                     ACT.Copy).then_inc(fold_free, 1)
            with act.Fori(0, B) as b:
                for n in range(TB // 2):
                    act.wait_ge(tr_full, ONE + b * (TB // 2) + n + 1)
                    nc.scalar.activation(xt[:, :, n * 2 * P:(n + 1) * 2 * P],
                                         ps[:, n, 0, :].rearrange("p (c t) -> p c t", c=DC),
                                         ACT.Copy).then_inc(xt_full, 1)
                for c in range(DC):
                    act.wait_ge(pr_full, b * 6 * DC + c * 6 + 2)
                    if c:
                        act.wait_ge(v_used, b * DC + c)
                    nc.scalar.activation(kre[:], ps[:, 0, :, :].rearrange("p a n -> p (a n)"), ACT.Copy)
                    nc.scalar.activation(kim[:], ps[:, 1, :, :].rearrange("p a n -> p (a n)"),
                                         ACT.Copy).then_inc(k_full, 1)

        @block.vector
        def _(dve):
            dve.sem_inc(y_used, ONE)
            def slot(i):
                return ps[:, i, :, :].rearrange("p a n -> p (a n)")

            with dve.Fori(0, B) as b:
                for t in range(TB):
                    dve.wait_ge(tr_full, ONE + b * (TB // 2) + max(0, t // 2 - 1))
                    nc.vector.tensor_scalar(xrow[:, t % 4, :], core.x[:, bass.ds(b * TB + t, 1), :].rearrange("p a d -> p (a d)"),
                                            core.mean_var[:, bass.ds(b * TB + t, 1), 0], core.rstd[:, bass.ds(b * TB + t, 1)],
                                            ALU.subtract, ALU.mult).then_inc(row_full, 1)
                for c in range(DC):
                    dve.wait_ge(k_full, b * DC + c + 1)
                    dve.wait_ge(pr_full, b * 6 * DC + c * 6 + 4)
                    nc.vector.tensor_tensor(t1[:], kre[:], slot(2), ALU.mult)
                    nc.vector.tensor_tensor(t2[:], kim[:], slot(3), ALU.mult)
                    nc.vector.tensor_tensor(t3[:], kre[:], slot(3), ALU.mult)
                    nc.vector.tensor_tensor(t4[:], kim[:], slot(2), ALU.mult)
                    dve.drain().then_inc(v_used, 1)
                    nc.vector.tensor_tensor_scan(kvr[:], t1[:], t2[:], 0.0, ALU.add, ALU.subtract)
                    nc.vector.tensor_tensor_scan(kvi[:], t3[:], t4[:], 0.0, ALU.add, ALU.add)
                    dve.drain()
                    dve.wait_ge(pr_full, b * 6 * DC + c * 6 + 6)
                    nc.vector.tensor_tensor(t1[:], kvr[:], slot(0), ALU.mult)
                    nc.vector.tensor_tensor(t2[:], kvi[:], slot(1), ALU.mult)
                    nc.vector.tensor_tensor(t3[:], kvi[:], slot(0), ALU.mult)
                    nc.vector.tensor_tensor(t4[:], kvr[:], slot(1), ALU.mult)
                    dve.drain().then_inc(q_used, 1)
                    if c == 0:
                        dve.wait_ge(y_full, ONE + b * TB)
                    nc.vector.tensor_tensor(ar[:, c, :], t1[:], t2[:], ALU.add)
                    nc.vector.tensor_tensor(ai[:, c, :], t3[:], t4[:], ALU.subtract)
                    dve.drain().then_inc(a_full, 1)
                for t in range(TB):
                    xv = core.x[:, bass.ds(b * TB + t, 1), :].rearrange("p a d -> p (a d)")
                    dve.wait_ge(y_full, ONE + b * TB + t + 1)
                    nc.vector.tensor_tensor(xv, ps[:, t % 4, t // 4, 0:D], xv, ALU.add).then_inc(y_used, 1)



def moe_shared_and_routed(core, name, router_dram, bias_dram, sw1, sw3, sw2, ew1, ew2):
    nc = core.nc
    HS, HR, NE = 512, 256, 8
    BLK = 512
    BT = BLK // P
    NB = B * S // BLK
    SC, RC = HS // P, HR // P
    NU = SC * 2 + NE * RC
    with Stage(core, name) as st:
        w1s, w3s = st.sb("w1s", [P, DC, HS]), st.sb("w3s", [P, DC, HS])
        w2s = st.sb("w2s", [P, SC, D])
        w1e = st.sb("w1e", [P, NE, DC, HR])
        w2e = st.sb("w2e", [P, NE, RC, D])
        rw = st.sb("rw", [P, DC, NE])
        rb = st.sb("rb", [P, NE])
        iota = st.sb("iota", [P, NE])
        xrow = st.sb("xrow", [P, BT, D])
        xt = st.sb("xt", [P, DC, BLK])
        sil = st.sb("sil", [P, SC, BLK])
        hs = st.sb("hs", [P, SC, BLK])
        he = st.sb("he", [P, NE * RC, BLK])
        score, sel = st.sb("score", [P, BT, NE]), st.sb("sel", [P, BT, NE])
        best, best_at = st.sb("best", [P, BT, 8]), st.sb("best_at", [P, BT, 8], U32)
        best_f = st.sb("best_f", [P, BT, 8])
        hot, hot2 = st.sb("hot", [P, BT, NE]), st.sb("hot2", [P, BT, NE])
        chosen, denom, inv, big, half = (st.sb(n, [P, BT, NE] if n == "chosen" else [P, BT])
                                         for n in ("chosen", "denom", "inv", "big", "half"))
        comb = st.sb("comb", [P, BT, NE])
        acc = st.sb("acc", [P, BT, D])
        up = st.ps("up", [P, 4, 512])
        dn = st.ps("dn", [P, 4, 512])

        w_in, io = st.sem("w_in"), st.sem("iota")
        row_full, tr_full = st.sem("row_full"), st.sem("tr_full")
        lg_full = st.sem("lg_full")
        up_full = st.sem("up_full")
        up_free = [st.sem(f"up_free{i}") for i in range(4)]
        dn_full, dn_used = st.sem("dn_full"), st.sem("dn_used")
        block = st.block()
        DN = BT * (1 + NE // 2)
        UPS = NU // 4

        @block.sync
        def _(sp):
            sp.dma_start(rw[:], router_dram.rearrange("(c p) n -> p c n", p=P)).then_inc(w_in, 16)
            sp.dma_start(rb[:], bias_dram.partition_broadcast(P)).then_inc(w_in, 16)
            sp.dma_start(w1s[:], sw1.rearrange("(c p) n -> p c n", p=P)).then_inc(w_in, 16)
            sp.dma_start(w3s[:], sw3.rearrange("(c p) n -> p c n", p=P)).then_inc(w_in, 16)
            sp.dma_start(w2s[:], sw2.rearrange("(c p) n -> p c n", p=P)).then_inc(w_in, 16)
            for e in range(NE):
                sp.dma_start(w1e[:, e], ew1[e].rearrange("(c p) n -> p c n", p=P)).then_inc(w_in, 16)
                sp.dma_start(w2e[:, e], ew2[e].rearrange("(c p) n -> p c n", p=P)).then_inc(w_in, 16)

        @block.gpsimd
        def _(pool):
            nc.gpsimd.iota(iota[:], pattern=[[1, NE]], base=0, channel_multiplier=0,
                           allow_small_or_imprecise_dtypes=True).then_inc(io, 1)

        @block.tensor
        def _(pe):
            pe.sem_inc(tr_full, ONE)
            pe.wait_ge(w_in, 16 * (5 + 2 * NE))
            with pe.Fori(0, NB) as k:
                pe.wait_ge(dn_used, ONE + k * (DN + 3))
                for t in range(BT):
                    pe.wait_ge(row_full, k * BT + t + 1)
                    for c in range(DC):
                        o = (c * 2 + t % 2) * P
                        last = nc.tensor.transpose(dn[:, t // 2, o:o + P], xrow[:, t, c * P:(c + 1) * P],
                                                   core.ident[:])
                last.then_inc(tr_full, 1)
                pe.wait_ge(dn_used, ONE + k * (DN + 3) + 2)
                for t in range(BT):
                    for c in range(DC):
                        last = nc.tensor.matmul(dn[:, 2, t * NE:(t + 1) * NE], xt[:, c, t * P:(t + 1) * P],
                                                rw[:, c, :], start=(c == 0), stop=(c == DC - 1))
                last.then_inc(lg_full, 1)
                for u in range(NU):
                    if u < 2 * SC:
                        w, m = ((w1s, w3s)[u % 2], u // 2)
                        lhs = [w[:, c, m * P:(m + 1) * P] for c in range(DC)]
                    else:
                        e, m = (u - 2 * SC) // RC, (u - 2 * SC) % RC
                        lhs = [w1e[:, e, c, m * P:(m + 1) * P] for c in range(DC)]
                    pe.wait_ge(up_free[u % 4], ONE + k * UPS + u // 4)
                    for c in range(DC):
                        last = nc.tensor.matmul(up[:, u % 4, :], lhs[c], xt[:, c, :],
                                                start=(c == 0), stop=(c == DC - 1))
                    last.then_inc(up_full, 1)
                n = 0
                for t in range(BT):
                    if t == 0:
                        for i in range(4):
                            pe.wait_ge(up_free[i], ONE + (k + 1) * UPS)
                    for g in range(1 + NE // 2):
                        pe.wait_ge(dn_used, ONE + k * (DN + 3) + 3 + max(0, n - 3))
                        if g == 0:
                            for m in range(SC):
                                last = nc.tensor.matmul(dn[:, n % 4, 0:D], hs[:, m, t * P:(t + 1) * P],
                                                        w2s[:, m, :], start=(m == 0), stop=(m == SC - 1))
                        else:
                            for e in (2 * g - 2, 2 * g - 1):
                                for m in range(RC):
                                    o = (e % 2) * D
                                    last = nc.tensor.matmul(dn[:, n % 4, o:o + D],
                                                            he[:, e * RC + m, t * P:(t + 1) * P],
                                                            w2e[:, e, m, :], start=(m == 0), stop=(m == RC - 1))
                        last.then_inc(dn_full, 1)
                        n += 1

        @block.scalar
        def _(act):
            act.sem_inc(dn_used, ONE)
            act.sem_inc(up_free[0], ONE)
            act.sem_inc(up_free[2], ONE)
            with act.Fori(0, NB) as k:
                act.wait_ge(tr_full, ONE + k + 1)
                for n in range(BT // 2):
                    nc.scalar.activation(xt[:, :, n * 2 * P:(n + 1) * 2 * P],
                                         dn[:, n, :].rearrange("p (c t) -> p c t", c=DC), ACT.Copy).then_inc(dn_used, 1)
                act.wait_ge(lg_full, k + 1)
                nc.scalar.activation(score[:], dn[:, 2, 0:BT * NE].rearrange("p (t e) -> p t e", e=NE),
                                     ACT.Sigmoid).then_inc(dn_used, 1)
                for u in range(0, 2 * SC, 2):
                    act.wait_ge(up_full, k * NU + u + 1)
                    nc.scalar.activation(sil[:, u // 2, :], up[:, u % 4, :], ACT.Silu).then_inc(up_free[u % 4], 1)
                for u in range(2 * SC, NU):
                    act.wait_ge(up_full, k * NU + u + 1)
                    nc.scalar.activation(he[:, u - 2 * SC, :], up[:, u % 4, :], ACT.Gelu).then_inc(up_free[u % 4], 1)

        @block.vector
        def _(dve):
            dve.sem_inc(up_free[1], ONE)
            dve.sem_inc(up_free[3], ONE)
            dve.wait_ge(io, 1)
            dve.wait_ge(w_in, 16 * (5 + 2 * NE))
            with dve.Fori(0, NB) as k:
                for t in range(BT):
                    dve.wait_ge(tr_full, ONE + k)
                    nc.vector.tensor_scalar(xrow[:, t, :], core.x[:, bass.ds(k * BT + t, 1), :].rearrange("p a d -> p (a d)"),
                                            core.mean_var[:, bass.ds(k * BT + t, 1), 0], core.rstd[:, bass.ds(k * BT + t, 1)],
                                            ALU.subtract, ALU.mult).then_inc(row_full, 1)
                dve.wait_ge(dn_used, ONE + k * (DN + 3) + 3)
                rb_b = rb[:].rearrange("p (a e) -> p a e", a=1).to_broadcast([P, BT, NE])
                io_b = iota[:].rearrange("p (a e) -> p a e", a=1).to_broadcast([P, BT, NE])
                nc.vector.tensor_tensor(sel[:], score[:], rb_b, ALU.add)
                dve.drain()
                for t in range(BT):
                    nc.vector.max(best[:, t, :], sel[:, t, :])
                dve.drain()
                for t in range(BT):
                    nc.vector.max_index(best_at[:, t, :], best[:, t, :], sel[:, t, :])
                dve.drain()
                nc.vector.tensor_copy(best_f[:], best_at[:])
                dve.drain()
                nc.vector.tensor_tensor(hot[:], io_b, best_f[:, :, 0:1].to_broadcast([P, BT, NE]), ALU.is_equal)
                nc.vector.tensor_tensor(hot2[:], io_b, best_f[:, :, 1:2].to_broadcast([P, BT, NE]), ALU.is_equal)
                dve.drain()
                nc.vector.tensor_tensor(hot[:], hot[:], hot2[:], ALU.add)
                dve.drain()
                nc.vector.tensor_tensor(chosen[:], hot[:], score[:], ALU.mult)
                dve.drain()
                nc.vector.tensor_reduce(denom[:], chosen[:], AX.X, ALU.add)
                dve.drain()
                nc.vector.tensor_scalar(inv[:], denom[:], 1e-9, None, ALU.add)
                nc.vector.tensor_scalar(big[:], denom[:], 1e-9, None, ALU.is_gt)
                dve.drain()
                nc.vector.reciprocal(inv[:], inv[:])
                nc.vector.tensor_scalar(half[:], big[:], -0.5, 0.5, ALU.mult, ALU.add)
                dve.drain()
                nc.vector.tensor_tensor(inv[:], inv[:], big[:], ALU.mult)
                dve.drain()

                def over_experts(v):
                    return v[:].rearrange("p (t a) -> p t a", a=1).to_broadcast([P, BT, NE])

                nc.vector.tensor_tensor(chosen[:], chosen[:], over_experts(inv), ALU.mult)
                nc.vector.tensor_tensor(hot[:], hot[:], over_experts(half), ALU.mult)
                dve.drain()
                nc.vector.tensor_tensor(comb[:], chosen[:], hot[:], ALU.add)
                dve.drain()
                for m in range(SC):
                    dve.wait_ge(up_free[(2 * m) % 4], ONE + k * UPS + m // 2 + 1)
                    dve.wait_ge(up_full, k * NU + 2 * m + 2)
                    nc.vector.tensor_tensor(hs[:, m, :], sil[:, m, :], up[:, (2 * m + 1) % 4, :],
                                            ALU.mult).then_inc(up_free[(2 * m + 1) % 4], 1)
                n = 0
                for t in range(BT):
                    xv = core.x[:, bass.ds(k * BT + t, 1), :].rearrange("p a d -> p (a d)")
                    for g in range(1 + NE // 2):
                        if g:
                            dve.drain()
                        dve.wait_ge(dn_full, k * DN + n + 1)
                        if g == 0:
                            last = nc.vector.tensor_copy(acc[:, t, :], dn[:, n % 4, 0:D])
                        else:
                            for e in (2 * g - 2, 2 * g - 1):
                                o = (e % 2) * D
                                if e % 2:
                                    dve.drain()
                                last = nc.vector.scalar_tensor_tensor(out=acc[:, t, :], in0=dn[:, n % 4, o:o + D],
                                                                      scalar=comb[:, t, e:e + 1], in1=acc[:, t, :],
                                                                      op0=ALU.mult, op1=ALU.add)
                        last.then_inc(dn_used, 1)
                        n += 1
                    dve.drain()
                    nc.vector.tensor_tensor(xv, acc[:, t, :], xv, ALU.add)



def delta_memory(core, wkvq_dram):
    with Stage(core, "delta_kvq") as st:
        kvq = st.sb("kvq", [P, NT, 3, D])
        delta_projections(core, wkvq_dram, kvq)
        delta_recurrence(core, kvq)


NBK, BK = 32, 8


def delta_projections(core, wkvq_dram, kvq):
    nc = core.nc
    with Stage(core, "delta") as st:
        w = st.sb("w", [P, DC, 3 * D])
        xrow = st.sb("xrow", [P, 2, D])
        xt = st.sb("xt", [P, 2, DC, P])
        sq = st.sb("sq", [P, 2, D])
        norm = st.sb("norm", [P, NT * NBK])
        tr = st.ps("tr", [P, 2, 512])
        pj = st.ps("pj", [P, 2, 1024])
        w_in = st.sem("w_in")
        row_full, tr_full, xt_full = (st.sem(n) for n in ("row_full", "tr_full", "xt_full"))
        pj_full, pj_used, sq_full, sq_used = (st.sem(n) for n in ("pj_full", "pj_used", "sq_full", "sq_used"))
        ss_full, root_full = st.sem("ss_full"), st.sem("root_full")

        block = st.block()

        @block.sync
        def _(sp):
            sp.dma_start(w[:], wkvq_dram.rearrange("(c p) n -> p c n", p=P)).then_inc(w_in, 16)

        @block.tensor
        def _(pe):
            pe.sem_inc(tr_full, ONE)
            pe.wait_ge(w_in, 16)
            with pe.Fori(0, NT // 2) as i:
                for j in range(2):
                    pe.wait_ge(row_full, i * 2 + j + 1)
                    for c in range(DC):
                        last = nc.tensor.transpose(tr[:, j, c * P:(c + 1) * P], xrow[:, j, c * P:(c + 1) * P],
                                                   core.ident[:])
                    last.then_inc(tr_full, 1)
                for j in range(2):
                    pe.wait_ge(xt_full, i * 2 + j + 1)
                    pe.wait_ge(pj_used, ONE + i * 2 + j)
                    for lo, hi in ((0, 512), (512, 768)):
                        for c in range(DC):
                            last = nc.tensor.matmul(pj[:, j, lo:hi], xt[:, j, c, :], w[:, c, lo:hi],
                                                    start=(c == 0), stop=(c == DC - 1))
                    last.then_inc(pj_full, 1)

        @block.scalar
        def _(act):
            act.sem_inc(pj_used, ONE)
            with act.Fori(0, NT // 2) as i:
                for j in range(2):
                    act.wait_ge(tr_full, ONE + i * 2 + j + 1)
                    nc.scalar.activation(xt[:, j], tr[:, j, 0:DC * P].rearrange("p (c t) -> p c t", c=DC),
                                         ACT.Copy).then_inc(xt_full, 1)
                for j in range(2):
                    act.wait_ge(pj_full, i * 2 + j + 1)
                    act.wait_ge(sq_used, ONE + i * 2 + j)
                    nc.scalar.activation(sq[:, j, :], pj[:, j, 0:D], ACT.Square).then_inc(sq_full, 1)
                    nc.scalar.activation(kvq[:, bass.ds(i * 2 + j, 1)].rearrange("p a b d -> p (a b d)"), pj[:, j, 0:3 * D],
                                         ACT.Copy).then_inc(pj_used, 1)
            act.wait_ge(ss_full, 1)
            nc.scalar.activation(norm[:], norm[:], ACT.Sqrt).then_inc(root_full, 1)

        @block.vector
        def _(dve):
            dve.sem_inc(sq_used, ONE)
            with dve.Fori(0, NT // 2) as i:
                for j in range(2):
                    dve.wait_ge(tr_full, ONE + i * 2)
                    nc.vector.tensor_scalar(xrow[:, j, :], core.x[:, bass.ds(i * 2 + j, 1), :].rearrange("p a d -> p (a d)"),
                                            core.mean_var[:, bass.ds(i * 2 + j, 1), 0], core.rstd[:, bass.ds(i * 2 + j, 1)],
                                            ALU.subtract, ALU.mult).then_inc(row_full, 1)
                for j in range(2):
                    dve.wait_ge(sq_full, i * 2 + j + 1)
                    nc.vector.tensor_reduce(norm[:, bass.ds((i * 2 + j) * NBK, NBK)],
                                            sq[:, j, :].rearrange("p (n e) -> p n e", e=BK), AX.X,
                                            ALU.add).then_inc(sq_used, 1)
            dve.drain().then_inc(ss_full, 1)
            dve.wait_ge(root_full, 1)
            nc.vector.tensor_scalar(norm[:], norm[:], 1e-6, None, ALU.add)
            dve.drain()
            nc.vector.reciprocal(norm[:], norm[:])
            dve.drain()
            for t in range(NT):
                k = kvq[:, t, 0, :].rearrange("p (n e) -> p n e", e=BK)
                r = norm[:, t * NBK:(t + 1) * NBK].rearrange("p (n a) -> p n a", a=1).to_broadcast([P, NBK, BK])
                nc.vector.tensor_tensor(k, k, r, ALU.mult)


def delta_recurrence(core, kvq):
    nc = core.nc
    with Stage(core, "recur") as s2:
        state = s2.sb("state", [P, NBK, BK, BK])
        prod = s2.sb("prod", [P, NBK, BK, BK])
        ret = s2.sb("ret", [P, NBK, BK])
        pre_full, tanh_full = s2.sem("pre_full"), s2.sem("tanh_full")
        sq_done, silu_done = s2.sem("sq_done"), s2.sem("silu_done")
        block2 = s2.block()
        full = [P, NBK, BK, BK]

        @block2.scalar
        def _(act):
            with act.Fori(0, TB) as i:
                for t in range(B):
                    act.wait_ge(pre_full, i * B + t + 1)
                    nc.scalar.activation(state[:], prod[:], ACT.Tanh).then_inc(tanh_full, 1)
            act.wait_ge(sq_done, 1)
            for t in range(NT):
                nc.scalar.activation(kvq[:, t, 2, :], kvq[:, t, 1, :], ACT.Silu).then_inc(silu_done, 1)

        @block2.vector
        def _(dve):
            with dve.Fori(0, TB) as i:
                for t in range(B):
                    def part(which):
                        v = kvq[:, bass.ds(i + t * TB, 1), which, :]
                        return v.rearrange("p a (n e) -> p (a n) e", e=BK)

                    def by_j(which):
                        v = kvq[:, bass.ds(i + t * TB, 1), which, :]
                        return v.rearrange("p a (n o e) -> p (a n) o e", e=BK, o=1).to_broadcast(full)

                    v_i = part(1)
                    if t > 0:
                        nc.vector.tensor_tensor(prod[:], state[:], by_j(0), ALU.mult)
                        dve.drain()
                        nc.vector.tensor_reduce(ret[:], prod[:], AX.X, ALU.add)
                        dve.drain()
                        nc.vector.tensor_tensor(ret[:], v_i, ret[:], ALU.subtract)
                        dve.drain()
                        d_i = ret[:].rearrange("p n (e o) -> p n e o", o=1).to_broadcast(full)
                        nc.vector.tensor_tensor(prod[:], d_i, by_j(0), ALU.mult)
                        dve.drain()
                        nc.vector.tensor_tensor(prod[:], prod[:], state[:], ALU.add).then_inc(pre_full, 1)
                    else:
                        v_e = kvq[:, bass.ds(i + t * TB, 1), 1, :].rearrange("p a (n e o) -> p (a n) e o", e=BK, o=1)
                        nc.vector.tensor_tensor(prod[:], v_e.to_broadcast(full), by_j(0), ALU.mult).then_inc(pre_full, 1)
                    dve.wait_ge(tanh_full, i * B + t + 1)
                    nc.vector.tensor_tensor(prod[:], state[:], by_j(2), ALU.mult)
                    dve.drain()
                    nc.vector.tensor_reduce(v_i, prod[:], AX.X, ALU.add)
                    dve.drain()
            dve.drain().then_inc(sq_done, 1)
            for t in range(NT):
                dve.wait_ge(silu_done, t + 1)
                nc.vector.tensor_tensor(kvq[:, t, 0, :], kvq[:, t, 1, :], kvq[:, t, 2, :], ALU.mult)
            dve.drain()
            for t in range(NT):
                nc.vector.tensor_tensor(core.x[:, t, :], core.x[:, t, :], kvq[:, t, 0, :], ALU.add)




def attention(core, name, wqkv_dram, wout_dram, scratch, *, causal, target, rows, bias=None, out_bias=None,
              col_scale=None, fancy=None):
    nc = core.nc
    QN = TB
    if causal:
        blocks = [list(range(0, q + 1)) for q in range(QN)]
    else:
        blocks = [list(range(q, QN)) for q in range(QN)]
    chunks = [[bl[i:i + 4] for i in range(0, len(bl), 4)] for bl in blocks]
    NTILE = NH * QN
    tiles = [(h, q) for h in range(NH) for q in range(QN)]
    topk = fancy is not None
    with Stage(core, name) as st:
        wqkv = st.sb("wqkv", [P, DC, 3 * D])
        wout = st.sb("wout", [P, DC, D])
        xrow = st.sb("xrow", [P, 4, D])
        PAD = 3 if topk else 0
        xt = st.sb("xt", [P, DC, PAD + S])
        qf = st.sb("qf", [P, S])
        rest = st.sb("rest", [P, S])
        part = [st.sb(f"part{i}", [P, S], BF16) for i in range(3)]
        qs = st.sb("qs", [QK_ROWS, NH, S], BF16)
        ks = st.sb("ks", [QK_ROWS, NH, S], BF16)
        v = st.sb("v", [P, TB, D])
        e = st.sb("e", [P, 2, S])
        pt = st.sb("pt", [P, 4, 512])
        o = st.sb("o", [P, QN, D])
        ot = st.sb("ot", [P, DC, S])
        nmax = st.sb("nmax", [P, 2, QN])
        rowsum = st.sb("rowsum", [P, 2, QN])
        rinv = st.sb("rinv", [P, QN])
        if bias is not None:
            bqk = st.sb("bqk", [P, 2 * DC])
            bqk4 = st.sb("bqk4", [P, 2 * DC])
            bv = st.sb("bv", [1, D])
        if out_bias is not None:
            bo = st.sb("bo", [1, D])
        if col_scale is not None:
            cs = st.sb("cs", [P, DC])
        if topk:
            conv = st.sb("conv", [P, DC, S])
            taps = st.sb("taps", [P, 3, 4])
            swap = st.sb("swap", [P, P])
            cos_t, sin_t = st.sb("cos", [P, S]), st.sb("sin", [P, S])
            gain = st.sb("gain", [P, DC, S])
            freq = st.sb("freq", [P, DC])
            phase = st.sb("phase", [P, DC])
            theta = st.sb("theta", [P, 1])
            work = st.sb("work", [P, S])
            top8 = st.sb("top8", [P, 2, 8])
            hp = st.sb("hp", [P, 1])
        sc = st.ps("sc", [P, 2, 1024])
        tp = st.ps("tp", [P, 2, 512])
        ov = st.ps("ov", [P, 2, 512])

        w_in = st.sem("w_in")
        row_full = st.sem("row_full")
        sc_full = st.sem("sc_full")
        sc_free = [st.sem(f"sc_free{i}") for i in range(2)]
        tp_full = st.sem("tp_full")
        tp_free = [st.sem(f"tp_free{i}") for i in range(2)]
        part_full, part_out, qk_in = (st.sem(n) for n in ("part_full", "part_out", "qk_in"))
        max_full, pt_used = st.sem("max_full"), st.sem("pt_used")
        ov_full, o_full = st.sem("ov_full"), st.sem("o_full")
        if topk:
            conv_full, gain_phase, gain_sin, pos_full, e_full = (
                st.sem(n) for n in ("conv_full", "gain_phase", "gain_sin", "pos_full", "e_full"))
        block = st.block()

        SWAPS = 4 if topk else 0
        SC_PRE = 4 + SWAPS
        SC_N = SC_PRE + NTILE
        T_HEAD = sum(len(c) for c in chunks)
        TP_ROWS, TP_V = TB // 2, TB // 2
        TP_PRE = TP_ROWS + TP_V
        TP_PT = NH * T_HEAD
        TP_N = TP_PRE + TP_PT + TB // 2 + TB // 2
        assert SC_N % 2 == 0 and TP_N % 2 == 0
        chunk0 = [0]
        for h, q in tiles:
            chunk0.append(chunk0[-1] + len(chunks[q]))
        PRE = ("q", "k")

        def on_vector(n):
            return (not topk) and n % 2 == 1

        def sc_wait(eng, b, n):
            eng.wait_ge(sc_free[n % 2], ONE + b * (SC_N // 2) + n // 2)

        def sc_taken(eng, b, n):
            eng.wait_ge(sc_free[n % 2], ONE + b * (SC_N // 2) + n // 2 + 1)

        def tp_wait(eng, b, n):
            eng.wait_ge(tp_free[n % 2], ONE + b * (TP_N // 2) + n // 2)

        def tp_copied(eng, b, n):
            eng.wait_ge(tp_free[n % 2], ONE + b * (TP_N // 2) + n // 2 + 1)

        n_in = 2 + (2 if bias is not None else 0) + (out_bias is not None) + (col_scale is not None) + (9 if topk else 0)

        @block.sync
        def _(sp):
            sp.dma_start(wqkv[:], wqkv_dram.rearrange("(c p) n -> p c n", p=P)).then_inc(w_in, 16)
            sp.dma_start(wout[:], wout_dram.rearrange("(c p) n -> p c n", p=P)).then_inc(w_in, 16)
            if bias is not None:
                sp.dma_start(bqk[:], bias[0]).then_inc(w_in, 16)
                sp.dma_start(bv[:], bias[1]).then_inc(w_in, 16)
            if out_bias is not None:
                sp.dma_start(bo[:], out_bias.rearrange("(a n) -> a n", a=1)).then_inc(w_in, 16)
            if col_scale is not None:
                sp.dma_start(cs[:], col_scale).then_inc(w_in, 16)
            if topk:
                for i, kern in enumerate(fancy["taps"]):
                    sp.dma_start(taps[:, i, :], kern.partition_broadcast(P)).then_inc(w_in, 16)
                sp.dma_start(cos_t[:], fancy["cos"]).then_inc(w_in, 16)
                sp.dma_start(sin_t[:], fancy["sin"]).then_inc(w_in, 16)
                sp.dma_start(swap[:], fancy["swap"]).then_inc(w_in, 16)
                sp.dma_start(freq[:], fancy["gamma"]).then_inc(w_in, 16)
                sp.dma_start(phase[:], fancy["phase"]).then_inc(w_in, 16)
                sp.dma_start(theta[:], fancy["theta"].partition_broadcast(P)).then_inc(w_in, 16)
            sp.sem_inc(part_out, ONE)
            with sp.Fori(0, B) as b:
                for n in range(4):
                    c, which = n // 2, n % 2
                    dst, slots = ((qs, Q_PART), (ks, K_PART))[which]
                    sp.wait_ge(part_full, b * 4 + n + 1)
                    for i in range(3):
                        sp.dma_start(scratch[which, i, c * P:(c + 1) * P, :], part[i][:]).then_inc(part_out, 16)
                    sp.wait_ge(part_out, ONE + (b * 4 + n + 1) * 48)
                    for j, i in enumerate(slots):
                        sp.dma_start(dst[j * HD:(j + 1) * HD, c * HC:(c + 1) * HC, :],
                                     scratch[which, i, c * P:(c + 1) * P, :].rearrange("(h r) t -> r h t", r=HD)
                                     ).then_inc(qk_in, 16)

        @block.tensor
        def _(pe):
            pe.sem_inc(tp_full, ONE)
            pe.sem_inc(pt_used, ONE)
            pe.wait_ge(w_in, 16 * n_in)
            with pe.Fori(0, B) as b:
                for t in range(TB):
                    n = t // 2
                    if t % 2 == 0:
                        tp_wait(pe, b, n)
                    pe.wait_ge(row_full, b * TB + t + 1)
                    for c in range(DC):
                        k0 = (c * 2 + t % 2) * P
                        last = nc.tensor.transpose(tp[:, n % 2, k0:k0 + P], xrow[:, t % 4, c * P:(c + 1) * P],
                                                   core.ident[:])
                    if t % 2:
                        last.then_inc(tp_full, 1)
                if not topk:
                    tp_copied(pe, b, TP_ROWS - 2)
                    tp_copied(pe, b, TP_ROWS - 1)
                    src = xt
                else:
                    src = conv
                n = 0
                for c in range(DC):
                    for which in range(2):
                        if topk:
                            pe.wait_ge(conv_full, b * 5 + c * 2 + which + 1)
                        sc_wait(pe, b, n)
                        for half in range(2):
                            for d in range(DC):
                                k0 = which * D + c * P
                                last = nc.tensor.matmul(sc[:, n % 2, half * 512:(half + 1) * 512],
                                                        wqkv[:, d, k0:k0 + P],
                                                        src[:, d, half * 512:(half + 1) * 512],
                                                        start=(d == 0), stop=(d == DC - 1))
                        last.then_inc(sc_full, 1)
                        n += 1
                        if topk:
                            sc_taken(pe, b, n - 1)
                            sc_wait(pe, b, n)
                            for half in range(2):
                                last = nc.tensor.matmul(sc[:, n % 2, half * 512:(half + 1) * 512], swap[:],
                                                        qf[:, half * 512:(half + 1) * 512], start=True, stop=True)
                            last.then_inc(sc_full, 1)
                            n += 1
                if topk:
                    pe.wait_ge(conv_full, (b + 1) * 5)
                for t in range(TB):
                    n = TP_ROWS + t // 2
                    if t % 2 == 0:
                        tp_wait(pe, b, n)
                    dst = tp[:, n % 2, (t % 2) * D:(t % 2 + 1) * D]
                    for c in range(DC):
                        last = nc.tensor.matmul(dst, src[:, c, t * P:(t + 1) * P], wqkv[:, c, 2 * D:3 * D],
                                                start=(c == 0), stop=(c == DC - 1 and bias is None))
                    if bias is not None:
                        last = nc.tensor.matmul(dst, core.ones[:], bv[:], start=False, stop=True)
                    if t % 2:
                        last.then_inc(tp_full, 1)

                def scores(i):
                    h, q = tiles[i]
                    n = SC_PRE + i
                    if i == 0:
                        pe.wait_ge(qk_in, b * (4 * 96) + 2 * 96)
                    if i == HC * QN:
                        pe.wait_ge(qk_in, b * (4 * 96) + 4 * 96)
                    sc_wait(pe, b, n)
                    k0, w = blocks[q][0], len(blocks[q]) * P
                    diag = (q - k0) * P
                    for lo in range(0, w, 512):
                        hi = min(w, lo + 512)
                        has_diag = lo <= diag < hi
                        last = nc.tensor.matmul(sc[:, n % 2, lo:hi], qs[:, h, q * P:(q + 1) * P],
                                                ks[:, h, k0 * P + lo:k0 * P + hi], start=True, stop=not has_diag)
                        if has_diag:
                            mask = core.above if causal else core.below
                            last = nc.tensor.matmul(sc[:, n % 2, diag:diag + P], core.ident_bf[:], mask[:],
                                                    start=False, stop=True)
                    last.then_inc(sc_full, 1)

                def transposes(i):
                    h, q = tiles[i]
                    sc_taken(pe, b, SC_PRE + i)
                    for j, ch in enumerate(chunks[q]):
                        n = TP_PRE + chunk0[i] + j
                        tp_wait(pe, b, n)
                        for m in range(len(ch)):
                            last = nc.tensor.transpose(tp[:, n % 2, m * P:(m + 1) * P],
                                                       e[:, i % 2, (4 * j + m) * P:(4 * j + m + 1) * P], core.ident[:])
                        last.then_inc(tp_full, 1)

                def values(i):
                    h, q = tiles[i]
                    if q == 0:
                        pe.wait_ge(o_full, ONE + b * NH + max(0, h - 1))
                    for j, ch in enumerate(chunks[q]):
                        n = chunk0[i] + j
                        tp_copied(pe, b, TP_PRE + n)
                        for m, kb in enumerate(ch):
                            last = nc.tensor.matmul(ov[:, h % 2, q * HD:(q + 1) * HD],
                                                    pt[:, n % 4, m * P:(m + 1) * P], v[:, kb, h * HD:(h + 1) * HD],
                                                    start=(kb == blocks[q][0]), stop=(kb == blocks[q][-1]))
                        last.then_inc(pt_used, 1)

                tp_copied(pe, b, TP_PRE - 1)
                tp_copied(pe, b, TP_PRE - 2)
                for i in range(NTILE + 2):
                    if i < NTILE:
                        scores(i)
                    if 1 <= i <= NTILE:
                        transposes(i - 1)
                    if i >= 2:
                        values(i - 2)
                pe.wait_ge(o_full, ONE + (b + 1) * NH)
                base = TP_PRE + TP_PT
                for t in range(TB):
                    n = base + t // 2
                    if t % 2 == 0:
                        tp_wait(pe, b, n)
                    for c in range(DC):
                        k0 = (c * 2 + t % 2) * P
                        last = nc.tensor.transpose(tp[:, n % 2, k0:k0 + P], o[:, t, c * P:(c + 1) * P], core.ident[:])
                    if t % 2:
                        last.then_inc(tp_full, 1)
                base += TB // 2
                tp_copied(pe, b, base - 1)
                tp_copied(pe, b, base - 2)
                for t in range(TB):
                    n = base + t // 2
                    if t % 2 == 0:
                        tp_wait(pe, b, n)
                    dst = tp[:, n % 2, (t % 2) * D:(t % 2 + 1) * D]
                    for c in range(DC):
                        last = nc.tensor.matmul(dst, ot[:, c, t * P:(t + 1) * P], wout[:, c, :],
                                                start=(c == 0), stop=(c == DC - 1 and out_bias is None))
                    if out_bias is not None:
                        last = nc.tensor.matmul(dst, core.ones[:], bo[:], start=False, stop=True)
                    if t % 2:
                        last.then_inc(tp_full, 1)

        @block.scalar
        def _(act):
            act.sem_inc(tp_free[0], ONE)
            act.sem_inc(tp_free[1], ONE)
            if not topk:
                for i in range(2):
                    act.sem_inc(sc_free[i], ONE)
            act.wait_ge(w_in, 16 * n_in)
            if bias is not None:
                nc.scalar.activation(bqk4[:], bqk[:], ACT.Copy, scale=0.25)
                act.drain()
            if topk:
                for n in range(DC + 1):
                    act.wait_ge(gain_phase, n + 1)
                    nc.scalar.activation(work[:], rest[:], ACT.Sin).then_inc(gain_sin, 1)

            def copy_chunk(b, i):
                for j, ch in enumerate(chunks[tiles[i][1]]):
                    n = chunk0[i] + j
                    if not on_vector(n):
                        act.wait_ge(tp_full, ONE + b * TP_N + TP_PRE + n + 1)
                        act.wait_ge(pt_used, ONE + b * TP_PT + max(0, n - 3))
                        nc.scalar.activation(pt[:, n % 4, 0:len(ch) * P], tp[:, (TP_PRE + n) % 2, 0:len(ch) * P],
                                             ACT.Copy).then_inc(tp_free[(TP_PRE + n) % 2], 1)

            with act.Fori(0, B) as b:
                for n in range(TP_ROWS):
                    act.wait_ge(tp_full, ONE + b * TP_N + n + 1)
                    src = tp[:, n % 2, :].rearrange("p (c t) -> p c t", c=DC)
                    if col_scale is None:
                        last = nc.scalar.activation(xt[:, :, PAD + n * 2 * P:PAD + (n + 1) * 2 * P], src, ACT.Copy)
                    else:
                        for c in range(DC):
                            last = nc.scalar.activation(xt[:, c, n * 2 * P:(n + 1) * 2 * P], src[:, c, :], ACT.Identity,
                                                        scale=cs[:, c:c + 1])
                    last.then_inc(tp_free[n % 2], 1)
                if not topk:
                    for n in range(4):
                        c, which = n // 2, n % 2
                        act.wait_ge(sc_full, b * SC_N + n + 1)
                        if n:
                            act.wait_ge(part_full, b * 4 + n)
                        if bias is None:
                            last = nc.scalar.activation(qf[:], sc[:, n % 2, :], ACT.Copy, scale=(0.25 if which == 0 else 1.0))
                        else:
                            bcol = (bqk4 if which == 0 else bqk)[:, which * DC + c:which * DC + c + 1]
                            last = nc.scalar.activation(qf[:], sc[:, n % 2, :], ACT.Identity, bias=bcol,
                                                        scale=(0.25 if which == 0 else 1.0))
                        last.then_inc(sc_free[n % 2], 1)
                for n in range(TP_ROWS, TP_PRE):
                    act.wait_ge(tp_full, ONE + b * TP_N + n + 1)
                    t = 2 * (n - TP_ROWS)
                    nc.scalar.activation(v[:, t:t + 2, :], tp[:, n % 2, :].rearrange("p (t d) -> p t d", t=2),
                                         ACT.Copy).then_inc(tp_free[n % 2], 1)
                for i in range(NTILE + 1):
                    if i < NTILE:
                        h, q = tiles[i]
                        n = SC_PRE + i
                        w = len(blocks[q]) * P
                        if i >= 2:
                            act.wait_ge(tp_full, ONE + b * TP_N + TP_PRE + chunk0[i - 1])
                        act.wait_ge(max_full, b * NTILE + i + 1)
                        if topk:
                            nc.scalar.activation(e[:, i % 2, 0:w], sc[:, n % 2, 0:w], ACT.Exp,
                                                 bias=nmax[:, h % 2, q:q + 1]).then_inc(e_full, 1)
                        else:
                            nc.scalar.activation(e[:, i % 2, 0:w], sc[:, n % 2, 0:w], ACT.Exp,
                                                 bias=nmax[:, h % 2, q:q + 1],
                                                 accum_out=rowsum[:, h % 2, q:q + 1]).then_inc(sc_free[n % 2], 1)
                    if i >= 1:
                        copy_chunk(b, i - 1)
                base = TP_PRE + TP_PT
                for n in range(base, base + TB // 2):
                    act.wait_ge(tp_full, ONE + b * TP_N + n + 1)
                    t = 2 * (n - base)
                    nc.scalar.activation(ot[:, :, t * P:(t + 2) * P], tp[:, n % 2, :].rearrange("p (c t) -> p c t", c=DC),
                                         ACT.Copy).then_inc(tp_free[n % 2], 1)

        if topk:
            @block.gpsimd
            def _(pool):
                nc.gpsimd.iota(qf[:], pattern=[[1, S]], base=0, channel_multiplier=0,
                               allow_small_or_imprecise_dtypes=True).then_inc(pos_full, 1)

        @block.vector
        def _(dve):
            dve.sem_inc(o_full, ONE)
            if topk:
                for i in range(2):
                    dve.sem_inc(sc_free[i], ONE)
            TWO_PI = 2 * pi
            if topk:
                dve.wait_ge(w_in, 16 * n_in)
                nc.vector.memset(xt[:, :, 0:PAD], 0.0)
                MAGIC = 12582912.0
                TWO_PI_MID = 4058 * 2.0 ** -21
                PI_PARTS = (6.28125, TWO_PI_MID, TWO_PI - 6.28125 - TWO_PI_MID)
                pos = qf
                for n in range(DC + 1):
                    gain_n = [gain[:, 0, :], gain[:, 1, :]][n] if n < DC else None
                    nc.vector.tensor_scalar(hp[:], freq[:, n:n + 1] if n < DC else theta[:], TWO_PI, None, ALU.mult)
                    if n == 0:
                        dve.wait_ge(pos_full, 1)
                    dve.drain()
                    nc.vector.tensor_scalar(work[:] if n == 0 else rest[:], pos[:], hp[:], None, ALU.mult)
                    dve.drain()
                    a = e[:, 0, :]
                    k = e[:, 1, :]
                    nc.vector.tensor_scalar(a, work[:] if n == 0 else rest[:], 0.01,
                                            phase[:, n:n + 1] if n < DC else 0.0, ALU.mult, ALU.add)
                    dve.drain()
                    nc.vector.tensor_scalar(k, a, 1.0 / TWO_PI, 0.25, ALU.mult, ALU.add)
                    dve.drain()
                    nc.vector.tensor_scalar(k, k, MAGIC, None, ALU.add)
                    dve.drain()
                    nc.vector.tensor_scalar(k, k, MAGIC, None, ALU.subtract)
                    dve.drain()
                    for pp in PI_PARTS:
                        nc.vector.scalar_tensor_tensor(out=a, in0=k, scalar=-pp, in1=a, op0=ALU.mult, op1=ALU.add)
                        dve.drain()
                    nc.vector.tensor_scalar(rest[:], a, pi / 2, 3.1415925, ALU.add, ALU.min)
                    dve.drain()
                    nc.vector.tensor_scalar(rest[:], rest[:], -3.1415925, None, ALU.max).then_inc(gain_phase, 1)
                    dve.wait_ge(gain_sin, n + 1)
                    if n < DC:
                        nc.vector.tensor_scalar(gain_n, work[:], 0.3, 0.5, ALU.mult, ALU.add)
                        dve.drain()
                    else:
                        for c in range(DC):
                            nc.vector.scalar_tensor_tensor(out=gain[:, c, :], in0=work[:], scalar=0.2,
                                                           in1=gain[:, c, :], op0=ALU.mult, op1=ALU.add)
                        dve.drain()

            def split(b, n):
                dve.wait_ge(part_out, ONE + (b * 4 + n) * 48)
                nc.vector.tensor_copy(part[0][:], qf[:])
                dve.drain()
                nc.vector.tensor_tensor(rest[:], qf[:], part[0][:], ALU.subtract)
                dve.drain()
                nc.vector.tensor_copy(part[1][:], rest[:])
                dve.drain()
                nc.vector.tensor_tensor(part[2][:], rest[:], part[1][:], ALU.subtract)
                dve.drain().then_inc(part_full, 1)

            def convolve(b, i):
                for j in range(4):
                    if j == 0:
                        nc.vector.tensor_scalar(conv[:], xt[:, :, 0:S], taps[:, i, 0:1], None, ALU.mult)
                    else:
                        for c in range(DC):
                            nc.vector.scalar_tensor_tensor(out=conv[:, c, :], in0=xt[:, c, j:j + S],
                                                           scalar=taps[:, i, j:j + 1], in1=conv[:, c, :],
                                                           op0=ALU.mult, op1=ALU.add)
                    dve.drain()

            def copy_chunk(b, i):
                for j, ch in enumerate(chunks[tiles[i][1]]):
                    n = chunk0[i] + j
                    if on_vector(n):
                        dve.wait_ge(tp_full, ONE + b * TP_N + TP_PRE + n + 1)
                        dve.wait_ge(pt_used, ONE + b * TP_PT + max(0, n - 3))
                        nc.vector.tensor_copy(pt[:, n % 4, 0:len(ch) * P],
                                              tp[:, (TP_PRE + n) % 2, 0:len(ch) * P]).then_inc(tp_free[(TP_PRE + n) % 2], 1)

            def head_out(b, h):
                dve.wait_ge(ov_ready(b, h)[0], ov_ready(b, h)[1])
                nc.vector.reciprocal(rinv[:], rowsum[:, h % 2, :])
                dve.drain()
                nc.vector.tensor_tensor(o[:, :, h * HD:(h + 1) * HD],
                                        ov[:, h % 2, 0:QN * HD].rearrange("p (q d) -> p q d", d=HD),
                                        rinv[:].rearrange("p (q a) -> p q a", a=1).to_broadcast([P, QN, HD]),
                                        ALU.mult).then_inc(o_full, 1)

            def ov_ready(b, h):
                return pt_used, ONE + b * TP_PT + (h + 1) * T_HEAD

            with dve.Fori(0, B) as b:
                for t in range(TB):
                    if t >= 2:
                        dve.wait_ge(tp_full, ONE + b * TP_N + t // 2 - 1)
                    rows(xrow[:, t % 4, :], b * TB + t).then_inc(row_full, 1)
                if not topk:
                    for n in range(4):
                        sc_taken(dve, b, n)
                        split(b, n)
                else:
                    tp_copied(dve, b, TP_ROWS - 2)
                    tp_copied(dve, b, TP_ROWS - 1)
                    for n in range(4):
                        c, which = n // 2, n % 2
                        convolve(b, which)
                        dve.drain().then_inc(conv_full, 1)
                        f = 2 * n
                        dve.wait_ge(sc_full, b * SC_N + f + 1)
                        nc.vector.scalar_tensor_tensor(out=qf[:], in0=sc[:, f % 2, :], scalar=(0.25 if which == 0 else 1.0),
                                                       in1=gain[:, c, :], op0=ALU.mult, op1=ALU.mult
                                                       ).then_inc(sc_free[f % 2], 1)
                        dve.drain()
                        nc.vector.tensor_tensor(work[:], qf[:], cos_t[:], ALU.mult)
                        dve.wait_ge(sc_full, b * SC_N + f + 2)
                        nc.vector.tensor_tensor(rest[:], sc[:, (f + 1) % 2, :], sin_t[:], ALU.mult)
                        dve.drain().then_inc(sc_free[(f + 1) % 2], 1)
                        nc.vector.tensor_tensor(qf[:], work[:], rest[:], ALU.add)
                        dve.drain()
                        split(b, n)
                    convolve(b, 2)
                    dve.drain().then_inc(conv_full, 1)
                for i in range(NTILE + 4):
                    if i < NTILE:
                        h, q = tiles[i]
                        n = SC_PRE + i
                        w = len(blocks[q]) * P
                        if q == 0 and not topk:
                            dve.drain()
                        dve.wait_ge(sc_full, b * SC_N + n + 1)
                        if not topk:
                            nc.vector.tensor_reduce(nmax[:, h % 2, q:q + 1], sc[:, n % 2, 0:w], AX.X, ALU.max,
                                                    negate=True).then_inc(max_full, 1)
                        else:
                            nc.vector.tensor_copy(work[:, 0:w], sc[:, n % 2, 0:w])
                            dve.drain()
                            for r in range((TOPK + 7) // 8):
                                nc.vector.max(top8[:, r % 2, :], work[:, 0:w])
                                dve.drain()
                                if r == 0:
                                    nc.vector.tensor_scalar(nmax[:, h % 2, q:q + 1], top8[:, 0, 0:1], -1.0, None,
                                                            ALU.mult).then_inc(max_full, 1)
                                if r < (TOPK + 7) // 8 - 1:
                                    nc.vector.match_replace(work[:, 0:w], top8[:, r % 2, :], work[:, 0:w], GONE)
                                    dve.drain()
                            kth = top8[:, ((TOPK + 7) // 8 - 1) % 2, (TOPK - 1) % 8:(TOPK - 1) % 8 + 1]
                            dve.wait_ge(e_full, b * NTILE + i + 1)
                            nc.vector.scalar_tensor_tensor(out=e[:, i % 2, 0:w], in0=sc[:, n % 2, 0:w], scalar=kth,
                                                           in1=e[:, i % 2, 0:w], op0=ALU.is_ge, op1=ALU.mult,
                                                           accum_out=rowsum[:, h % 2, q:q + 1]
                                                           ).then_inc(sc_free[n % 2], 1)
                    if 1 <= i <= NTILE:
                        copy_chunk(b, i - 1)
                    if i >= 4 and (i - 4) % QN == QN - 1:
                        head_out(b, (i - 4) // QN)
                base = TP_PRE + TP_PT + TB // 2
                for n in range(base, base + TB // 2):
                    dve.wait_ge(tp_full, ONE + b * TP_N + n + 1)
                    t = 2 * (n - base)
                    tv = target[:, bass.ds(b * TB + t, 2), :]
                    nc.vector.tensor_tensor(tv, tp[:, n % 2, :].rearrange("p (t d) -> p t d", t=2), tv,
                                            ALU.add).then_inc(tp_free[n % 2], 1)



def mlp_gated_by_top2(core, name, xn, rinv, norm_dram, gate_dram, up_dram, down_dram):
    nc = core.nc
    ED, NE = 1024, 8
    BLK = 512
    BT = BLK // P
    NB = B * S // BLK
    EC = ED // P
    with Stage(core, name) as st:
        up_w = st.sb("up_w", [P, DC, ED])
        down_w = st.sb("down_w", [P, EC, D])
        gate_w = st.sb("gate_w", [P, DC, NE])
        n2 = st.sb("n2", [P, DC])
        xrow = st.sb("xrow", [P, BT, D])
        xt = st.sb("xt", [P, DC, BLK])
        h = st.sb("h", [P, EC, BLK])
        gp = st.sb("gp", [P, BT, NE])
        gm, gs, top2, w = (st.sb(n, [P, BT]) for n in ("gm", "gs", "top2", "w"))
        best = st.sb("best", [P, BT, 8])
        up = st.ps("up", [P, 4, 512])
        dn = st.ps("dn", [P, 4, 512])
        w_in = st.sem("w_in")
        row_full, tr_full, lg_full = st.sem("row_full"), st.sem("tr_full"), st.sem("lg_full")
        shifted, exp_full = st.sem("shifted"), st.sem("exp_full")
        up_full = st.sem("up_full")
        up_free = [st.sem(f"up_free{i}") for i in range(4)]
        dn_full, dn_used = st.sem("dn_full"), st.sem("dn_used")
        block = st.block()
        DN = BT + 3
        UPS = EC // 4

        @block.sync
        def _(sp):
            sp.dma_start(gate_w[:], gate_dram.rearrange("(c p) n -> p c n", p=P)).then_inc(w_in, 16)
            sp.dma_start(n2[:], norm_dram).then_inc(w_in, 16)
            sp.dma_start(up_w[:], up_dram.rearrange("(c p) n -> p c n", p=P)).then_inc(w_in, 16)
            sp.dma_start(down_w[:], down_dram.rearrange("(c p) n -> p c n", p=P)).then_inc(w_in, 16)

        @block.tensor
        def _(pe):
            pe.sem_inc(tr_full, ONE)
            pe.wait_ge(w_in, 64)
            with pe.Fori(0, NB) as k:
                pe.wait_ge(dn_used, ONE + k * DN)
                for t in range(BT):
                    pe.wait_ge(row_full, k * BT + t + 1)
                    for c in range(DC):
                        o = (c * 2 + t % 2) * P
                        last = nc.tensor.transpose(dn[:, t // 2, o:o + P], xrow[:, t, c * P:(c + 1) * P], core.ident[:])
                last.then_inc(tr_full, 1)
                pe.wait_ge(dn_used, ONE + k * DN + 2)
                for t in range(BT):
                    for c in range(DC):
                        last = nc.tensor.matmul(dn[:, 2, t * NE:(t + 1) * NE], xt[:, c, t * P:(t + 1) * P],
                                                gate_w[:, c, :], start=(c == 0), stop=(c == DC - 1))
                last.then_inc(lg_full, 1)
                for u in range(EC):
                    pe.wait_ge(up_free[u % 4], ONE + k * UPS + u // 4)
                    for c in range(DC):
                        last = nc.tensor.matmul(up[:, u % 4, :], up_w[:, c, u * P:(u + 1) * P], xt[:, c, :],
                                                start=(c == 0), stop=(c == DC - 1))
                    last.then_inc(up_full, 1)
                for i in range(4):
                    pe.wait_ge(up_free[i], ONE + (k + 1) * UPS)
                pe.wait_ge(dn_used, ONE + k * DN + 3)
                for t in range(BT):
                    for m in range(EC):
                        last = nc.tensor.matmul(dn[:, t, 0:D], h[:, m, t * P:(t + 1) * P], down_w[:, m, :],
                                                start=(m == 0), stop=(m == EC - 1))
                    last.then_inc(dn_full, 1)

        @block.scalar
        def _(act):
            act.sem_inc(dn_used, ONE)
            act.sem_inc(up_free[0], ONE)
            act.sem_inc(up_free[1], ONE)
            act.sem_inc(up_free[2], ONE)
            act.sem_inc(up_free[3], ONE)
            act.wait_ge(w_in, 64)
            with act.Fori(0, NB) as k:
                act.wait_ge(tr_full, ONE + k + 1)
                for n in range(BT // 2):
                    for c in range(DC):
                        last = nc.scalar.activation(xt[:, c, n * 2 * P:(n + 1) * 2 * P], dn[:, n, c * 2 * P:(c + 1) * 2 * P],
                                                    ACT.Identity, scale=n2[:, c:c + 1])
                    last.then_inc(dn_used, 1)
                act.wait_ge(shifted, k + 1)
                nc.scalar.activation(gp[:], gp[:], ACT.Exp).then_inc(exp_full, 1)
                for u in range(EC):
                    act.wait_ge(up_full, k * EC + u + 1)
                    nc.scalar.activation(h[:, u, :], up[:, u % 4, :], ACT.Silu).then_inc(up_free[u % 4], 1)

        @block.vector
        def _(dve):
            def over_experts(v):
                return v[:].rearrange("p (t a) -> p t a", a=1).to_broadcast([P, BT, NE])

            with dve.Fori(0, NB) as k:
                for t in range(BT):
                    dve.wait_ge(tr_full, ONE + k)
                    nc.vector.tensor_scalar(xrow[:, t, :], xn[:, bass.ds(k * BT + t, 1), :].rearrange("p a d -> p (a d)"),
                                            rinv[:, bass.ds(k * BT + t, 1)], None, ALU.mult).then_inc(row_full, 1)
                dve.wait_ge(lg_full, k + 1)
                lg = dn[:, 2, 0:BT * NE].rearrange("p (t e) -> p t e", e=NE)
                nc.vector.tensor_reduce(gm[:], lg, AX.X, ALU.max)
                dve.drain()
                nc.vector.tensor_tensor(gp[:], lg, over_experts(gm), ALU.subtract)
                dve.drain().then_inc(shifted, 1)
                dve.wait_ge(exp_full, k + 1)
                nc.vector.tensor_reduce(gs[:], gp[:], AX.X, ALU.add).then_inc(dn_used, 1)
                dve.drain()
                nc.vector.reciprocal(gs[:], gs[:])
                dve.drain()
                nc.vector.tensor_tensor(gp[:], gp[:], over_experts(gs), ALU.mult)
                dve.drain()
                for t in range(BT):
                    nc.vector.max(best[:, t, :], gp[:, t, :])
                dve.drain()
                nc.vector.tensor_reduce(top2[:], best[:, :, 0:2], AX.X, ALU.add)
                dve.drain()
                nc.vector.tensor_scalar(w[:], top2[:], 1e-9, None, ALU.add)
                dve.drain()
                nc.vector.reciprocal(w[:], w[:])
                dve.drain()
                nc.vector.tensor_tensor(w[:], w[:], top2[:], ALU.mult)
                dve.drain()
                for t in range(BT):
                    nv = xn[:, bass.ds(k * BT + t, 1), :].rearrange("p a d -> p (a d)")
                    xv = core.x[:, bass.ds(k * BT + t, 1), :].rearrange("p a d -> p (a d)")
                    dve.wait_ge(dn_full, k * BT + t + 1)
                    nc.vector.scalar_tensor_tensor(out=nv, in0=dn[:, t, 0:D], scalar=w[:, t:t + 1], in1=nv,
                                                   op0=ALU.mult, op1=ALU.add).then_inc(dn_used, 1)
                    dve.drain()
                    nc.vector.tensor_tensor(xv, xv, nv, ALU.add)



def build(nc, a, out, upto=99):
    ctx = ExitStack()
    with ctx:
        core = Core(nc, ctx)
        scratch = nc.dram_tensor("qk_parts", [2, 3, D, S], BF16, kind="Internal").ap()
        load_and_constants(core, a["x"])

        def layernormed(dst, at):
            return nc.vector.tensor_scalar(dst, core.x[:, bass.ds(at, 1), :].rearrange("p a d -> p (a d)"),
                                           core.mean_var[:, bass.ds(at, 1), 0], core.rstd[:, bass.ds(at, 1)],
                                           ALU.subtract, ALU.mult)

        def l0_ffn(name):
            layernorm_statistics(core, name + "_stat")
            moe_shared_and_routed(core, name, a["router"], a["router_bias"], a["sw1"], a["sw3"], a["sw2"], a["ew1"], a["ew2"])

        def l1_ffn(name):
            layernorm_statistics(core, name + "_stat")
            with Stage(core, name + "_rows") as st:
                xn = st.sb("xn", [P, NT, D])
                rinv = st.sb("rinv", [P, NT])
                layernorm_rows(core, name + "_ln", xn)
                rms_statistics(core, name + "_rms1", xn, rinv)

                def rms_rows(dst, at):
                    return nc.vector.tensor_scalar(dst, xn[:, bass.ds(at, 1), :].rearrange("p a d -> p (a d)"),
                                                   rinv[:, bass.ds(at, 1)], None, ALU.mult)

                attention(core, name + "_attn", a["f_qkv"], a["f_o"], scratch, causal=True, target=xn,
                          rows=rms_rows, col_scale=a["n1"])
                rms_statistics(core, name + "_rms2", xn, rinv)
                mlp_gated_by_top2(core, name + "_mlp", xn, rinv, a["n2"], a["gate"], a["up"], a["down"])

        stages = [
            lambda: (layernorm_statistics(core, "s1"), holographic(core, a["holo_wt"], a["holo_wout"], a["dft"])),
            lambda: l0_ffn("ffn1"),
            lambda: (layernorm_statistics(core, "s3"), delta_memory(core, a["kvq"])),
            lambda: l0_ffn("ffn2"),
            lambda: (layernorm_statistics(core, "s5"),
                     attention(core, "attn_a", a["a_qkv"], a["a_out"], scratch, causal=False, target=core.x,
                               rows=layernormed, bias=(a["a_bqk"], a["a_bv"]), out_bias=a["a_bout"])),
            lambda: l1_ffn("ffn3"),
            lambda: (layernorm_statistics(core, "s7"),
                     attention(core, "attn_b", a["b_qkv"], a["b_proj"], scratch, causal=True, target=core.x,
                               rows=layernormed, out_bias=a["b_bias"],
                               fancy=dict(taps=[a["tq"], a["tk"], a["tv"]], cos=a["cos"], sin=a["sin"],
                                          swap=a["swap"], gamma=a["gamma"], phase=a["phase"], theta=a["theta"]))),
            lambda: l1_ffn("ffn4"),
        ]
        for s in ([stages[i] for i in upto] if isinstance(upto, (list, tuple)) else stages[:upto]):
            s()
        store(core, out)


def shape_tables(np):
    n = np.arange(32)
    ang = 2 * np.pi * ((n[:, None] * n[None, :]) % 32) / 32
    eye = np.eye(4)
    fwd = [np.kron(eye, np.cos(ang)), np.kron(eye, -np.sin(ang))]
    dft = np.stack(fwd + [m / 32 for m in fwd]).astype(np.float32)
    inv_freq = np.float32(1.0) / np.power(np.float32(10000.0), np.arange(0, HD, 2, dtype=np.float32) / np.float32(HD))
    freqs = (np.arange(S, dtype=np.float32)[None, :] * inv_freq.astype(np.float32)[:, None]).astype(np.float32)
    r = np.arange(P)
    cos = np.cos(freqs.astype(np.float64))[(r % HD) // 2].astype(np.float32)
    sin = (np.sin(freqs.astype(np.float64))[(r % HD) // 2] * np.where(r % 2, 1.0, -1.0)[:, None]).astype(np.float32)
    swap = np.zeros((P, P), np.float32)
    swap[r, r ^ 1] = 1.0
    return {"dft": dft, "cos": cos, "sin": sin, "swap": swap}


def layout(inputs, np):
    def arr(k):
        return np.asarray(inputs[k])

    def columns(v):
        return np.ascontiguousarray(v.reshape(-1, P).T)

    c = np.ascontiguousarray
    f = {
        "x": arr("L0_attn_a_x").reshape(B * S, D),
        "holo_wt": c(arr("L0_attn_a_w_qkv").T), "holo_wout": arr("L0_attn_a_w_out"),
        "router": c(arr("L0_ffn_router_w").T), "router_bias": arr("L0_ffn_router_bias"),
        "sw1": arr("L0_ffn_sw1"), "sw3": arr("L0_ffn_sw3"), "sw2": arr("L0_ffn_sw2"),
        "ew1": arr("L0_ffn_ew1"), "ew2": arr("L0_ffn_ew2"),
        "kvq": c(np.concatenate([arr("L0_attn_b_W_k").T, arr("L0_attn_b_W_v").T, arr("L0_attn_b_W_q").T], axis=1)),
        "a_qkv": arr("L1_attn_a_w_qkv"), "a_bqk": columns(arr("L1_attn_a_b_qkv")[0:2 * D]),
        "a_bv": arr("L1_attn_a_b_qkv")[2 * D:3 * D].reshape(1, D),
        "a_out": arr("L1_attn_a_w_out"), "a_bout": arr("L1_attn_a_b_out"),
        "b_qkv": c(arr("L1_attn_b_qkv_w").T), "b_proj": c(arr("L1_attn_b_proj_w").T), "b_bias": arr("L1_attn_b_proj_b"),
        "tq": arr("L1_attn_b_kernel_q"), "tk": arr("L1_attn_b_kernel_k"), "tv": arr("L1_attn_b_kernel_v"),
        "gamma": columns(arr("L1_attn_b_gamma_freq")), "theta": arr("L1_attn_b_theta_freq"), "phase": columns(arr("L1_attn_b_phase")),
        "n1": columns(arr("L1_ffn_n1_w")), "f_qkv": c(arr("L1_ffn_qkv_w").T), "f_o": c(arr("L1_ffn_o_w").T),
        "n2": columns(arr("L1_ffn_n2_w")), "gate": c(arr("L1_ffn_gate_w").T), "up": c(arr("L1_ffn_up_w").T),
        "down": c(arr("L1_ffn_down_w").T),
    }
    f.update(shape_tables(np))
    return f


def kernel(**inputs):
    import numpy as np
    import concourse.bacc as bacc
    from concourse.bass_utils import run_bass_kernel_spmd as run

    arrays = layout(inputs, np)
    nc = bacc.Bacc("TRN2", target_bir_lowering=False, num_devices=1)
    args = {k: nc.dram_tensor(f"in_{k}", v.shape, mybir.dt.from_np(v.dtype), kind="ExternalInput").ap()
            for k, v in arrays.items()}
    out = nc.dram_tensor("out", (B * S, D), F32, kind="ExternalOutput").ap()
    build(nc, args, out)
    r = run(nc, [{f"in_{k}": v for k, v in arrays.items()}], core_ids=[0])
    return r.results[0]["out"].reshape(B, S, D)
```

```python
import concourse.bass as bass
from concourse import mybir
from contextlib import ExitStack
from math import erf, exp, pi, sqrt

F32 = mybir.dt.float32
BF16 = mybir.dt.bfloat16
U32 = mybir.dt.uint32
ALU = mybir.AluOpType
ACT = mybir.ActivationFunctionType
AX = mybir.AxisListType

P = 128
B, S, D = 4, 1024, 256
NT = B * S // P
TB = S // P
DC = D // P
NEG = -1.0e30
GONE = -3.0e38
NH, HD = 16, 16
HC = P // HD
TOPK = max(1, int(S * 0.1))
ONE = 1
LN_EPS, RMS_EPS = 1e-5, 1e-6

Q_PART = (0, 0, 1, 1, 0, 2)
K_PART = (0, 1, 0, 1, 2, 0)
QK_ROWS = len(Q_PART) * HD
VH = HD + 1


class Core:

    def __init__(self, nc, ctx):
        self.nc = nc
        self.numbers = sorted(nc.free_semaphores)
        self.turn = 0

        def sb(name, shape, dt=F32):
            return ctx.enter_context(nc.sbuf_tensor(name, shape, dt))

        self.x = sb("x", [P, NT, D])
        self.ident = sb("ident", [P, P])
        self.ident_bf = sb("ident_bf", [P, P], BF16)
        self.above = sb("above", [P, P], BF16)
        self.below = sb("below", [P, P], BF16)
        self.ones = sb("ones", [1, P])
        self.mean_var = sb("mean_var", [P, NT, 2])
        self.rstd = sb("rstd", [P, NT])


class Stage:

    def __init__(self, core, name):
        self.core, self.nc, self.name = core, core.nc, name
        self.ctx = ExitStack()
        self.sems = []

    def __enter__(self):
        self.ctx.__enter__()
        return self

    def __exit__(self, *a):
        done = self.ctx.__exit__(*a)
        if self.sems and a[0] is None:
            self.nc.clear_and_free_semaphores(self.sems)
        return done

    def sb(self, name, shape, dt=F32):
        return self.ctx.enter_context(self.nc.sbuf_tensor(f"{self.name}_{name}", shape, dt))

    def ps(self, name, shape, dt=F32):
        return self.ctx.enter_context(self.nc.psum_tensor(f"{self.name}_{name}", shape, dt))

    def sem(self, name):
        number = self.core.numbers[self.core.turn % len(self.core.numbers)]
        self.core.turn += 1
        self.sems.append(self.nc.alloc_semaphore(f"{self.name}_{name}", num=number))
        return self.sems[-1]

    def block(self):
        return self.ctx.enter_context(self.nc.Block())



def load_and_constants(core, x_dram):
    nc = core.nc
    with Stage(core, "start") as st:
        x_loaded, zeroed, ready = st.sem("x_loaded"), st.sem("zeroed"), st.sem("ready")
        block = st.block()

        @block.sync
        def _(sp):
            xv = x_dram.rearrange("(t p) d -> p t d", p=P)
            for b in range(B):
                sp.dma_start(core.x[:, b * TB:(b + 1) * TB, :], xv[:, b * TB:(b + 1) * TB, :]).then_inc(x_loaded, 16)
            sp.wait_ge(x_loaded, 16 * B)

        @block.gpsimd
        def _(pool):
            for t in (core.ident, core.ident_bf, core.above, core.below):
                nc.gpsimd.memset(t[:], 0.0).then_inc(zeroed, 1)
            nc.gpsimd.memset(core.ones[:], 1.0)
            pool.wait_ge(zeroed, 4)
            for t in (core.ident, core.ident_bf):
                nc.gpsimd.affine_select(out=t[:], in_=t[:], compare_op=ALU.not_equal, fill=1.0,
                                        base=0, pattern=[[-1, P]], channel_multiplier=1).then_inc(ready, 1)
            nc.gpsimd.affine_select(out=core.above[:], in_=core.above[:], compare_op=ALU.is_ge, fill=NEG,
                                    base=0, pattern=[[-1, P]], channel_multiplier=1).then_inc(ready, 1)
            nc.gpsimd.affine_select(out=core.below[:], in_=core.below[:], compare_op=ALU.is_ge, fill=NEG,
                                    base=0, pattern=[[1, P]], channel_multiplier=-1).then_inc(ready, 1)
            pool.wait_ge(ready, 4)


def store(core, out_dram):
    with Stage(core, "end") as st:
        stored = st.sem("stored")
        block = st.block()

        @block.sync
        def _(sp):
            ov = out_dram.rearrange("(t p) d -> p t d", p=P)
            for b in range(B):
                sp.dma_start(ov[:, b * TB:(b + 1) * TB, :], core.x[:, b * TB:(b + 1) * TB, :]).then_inc(stored, 16)
            sp.wait_ge(stored, 16 * B)



def layernorm_statistics(core, name):
    nc = core.nc
    with Stage(core, name) as st:
        parts = st.sb("parts", [P, NT, 6])
        std = st.sb("std", [P, NT])
        var_ready, std_ready = st.sem("var_ready"), st.sem("std_ready")
        eps = st.sb("eps", [P, 1])
        block = st.block()

        @block.vector
        def _(dve):
            nc.vector.memset(eps[:], LN_EPS)
            for t in range(NT):
                nc.vector.bn_stats(parts[:, t, :], core.x[:, t, :])
            dve.drain()
            for t in range(NT):
                last = nc.vector.bn_aggr(core.mean_var[:, t, :], parts[:, t, :])
            last.then_inc(var_ready, 1)
            dve.wait_ge(std_ready, 1)
            nc.vector.reciprocal(core.rstd[:], std[:])

        @block.scalar
        def _(act):
            act.wait_ge(var_ready, 1)
            nc.scalar.activation(std[:], core.mean_var[:, :, 1], ACT.Sqrt, bias=eps[:]).then_inc(std_ready, 1)


def layernorm_rows(core, name, xn):
    nc = core.nc
    with Stage(core, name) as st:
        block = st.block()

        @block.vector
        def _(dve):
            for t in range(NT):
                nc.vector.tensor_scalar(xn[:, t, :], core.x[:, t, :], core.mean_var[:, t, 0:1],
                                        core.rstd[:, t:t + 1], ALU.subtract, ALU.mult)


def rms_statistics(core, name, xn, rinv):
    nc = core.nc
    with Stage(core, name) as st:
        sums = st.sb("sums", [P, NT])
        std = st.sb("std", [P, NT])
        junk = st.sb("junk", [P, D])
        eps = st.sb("eps", [P, 1])
        sums_ready, std_ready = st.sem("sums_ready"), st.sem("std_ready")
        block = st.block()

        @block.vector
        def _(dve):
            nc.vector.memset(eps[:], RMS_EPS)
            for t in range(NT):
                last = nc.vector.tensor_tensor_reduce(
                    out=junk[:], in0=xn[:, t, :], in1=xn[:, t, :], scale=1.0, scalar=0.0,
                    op0=ALU.mult, op1=ALU.add, accum_out=sums[:, t:t + 1])
                dve.drain()
            dve.drain().then_inc(sums_ready, 1)
            dve.wait_ge(std_ready, 1)
            nc.vector.reciprocal(rinv[:], std[:])

        @block.scalar
        def _(act):
            act.wait_ge(sums_ready, 1)
            nc.scalar.activation(std[:], sums[:], ACT.Sqrt, bias=eps[:], scale=1.0 / D).then_inc(std_ready, 1)



def holographic(core, wt_dram, wout_dram, dft_dram):
    nc = core.nc
    NJ = 3 * DC
    with Stage(core, "holo") as st:
        wt = st.sb("wt", [P, NJ, D])
        wout = st.sb("wout", [P, DC, D])
        dft = st.sb("dft", [P, 4, P])
        wf = st.sb("wf", [P, DC, NJ, 2, P])
        wg = st.sb("wg", [P, DC, 2, D])
        xrow = st.sb("xrow", [P, 4, D])
        xt = st.sb("xt", [P, DC, S])
        kre, kim = st.sb("kre", [P, S]), st.sb("kim", [P, S])
        t1, t2, t3, t4 = (st.sb(f"t{i}", [P, S]) for i in range(1, 5))
        kvr, kvi = st.sb("kvr", [P, S]), st.sb("kvi", [P, S])
        ar, ai = st.sb("ar", [P, DC, S]), st.sb("ai", [P, DC, S])
        ps = st.ps("ps", [P, 4, 2, 512])

        w_in, fold_full, fold_free = st.sem("w_in"), st.sem("fold_full"), st.sem("fold_free")
        row_full = st.sem("row_full")
        tr_full, xt_full = st.sem("tr_full"), st.sem("xt_full")
        pr_full, k_full = st.sem("pr_full"), st.sem("k_full")
        v_used, q_used = st.sem("v_used"), st.sem("q_used")
        prod_full, a_full = st.sem("prod_full"), st.sem("a_full")
        y_full, y_used = st.sem("y_full"), st.sem("y_used")
        block = st.block()
        NF = NJ * DC

        @block.sync
        def _(sp):
            sp.dma_start(wt[:], wt_dram.rearrange("(j p) d -> p j d", p=P)).then_inc(w_in, 16)
            sp.dma_start(wout[:], wout_dram.rearrange("(c p) d -> p c d", p=P)).then_inc(w_in, 16)
            sp.dma_start(dft[:], dft_dram.rearrange("a p n -> p a n")).then_inc(w_in, 16)

        @block.tensor
        def _(pe):
            pe.sem_inc(tr_full, ONE)
            pe.sem_inc(y_full, ONE)
            pe.wait_ge(w_in, 48)
            for j in range(NJ):
                for c in range(DC):
                    n = j * DC + c
                    if n >= 4:
                        pe.wait_ge(fold_free, n - 3)
                    for part in range(2):
                        last = nc.tensor.matmul(ps[:, n % 4, 0, part * P:part * P + P],
                                                wt[:, j, c * P:(c + 1) * P], dft[:, part, :], start=True, stop=True)
                    last.then_inc(fold_full, 1)
            for c in range(DC):
                for part in range(2):
                    n = NF + c * 2 + part
                    pe.wait_ge(fold_free, n - 3)
                    nc.tensor.matmul(ps[:, n % 4, 0, 0:D], dft[:, 2 + part, :], wout[:, c, :],
                                     start=True, stop=True).then_inc(fold_full, 1)
            pe.wait_ge(fold_free, NF + 2 * DC)
            with pe.Fori(0, B) as b:
                pe.wait_ge(y_used, ONE + b * TB)
                for t in range(TB):
                    pe.wait_ge(row_full, b * TB + t + 1)
                    for c in range(DC):
                        last = nc.tensor.transpose(ps[:, t // 2, 0, (c * 2 + t % 2) * P:(c * 2 + t % 2 + 1) * P],
                                                   xrow[:, t % 4, c * P:(c + 1) * P], core.ident[:])
                    if t % 2:
                        last.then_inc(tr_full, 1)
                pe.wait_ge(xt_full, (b + 1) * (TB // 2))

                def project(which, c, part, slot):
                    for half in range(2):
                        for d in range(DC):
                            last = nc.tensor.matmul(ps[:, slot, half, :], wf[:, d, which * DC + c, part, :],
                                                    xt[:, d, half * 512:(half + 1) * 512],
                                                    start=(d == 0), stop=(d == DC - 1))
                    last.then_inc(pr_full, 1)

                for c in range(DC):
                    if c:
                        pe.wait_ge(q_used, b * DC + c)
                    for part in range(2):
                        project(1, c, part, part)
                    if c:
                        pe.wait_ge(v_used, b * DC + c)
                    for part in range(2):
                        project(2, c, part, 2 + part)
                    pe.wait_ge(k_full, b * DC + c + 1)
                    for part in range(2):
                        project(0, c, part, part)
                pe.wait_ge(a_full, (b + 1) * DC)
                for t in range(TB):
                    slot, bank = t % 4, t // 4
                    for n in range(2 * DC):
                        c, part = n // 2, n % 2
                        a = (ar, ai)[part]
                        last = nc.tensor.matmul(ps[:, slot, bank, 0:D], a[:, c, t * P:(t + 1) * P], wg[:, c, part, :],
                                                start=(n == 0), stop=(n == 2 * DC - 1))
                    last.then_inc(y_full, 1)

        @block.scalar
        def _(act):
            for n in range(NF):
                act.wait_ge(fold_full, n + 1)
                nc.scalar.activation(wf[:, n % DC, n // DC, :, :],
                                     ps[:, n % 4, 0, 0:2 * P].rearrange("p (a f) -> p a f", a=2),
                                     ACT.Copy).then_inc(fold_free, 1)
            for n in range(NF, NF + 2 * DC):
                act.wait_ge(fold_full, n + 1)
                nc.scalar.activation(wg[:, (n - NF) // 2, (n - NF) % 2, :], ps[:, n % 4, 0, 0:D],
                                     ACT.Copy).then_inc(fold_free, 1)
            with act.Fori(0, B) as b:
                for n in range(TB // 2):
                    act.wait_ge(tr_full, ONE + b * (TB // 2) + n + 1)
                    nc.scalar.activation(xt[:, :, n * 2 * P:(n + 1) * 2 * P],
                                         ps[:, n, 0, :].rearrange("p (c t) -> p c t", c=DC),
                                         ACT.Copy).then_inc(xt_full, 1)
                for c in range(DC):
                    act.wait_ge(pr_full, b * 6 * DC + c * 6 + 2)
                    if c:
                        act.wait_ge(v_used, b * DC + c)
                    nc.scalar.activation(kre[:], ps[:, 0, :, :].rearrange("p a n -> p (a n)"), ACT.Copy)
                    nc.scalar.activation(kim[:], ps[:, 1, :, :].rearrange("p a n -> p (a n)"),
                                         ACT.Copy).then_inc(k_full, 1)

        @block.vector
        def _(dve):
            dve.sem_inc(y_used, ONE)
            def slot(i):
                return ps[:, i, :, :].rearrange("p a n -> p (a n)")

            with dve.Fori(0, B) as b:
                for t in range(TB):
                    dve.wait_ge(tr_full, ONE + b * (TB // 2) + max(0, t // 2 - 1))
                    nc.vector.tensor_scalar(xrow[:, t % 4, :], core.x[:, bass.ds(b * TB + t, 1), :].rearrange("p a d -> p (a d)"),
                                            core.mean_var[:, bass.ds(b * TB + t, 1), 0], core.rstd[:, bass.ds(b * TB + t, 1)],
                                            ALU.subtract, ALU.mult).then_inc(row_full, 1)
                for c in range(DC):
                    dve.wait_ge(k_full, b * DC + c + 1)
                    dve.wait_ge(pr_full, b * 6 * DC + c * 6 + 4)
                    nc.vector.tensor_tensor(t1[:], kre[:], slot(2), ALU.mult)
                    nc.vector.tensor_tensor(t2[:], kim[:], slot(3), ALU.mult)
                    nc.vector.tensor_tensor(t3[:], kre[:], slot(3), ALU.mult)
                    nc.vector.tensor_tensor(t4[:], kim[:], slot(2), ALU.mult)
                    dve.drain().then_inc(v_used, 1)
                    nc.vector.tensor_tensor_scan(kvr[:], t1[:], t2[:], 0.0, ALU.add, ALU.subtract)
                    nc.vector.tensor_tensor_scan(kvi[:], t3[:], t4[:], 0.0, ALU.add, ALU.add)
                    dve.drain()
                    dve.wait_ge(pr_full, b * 6 * DC + c * 6 + 6)
                    nc.vector.tensor_tensor(t1[:], kvr[:], slot(0), ALU.mult)
                    nc.vector.tensor_tensor(t2[:], kvi[:], slot(1), ALU.mult)
                    nc.vector.tensor_tensor(t3[:], kvi[:], slot(0), ALU.mult)
                    nc.vector.tensor_tensor(t4[:], kvr[:], slot(1), ALU.mult)
                    dve.drain().then_inc(q_used, 1)
                    if c == 0:
                        dve.wait_ge(y_full, ONE + b * TB)
                    nc.vector.tensor_tensor(ar[:, c, :], t1[:], t2[:], ALU.add)
                    nc.vector.tensor_tensor(ai[:, c, :], t3[:], t4[:], ALU.subtract)
                    dve.drain().then_inc(a_full, 1)
                for t in range(TB):
                    xv = core.x[:, bass.ds(b * TB + t, 1), :].rearrange("p a d -> p (a d)")
                    dve.wait_ge(y_full, ONE + b * TB + t + 1)
                    nc.vector.tensor_tensor(xv, ps[:, t % 4, t // 4, 0:D], xv, ALU.add).then_inc(y_used, 1)



def moe_shared_and_routed(core, name, router_dram, bias_dram, sw1, sw3, sw2, ew1, ew2):
    nc = core.nc
    HS, HR, NE = 512, 256, 8
    BLK = 512
    BT = BLK // P
    NB = B * S // BLK
    SC, RC = HS // P, HR // P
    NU = SC * 2 + NE * RC
    with Stage(core, name) as st:
        w1s, w3s = st.sb("w1s", [P, DC, HS]), st.sb("w3s", [P, DC, HS])
        w2s = st.sb("w2s", [P, SC, D])
        w1e = st.sb("w1e", [P, NE, DC, HR])
        w2e = st.sb("w2e", [P, NE, RC, D])
        rw = st.sb("rw", [P, DC, NE])
        rb = st.sb("rb", [P, NE])
        iota = st.sb("iota", [P, NE])
        xrow = st.sb("xrow", [P, BT, D])
        xt = st.sb("xt", [P, DC, BLK])
        sil = st.sb("sil", [P, SC, BLK])
        hs = st.sb("hs", [P, SC, BLK])
        he = st.sb("he", [P, NE * RC, BLK])
        score, sel = st.sb("score", [P, BT, NE]), st.sb("sel", [P, BT, NE])
        best, best_at = st.sb("best", [P, BT, 8]), st.sb("best_at", [P, BT, 8], U32)
        best_f = st.sb("best_f", [P, BT, 8])
        hot, hot2 = st.sb("hot", [P, BT, NE]), st.sb("hot2", [P, BT, NE])
        chosen, denom, inv, big, half = (st.sb(n, [P, BT, NE] if n == "chosen" else [P, BT])
                                         for n in ("chosen", "denom", "inv", "big", "half"))
        comb = st.sb("comb", [P, BT, NE])
        acc = st.sb("acc", [P, BT, D])
        up = st.ps("up", [P, 4, 512])
        dn = st.ps("dn", [P, 4, 512])

        w_in, io = st.sem("w_in"), st.sem("iota")
        row_full, tr_full = st.sem("row_full"), st.sem("tr_full")
        lg_full = st.sem("lg_full")
        up_full = st.sem("up_full")
        up_free = [st.sem(f"up_free{i}") for i in range(4)]
        dn_full, dn_used = st.sem("dn_full"), st.sem("dn_used")
        block = st.block()
        DN = BT * (1 + NE // 2)
        UPS = NU // 4

        @block.sync
        def _(sp):
            sp.dma_start(rw[:], router_dram.rearrange("(c p) n -> p c n", p=P)).then_inc(w_in, 16)
            sp.dma_start(rb[:], bias_dram.partition_broadcast(P)).then_inc(w_in, 16)
            sp.dma_start(w1s[:], sw1.rearrange("(c p) n -> p c n", p=P)).then_inc(w_in, 16)
            sp.dma_start(w3s[:], sw3.rearrange("(c p) n -> p c n", p=P)).then_inc(w_in, 16)
            sp.dma_start(w2s[:], sw2.rearrange("(c p) n -> p c n", p=P)).then_inc(w_in, 16)
            for e in range(NE):
                sp.dma_start(w1e[:, e], ew1[e].rearrange("(c p) n -> p c n", p=P)).then_inc(w_in, 16)
                sp.dma_start(w2e[:, e], ew2[e].rearrange("(c p) n -> p c n", p=P)).then_inc(w_in, 16)

        @block.gpsimd
        def _(pool):
            nc.gpsimd.iota(iota[:], pattern=[[1, NE]], base=0, channel_multiplier=0,
                           allow_small_or_imprecise_dtypes=True).then_inc(io, 1)

        @block.tensor
        def _(pe):
            pe.sem_inc(tr_full, ONE)
            pe.wait_ge(w_in, 16 * (5 + 2 * NE))
            with pe.Fori(0, NB) as k:
                pe.wait_ge(dn_used, ONE + k * (DN + 3))
                for t in range(BT):
                    pe.wait_ge(row_full, k * BT + t + 1)
                    for c in range(DC):
                        o = (c * 2 + t % 2) * P
                        last = nc.tensor.transpose(dn[:, t // 2, o:o + P], xrow[:, t, c * P:(c + 1) * P],
                                                   core.ident[:])
                last.then_inc(tr_full, 1)
                pe.wait_ge(dn_used, ONE + k * (DN + 3) + 2)
                for t in range(BT):
                    for c in range(DC):
                        last = nc.tensor.matmul(dn[:, 2, t * NE:(t + 1) * NE], xt[:, c, t * P:(t + 1) * P],
                                                rw[:, c, :], start=(c == 0), stop=(c == DC - 1))
                last.then_inc(lg_full, 1)
                for u in range(NU):
                    if u < 2 * SC:
                        w, m = ((w1s, w3s)[u % 2], u // 2)
                        lhs = [w[:, c, m * P:(m + 1) * P] for c in range(DC)]
                    else:
                        e, m = (u - 2 * SC) // RC, (u - 2 * SC) % RC
                        lhs = [w1e[:, e, c, m * P:(m + 1) * P] for c in range(DC)]
                    pe.wait_ge(up_free[u % 4], ONE + k * UPS + u // 4)
                    for c in range(DC):
                        last = nc.tensor.matmul(up[:, u % 4, :], lhs[c], xt[:, c, :],
                                                start=(c == 0), stop=(c == DC - 1))
                    last.then_inc(up_full, 1)
                n = 0
                for t in range(BT):
                    if t == 0:
                        for i in range(4):
                            pe.wait_ge(up_free[i], ONE + (k + 1) * UPS)
                    for g in range(1 + NE // 2):
                        pe.wait_ge(dn_used, ONE + k * (DN + 3) + 3 + max(0, n - 3))
                        if g == 0:
                            for m in range(SC):
                                last = nc.tensor.matmul(dn[:, n % 4, 0:D], hs[:, m, t * P:(t + 1) * P],
                                                        w2s[:, m, :], start=(m == 0), stop=(m == SC - 1))
                        else:
                            for e in (2 * g - 2, 2 * g - 1):
                                for m in range(RC):
                                    o = (e % 2) * D
                                    last = nc.tensor.matmul(dn[:, n % 4, o:o + D],
                                                            he[:, e * RC + m, t * P:(t + 1) * P],
                                                            w2e[:, e, m, :], start=(m == 0), stop=(m == RC - 1))
                        last.then_inc(dn_full, 1)
                        n += 1

        @block.scalar
        def _(act):
            act.sem_inc(dn_used, ONE)
            act.sem_inc(up_free[0], ONE)
            act.sem_inc(up_free[2], ONE)
            with act.Fori(0, NB) as k:
                act.wait_ge(tr_full, ONE + k + 1)
                for n in range(BT // 2):
                    nc.scalar.activation(xt[:, :, n * 2 * P:(n + 1) * 2 * P],
                                         dn[:, n, :].rearrange("p (c t) -> p c t", c=DC), ACT.Copy).then_inc(dn_used, 1)
                act.wait_ge(lg_full, k + 1)
                nc.scalar.activation(score[:], dn[:, 2, 0:BT * NE].rearrange("p (t e) -> p t e", e=NE),
                                     ACT.Sigmoid).then_inc(dn_used, 1)
                for u in range(0, 2 * SC, 2):
                    act.wait_ge(up_full, k * NU + u + 1)
                    nc.scalar.activation(sil[:, u // 2, :], up[:, u % 4, :], ACT.Silu).then_inc(up_free[u % 4], 1)
                for u in range(2 * SC, NU):
                    act.wait_ge(up_full, k * NU + u + 1)
                    nc.scalar.activation(he[:, u - 2 * SC, :], up[:, u % 4, :], ACT.Gelu).then_inc(up_free[u % 4], 1)

        @block.vector
        def _(dve):
            dve.sem_inc(up_free[1], ONE)
            dve.sem_inc(up_free[3], ONE)
            dve.wait_ge(io, 1)
            dve.wait_ge(w_in, 16 * (5 + 2 * NE))
            with dve.Fori(0, NB) as k:
                for t in range(BT):
                    dve.wait_ge(tr_full, ONE + k)
                    nc.vector.tensor_scalar(xrow[:, t, :], core.x[:, bass.ds(k * BT + t, 1), :].rearrange("p a d -> p (a d)"),
                                            core.mean_var[:, bass.ds(k * BT + t, 1), 0], core.rstd[:, bass.ds(k * BT + t, 1)],
                                            ALU.subtract, ALU.mult).then_inc(row_full, 1)
                dve.wait_ge(dn_used, ONE + k * (DN + 3) + 3)
                rb_b = rb[:].rearrange("p (a e) -> p a e", a=1).to_broadcast([P, BT, NE])
                io_b = iota[:].rearrange("p (a e) -> p a e", a=1).to_broadcast([P, BT, NE])
                nc.vector.tensor_tensor(sel[:], score[:], rb_b, ALU.add)
                dve.drain()
                for t in range(BT):
                    nc.vector.max(best[:, t, :], sel[:, t, :])
                dve.drain()
                for t in range(BT):
                    nc.vector.max_index(best_at[:, t, :], best[:, t, :], sel[:, t, :])
                dve.drain()
                nc.vector.tensor_copy(best_f[:], best_at[:])
                dve.drain()
                nc.vector.tensor_tensor(hot[:], io_b, best_f[:, :, 0:1].to_broadcast([P, BT, NE]), ALU.is_equal)
                nc.vector.tensor_tensor(hot2[:], io_b, best_f[:, :, 1:2].to_broadcast([P, BT, NE]), ALU.is_equal)
                dve.drain()
                nc.vector.tensor_tensor(hot[:], hot[:], hot2[:], ALU.add)
                dve.drain()
                nc.vector.tensor_tensor(chosen[:], hot[:], score[:], ALU.mult)
                dve.drain()
                nc.vector.tensor_reduce(denom[:], chosen[:], AX.X, ALU.add)
                dve.drain()
                nc.vector.tensor_scalar(inv[:], denom[:], 1e-9, None, ALU.add)
                nc.vector.tensor_scalar(big[:], denom[:], 1e-9, None, ALU.is_gt)
                dve.drain()
                nc.vector.reciprocal(inv[:], inv[:])
                nc.vector.tensor_scalar(half[:], big[:], -0.5, 0.5, ALU.mult, ALU.add)
                dve.drain()
                nc.vector.tensor_tensor(inv[:], inv[:], big[:], ALU.mult)
                dve.drain()

                def over_experts(v):
                    return v[:].rearrange("p (t a) -> p t a", a=1).to_broadcast([P, BT, NE])

                nc.vector.tensor_tensor(chosen[:], chosen[:], over_experts(inv), ALU.mult)
                nc.vector.tensor_tensor(hot[:], hot[:], over_experts(half), ALU.mult)
                dve.drain()
                nc.vector.tensor_tensor(comb[:], chosen[:], hot[:], ALU.add)
                dve.drain()
                for m in range(SC):
                    dve.wait_ge(up_free[(2 * m) % 4], ONE + k * UPS + m // 2 + 1)
                    dve.wait_ge(up_full, k * NU + 2 * m + 2)
                    nc.vector.tensor_tensor(hs[:, m, :], sil[:, m, :], up[:, (2 * m + 1) % 4, :],
                                            ALU.mult).then_inc(up_free[(2 * m + 1) % 4], 1)
                n = 0
                for t in range(BT):
                    xv = core.x[:, bass.ds(k * BT + t, 1), :].rearrange("p a d -> p (a d)")
                    for g in range(1 + NE // 2):
                        if g:
                            dve.drain()
                        dve.wait_ge(dn_full, k * DN + n + 1)
                        if g == 0:
                            last = nc.vector.tensor_copy(acc[:, t, :], dn[:, n % 4, 0:D])
                        else:
                            for e in (2 * g - 2, 2 * g - 1):
                                o = (e % 2) * D
                                if e % 2:
                                    dve.drain()
                                last = nc.vector.scalar_tensor_tensor(out=acc[:, t, :], in0=dn[:, n % 4, o:o + D],
                                                                      scalar=comb[:, t, e:e + 1], in1=acc[:, t, :],
                                                                      op0=ALU.mult, op1=ALU.add)
                        last.then_inc(dn_used, 1)
                        n += 1
                    dve.drain()
                    nc.vector.tensor_tensor(xv, acc[:, t, :], xv, ALU.add)



def delta_memory(core, wkvq_dram):
    with Stage(core, "delta_kvq") as st:
        kvq = st.sb("kvq", [P, NT, 3, D])
        delta_projections(core, wkvq_dram, kvq)
        delta_recurrence(core, kvq)


NBK, BK = 32, 8


def delta_projections(core, wkvq_dram, kvq):
    nc = core.nc
    with Stage(core, "delta") as st:
        w = st.sb("w", [P, DC, 3 * D])
        xrow = st.sb("xrow", [P, 2, D])
        xt = st.sb("xt", [P, 2, DC, P])
        sq = st.sb("sq", [P, 2, D])
        norm = st.sb("norm", [P, NT * NBK])
        tr = st.ps("tr", [P, 2, 512])
        pj = st.ps("pj", [P, 2, 1024])
        w_in = st.sem("w_in")
        row_full, tr_full, xt_full = (st.sem(n) for n in ("row_full", "tr_full", "xt_full"))
        pj_full, pj_used, sq_full, sq_used = (st.sem(n) for n in ("pj_full", "pj_used", "sq_full", "sq_used"))
        ss_full, root_full = st.sem("ss_full"), st.sem("root_full")

        block = st.block()

        @block.sync
        def _(sp):
            sp.dma_start(w[:], wkvq_dram.rearrange("(c p) n -> p c n", p=P)).then_inc(w_in, 16)

        @block.tensor
        def _(pe):
            pe.sem_inc(tr_full, ONE)
            pe.wait_ge(w_in, 16)
            with pe.Fori(0, NT // 2) as i:
                for j in range(2):
                    pe.wait_ge(row_full, i * 2 + j + 1)
                    for c in range(DC):
                        last = nc.tensor.transpose(tr[:, j, c * P:(c + 1) * P], xrow[:, j, c * P:(c + 1) * P],
                                                   core.ident[:])
                    last.then_inc(tr_full, 1)
                for j in range(2):
                    pe.wait_ge(xt_full, i * 2 + j + 1)
                    pe.wait_ge(pj_used, ONE + i * 2 + j)
                    for lo, hi in ((0, 512), (512, 768)):
                        for c in range(DC):
                            last = nc.tensor.matmul(pj[:, j, lo:hi], xt[:, j, c, :], w[:, c, lo:hi],
                                                    start=(c == 0), stop=(c == DC - 1))
                    last.then_inc(pj_full, 1)

        @block.scalar
        def _(act):
            act.sem_inc(pj_used, ONE)
            with act.Fori(0, NT // 2) as i:
                for j in range(2):
                    act.wait_ge(tr_full, ONE + i * 2 + j + 1)
                    nc.scalar.activation(xt[:, j], tr[:, j, 0:DC * P].rearrange("p (c t) -> p c t", c=DC),
                                         ACT.Copy).then_inc(xt_full, 1)
                for j in range(2):
                    act.wait_ge(pj_full, i * 2 + j + 1)
                    act.wait_ge(sq_used, ONE + i * 2 + j)
                    nc.scalar.activation(sq[:, j, :], pj[:, j, 0:D], ACT.Square).then_inc(sq_full, 1)
                    nc.scalar.activation(kvq[:, bass.ds(i * 2 + j, 1)].rearrange("p a b d -> p (a b d)"), pj[:, j, 0:3 * D],
                                         ACT.Copy).then_inc(pj_used, 1)
            act.wait_ge(ss_full, 1)
            nc.scalar.activation(norm[:], norm[:], ACT.Sqrt).then_inc(root_full, 1)

        @block.vector
        def _(dve):
            dve.sem_inc(sq_used, ONE)
            with dve.Fori(0, NT // 2) as i:
                for j in range(2):
                    dve.wait_ge(tr_full, ONE + i * 2)
                    nc.vector.tensor_scalar(xrow[:, j, :], core.x[:, bass.ds(i * 2 + j, 1), :].rearrange("p a d -> p (a d)"),
                                            core.mean_var[:, bass.ds(i * 2 + j, 1), 0], core.rstd[:, bass.ds(i * 2 + j, 1)],
                                            ALU.subtract, ALU.mult).then_inc(row_full, 1)
                for j in range(2):
                    dve.wait_ge(sq_full, i * 2 + j + 1)
                    nc.vector.tensor_reduce(norm[:, bass.ds((i * 2 + j) * NBK, NBK)],
                                            sq[:, j, :].rearrange("p (n e) -> p n e", e=BK), AX.X,
                                            ALU.add).then_inc(sq_used, 1)
            dve.drain().then_inc(ss_full, 1)
            dve.wait_ge(root_full, 1)
            nc.vector.tensor_scalar(norm[:], norm[:], 1e-6, None, ALU.add)
            dve.drain()
            nc.vector.reciprocal(norm[:], norm[:])
            dve.drain()
            for t in range(NT):
                k = kvq[:, t, 0, :].rearrange("p (n e) -> p n e", e=BK)
                r = norm[:, t * NBK:(t + 1) * NBK].rearrange("p (n a) -> p n a", a=1).to_broadcast([P, NBK, BK])
                nc.vector.tensor_tensor(k, k, r, ALU.mult)


def delta_recurrence(core, kvq):
    nc = core.nc
    with Stage(core, "recur") as s2:
        state = s2.sb("state", [P, NBK, BK, BK])
        prod = s2.sb("prod", [P, NBK, BK, BK])
        ret = s2.sb("ret", [P, NBK, BK])
        pre_full, tanh_full = s2.sem("pre_full"), s2.sem("tanh_full")
        sq_done, silu_done = s2.sem("sq_done"), s2.sem("silu_done")
        block2 = s2.block()
        full = [P, NBK, BK, BK]

        @block2.scalar
        def _(act):
            with act.Fori(0, TB) as i:
                for t in range(B):
                    act.wait_ge(pre_full, i * B + t + 1)
                    nc.scalar.activation(state[:], prod[:], ACT.Tanh).then_inc(tanh_full, 1)
            act.wait_ge(sq_done, 1)
            for t in range(NT):
                nc.scalar.activation(kvq[:, t, 2, :], kvq[:, t, 1, :], ACT.Silu).then_inc(silu_done, 1)

        @block2.vector
        def _(dve):
            with dve.Fori(0, TB) as i:
                for t in range(B):
                    def part(which):
                        v = kvq[:, bass.ds(i + t * TB, 1), which, :]
                        return v.rearrange("p a (n e) -> p (a n) e", e=BK)

                    def by_j(which):
                        v = kvq[:, bass.ds(i + t * TB, 1), which, :]
                        return v.rearrange("p a (n o e) -> p (a n) o e", e=BK, o=1).to_broadcast(full)

                    v_i = part(1)
                    if t > 0:
                        nc.vector.tensor_tensor(prod[:], state[:], by_j(0), ALU.mult)
                        dve.drain()
                        nc.vector.tensor_reduce(ret[:], prod[:], AX.X, ALU.add)
                        dve.drain()
                        nc.vector.tensor_tensor(ret[:], v_i, ret[:], ALU.subtract)
                        dve.drain()
                        d_i = ret[:].rearrange("p n (e o) -> p n e o", o=1).to_broadcast(full)
                        nc.vector.tensor_tensor(prod[:], d_i, by_j(0), ALU.mult)
                        dve.drain()
                        nc.vector.tensor_tensor(prod[:], prod[:], state[:], ALU.add).then_inc(pre_full, 1)
                    else:
                        v_e = kvq[:, bass.ds(i + t * TB, 1), 1, :].rearrange("p a (n e o) -> p (a n) e o", e=BK, o=1)
                        nc.vector.tensor_tensor(prod[:], v_e.to_broadcast(full), by_j(0), ALU.mult).then_inc(pre_full, 1)
                    dve.wait_ge(tanh_full, i * B + t + 1)
                    nc.vector.tensor_tensor(prod[:], state[:], by_j(2), ALU.mult)
                    dve.drain()
                    nc.vector.tensor_reduce(v_i, prod[:], AX.X, ALU.add)
                    dve.drain()
            dve.drain().then_inc(sq_done, 1)
            for t in range(NT):
                dve.wait_ge(silu_done, t + 1)
                nc.vector.tensor_tensor(kvq[:, t, 0, :], kvq[:, t, 1, :], kvq[:, t, 2, :], ALU.mult)
            dve.drain()
            for t in range(NT):
                nc.vector.tensor_tensor(core.x[:, t, :], core.x[:, t, :], kvq[:, t, 0, :], ALU.add)




def project_qkv(core, name, wqkv_dram, qk_dram, v_dram, *, rows, bias=None, col_scale=None, fancy=None):
    nc = core.nc
    FANCY = fancy is not None
    with Stage(core, name) as st:
        wqkv = st.sb("wqkv", [P, DC, 3 * D])
        xrow = st.sb("xrow", [P, 4, D])
        PAD = 3 if FANCY else 0
        xt = st.sb("xt", [P, DC, PAD + S])
        qf = st.sb("qf", [P, 2, S])
        rest = st.sb("rest", [P, S])
        part = st.sb("part", [P, 2, 3, S], BF16)
        vt = st.sb("vt", [P, NH, TB, VH])
        if bias is not None:
            bqk = st.sb("bqk", [P, 2 * DC])
            bqk4 = st.sb("bqk4", [P, 2 * DC])
            bv = st.sb("bv", [1, D])
        if col_scale is not None:
            cs = st.sb("cs", [P, DC])
        if FANCY:
            conv = st.sb("conv", [P, DC, S])
            taps = st.sb("taps", [P, 3, 4])
            swap = st.sb("swap", [P, P])
            cos_t, sin_t = st.sb("cos", [P, S]), st.sb("sin", [P, S])
            gain = st.sb("gain", [P, DC, S])
            freq, phase = st.sb("freq", [P, DC]), st.sb("phase", [P, DC])
            theta = st.sb("theta", [P, 1])
            work = st.sb("work", [P, S])
            angle, turns = st.sb("angle", [P, S]), st.sb("turns", [P, S])
            hp = st.sb("hp", [P, 1])
        sc = st.ps("sc", [P, 2, 1024])
        tp = st.ps("tp", [P, 2, 512])

        w_in, row_full = st.sem("w_in"), st.sem("row_full")
        sc_full, sc_free = st.sem("sc_full"), st.sem("sc_free")
        tp_full, tp_free = st.sem("tp_full"), st.sem("tp_free")
        part_full = st.sem("part_full")
        part_out = [st.sem("part_out0"), st.sem("part_out1")]
        v_full, v_out, ones_set = st.sem("v_full"), st.sem("v_out"), st.sem("ones_set")
        qf_full = st.sem("qf_full")
        if FANCY:
            conv_full, gain_phase, gain_sin, pos_full = (
                st.sem(n) for n in ("conv_full", "gain_phase", "gain_sin", "pos_full"))
        block = st.block()

        SC_N = 8 if FANCY else 4
        TP_ROWS = TB // 2
        TP_N = 2 * TP_ROWS
        n_in = 1 + (2 if bias is not None else 0) + (col_scale is not None) + (9 if FANCY else 0)

        def part_slot_free(eng, b, n):
            eng.wait_ge(part_out[n % 2], ONE + b * 96 + n // 2 * 48)

        @block.sync
        def _(sp):
            sp.dma_start(wqkv[:], wqkv_dram.rearrange("(c p) n -> p c n", p=P)).then_inc(w_in, 16)
            if bias is not None:
                sp.dma_start(bqk[:], bias[0]).then_inc(w_in, 16)
                sp.dma_start(bv[:], bias[1]).then_inc(w_in, 16)
            if col_scale is not None:
                sp.dma_start(cs[:], col_scale).then_inc(w_in, 16)
            if FANCY:
                for i, kern in enumerate(fancy["taps"]):
                    sp.dma_start(taps[:, i, :], kern.partition_broadcast(P)).then_inc(w_in, 16)
                sp.dma_start(cos_t[:], fancy["cos"]).then_inc(w_in, 16)
                sp.dma_start(sin_t[:], fancy["sin"]).then_inc(w_in, 16)
                sp.dma_start(swap[:], fancy["swap"]).then_inc(w_in, 16)
                sp.dma_start(freq[:], fancy["gamma"]).then_inc(w_in, 16)
                sp.dma_start(phase[:], fancy["phase"]).then_inc(w_in, 16)
                sp.dma_start(theta[:], fancy["theta"].partition_broadcast(P)).then_inc(w_in, 16)
            for sem in part_out + [v_out]:
                sp.sem_inc(sem, ONE)
            with sp.Fori(0, B) as b:
                for n in range(4):
                    c, which = n // 2, n % 2
                    sp.wait_ge(part_full, ONE + 1 + b * 4 + n + 1)
                    for i in range(3):
                        sp.dma_start(qk_dram[which, i, bass.ds(b * D + c * P, P), :],
                                     part[:, n % 2, i, :]).then_inc(part_out[n % 2], 16)
                sp.wait_ge(v_full, b + 1)
                sp.dma_start(v_dram[bass.ds(b * NH, NH), :, :].rearrange("h p e -> p h e"),
                             vt[:].rearrange("p h t e -> p h (t e)")).then_inc(v_out, 16)
            for sem in part_out:
                sp.wait_ge(sem, ONE + B * 96)
            sp.wait_ge(v_out, ONE + B * 16)

        @block.tensor
        def _(pe):
            pe.sem_inc(tp_full, ONE)
            pe.wait_ge(w_in, 16 * n_in)
            with pe.Fori(0, B) as b:
                for t in range(TB):
                    n = t // 2
                    if t % 2 == 0:
                        pe.wait_ge(tp_free, ONE + b * TP_N + n)
                    pe.wait_ge(row_full, b * TB + t + 1)
                    for c in range(DC):
                        k0 = (c * 2 + t % 2) * P
                        last = nc.tensor.transpose(tp[:, n % 2, k0:k0 + P], xrow[:, t % 4, c * P:(c + 1) * P],
                                                   core.ident[:])
                    if t % 2:
                        last.then_inc(tp_full, 1)
                pe.wait_ge(tp_free, ONE + b * TP_N + TP_ROWS + 1)
                src = conv if FANCY else xt

                def values(t):
                    n = TP_ROWS + t // 2
                    if t % 2 == 0:
                        pe.wait_ge(tp_free, ONE + b * TP_N + n)
                    dst = tp[:, n % 2, (t % 2) * D:(t % 2 + 1) * D]
                    for c in range(DC):
                        last = nc.tensor.matmul(dst, src[:, c, t * P:(t + 1) * P], wqkv[:, c, 2 * D:3 * D],
                                                start=(c == 0), stop=(c == DC - 1 and bias is None))
                    if bias is not None:
                        last = nc.tensor.matmul(dst, core.ones[:], bv[:], start=False, stop=True)
                    if t % 2:
                        last.then_inc(tp_full, 1)

                n = 0
                for c in range(DC):
                    for which in range(2):
                        if FANCY:
                            pe.wait_ge(conv_full, b * 5 + c * 2 + which + 1)
                        pe.wait_ge(sc_free, ONE + b * SC_N + n)
                        for half in range(2):
                            for d in range(DC):
                                k0 = which * D + c * P
                                last = nc.tensor.matmul(sc[:, n % 2, half * 512:(half + 1) * 512],
                                                        wqkv[:, d, k0:k0 + P],
                                                        src[:, d, half * 512:(half + 1) * 512],
                                                        start=(d == 0), stop=(d == DC - 1))
                        last.then_inc(sc_full, 1)
                        n += 1
                        if FANCY:
                            pe.wait_ge(sc_free, ONE + b * SC_N + n + 1)
                            for half in range(2):
                                last = nc.tensor.matmul(sc[:, n % 2, half * 512:(half + 1) * 512], swap[:],
                                                        qf[:, 0, half * 512:(half + 1) * 512], start=True, stop=True)
                            last.then_inc(sc_full, 1)
                            n += 1
                        else:
                            for t in range(2 * (2 * c + which), 2 * (2 * c + which) + 2):
                                values(t)
                if FANCY:
                    pe.wait_ge(conv_full, (b + 1) * 5)
                    for t in range(TB):
                        values(t)

        @block.scalar
        def _(act):
            act.sem_inc(tp_free, ONE + 1)
            if not FANCY:
                act.sem_inc(sc_free, ONE + 1)
            act.wait_ge(w_in, 16 * n_in)
            act.wait_ge(ones_set, 1)
            if bias is not None:
                nc.scalar.activation(bqk4[:], bqk[:], ACT.Copy, scale=0.25)
                act.drain()
            if FANCY:
                for n in range(DC + 1):
                    act.wait_ge(gain_phase, n + 1)
                    nc.scalar.activation(work[:], rest[:], ACT.Sin).then_inc(gain_sin, 1)
            with act.Fori(0, B) as b:
                for n in range(TP_ROWS):
                    act.wait_ge(tp_full, ONE + b * TP_N + n + 1)
                    src = tp[:, n % 2, :].rearrange("p (c t) -> p c t", c=DC)
                    if col_scale is None:
                        last = nc.scalar.activation(xt[:, :, PAD + n * 2 * P:PAD + (n + 1) * 2 * P], src, ACT.Copy)
                    else:
                        for c in range(DC):
                            last = nc.scalar.activation(xt[:, c, n * 2 * P:(n + 1) * 2 * P], src[:, c, :], ACT.Identity,
                                                        scale=cs[:, c:c + 1])
                    last.then_inc(tp_free, 1)

                def copy_values(n):
                    act.wait_ge(tp_full, ONE + b * TP_N + n + 1)
                    t = 2 * (n - TP_ROWS)
                    if t == 0:
                        act.wait_ge(v_out, ONE + b * 16)
                    nc.scalar.activation(vt[:, :, t:t + 2, 0:HD],
                                         tp[:, n % 2, :].rearrange("p (t h d) -> p h t d", t=2, h=NH),
                                         ACT.Copy).then_inc(tp_free, 1)

                for n in range(4):
                    c, which = n // 2, n % 2
                    if not FANCY:
                        act.wait_ge(sc_full, b * SC_N + n + 1)
                        act.wait_ge(part_full, ONE + b * 4 + n)
                        scale = 0.25 if which == 0 else 1.0
                        if bias is None:
                            last = nc.scalar.activation(qf[:, n % 2, :], sc[:, n % 2, :], ACT.Copy, scale=scale)
                        else:
                            bcol = (bqk4 if which == 0 else bqk)[:, which * DC + c:which * DC + c + 1]
                            last = nc.scalar.activation(qf[:, n % 2, :], sc[:, n % 2, :], ACT.Identity, bias=bcol,
                                                        scale=scale)
                        last.then_inc(sc_free, 1)
                    copy_values(TP_ROWS + n)
                act.drain().then_inc(v_full, 1)

        @block.gpsimd
        def _(pool):
            nc.gpsimd.memset(vt[:, :, :, HD:VH], 1.0).then_inc(ones_set, 1)
            if FANCY:
                nc.gpsimd.iota(qf[:, 0, :], pattern=[[1, S]], base=0, channel_multiplier=0,
                               allow_small_or_imprecise_dtypes=True).then_inc(pos_full, 1)

        @block.vector
        def _(dve):
            if FANCY:
                dve.sem_inc(sc_free, ONE + 1)
            TWO_PI = 2 * pi
            if FANCY:
                dve.wait_ge(w_in, 16 * n_in)
                nc.vector.memset(xt[:, :, 0:PAD], 0.0)
                MAGIC = 12582912.0
                TWO_PI_MID = 4058 * 2.0 ** -21
                PI_PARTS = (6.28125, TWO_PI_MID, TWO_PI - 6.28125 - TWO_PI_MID)
                dve.wait_ge(pos_full, 1)
                for n in range(DC + 1):
                    gain_n = gain[:, n, :] if n < DC else None
                    nc.vector.tensor_scalar(hp[:], freq[:, n:n + 1] if n < DC else theta[:], TWO_PI, None, ALU.mult)
                    dve.drain()
                    nc.vector.tensor_scalar(rest[:], qf[:, 0, :], hp[:], None, ALU.mult)
                    dve.drain()
                    nc.vector.tensor_scalar(angle[:], rest[:], 0.01,
                                            phase[:, n:n + 1] if n < DC else 0.0, ALU.mult, ALU.add)
                    dve.drain()
                    nc.vector.tensor_scalar(turns[:], angle[:], 1.0 / TWO_PI, 0.25, ALU.mult, ALU.add)
                    dve.drain()
                    nc.vector.tensor_scalar(turns[:], turns[:], MAGIC, None, ALU.add)
                    dve.drain()
                    nc.vector.tensor_scalar(turns[:], turns[:], MAGIC, None, ALU.subtract)
                    dve.drain()
                    for pp in PI_PARTS:
                        nc.vector.scalar_tensor_tensor(out=angle[:], in0=turns[:], scalar=-pp, in1=angle[:],
                                                       op0=ALU.mult, op1=ALU.add)
                        dve.drain()
                    nc.vector.tensor_scalar(rest[:], angle[:], pi / 2, 3.1415925, ALU.add, ALU.min)
                    dve.drain()
                    nc.vector.tensor_scalar(rest[:], rest[:], -3.1415925, None, ALU.max).then_inc(gain_phase, 1)
                    dve.wait_ge(gain_sin, n + 1)
                    if n < DC:
                        nc.vector.tensor_scalar(gain_n, work[:], 0.3, 0.5, ALU.mult, ALU.add)
                        dve.drain()
                    else:
                        for c in range(DC):
                            nc.vector.scalar_tensor_tensor(out=gain[:, c, :], in0=work[:], scalar=0.2,
                                                           in1=gain[:, c, :], op0=ALU.mult, op1=ALU.add)
                        dve.drain()

            def split(b, n, src):
                part_slot_free(dve, b, n)
                p0, p1, p2 = (part[:, n % 2, i, :] for i in range(3))
                nc.vector.tensor_copy(p0, src)
                dve.drain()
                nc.vector.tensor_tensor(rest[:], src, p0, ALU.subtract)
                dve.drain()
                nc.vector.tensor_copy(p1, rest[:])
                dve.drain()
                nc.vector.tensor_tensor(p2, rest[:], p1, ALU.subtract)
                dve.drain().then_inc(part_full, 1)

            def convolve(b, i):
                for j in range(4):
                    if j == 0:
                        nc.vector.tensor_scalar(conv[:], xt[:, :, 0:S], taps[:, i, 0:1], None, ALU.mult)
                    else:
                        for c in range(DC):
                            nc.vector.scalar_tensor_tensor(out=conv[:, c, :], in0=xt[:, c, j:j + S],
                                                           scalar=taps[:, i, j:j + 1], in1=conv[:, c, :],
                                                           op0=ALU.mult, op1=ALU.add)
                    dve.drain()

            dve.sem_inc(part_full, ONE + 1)
            with dve.Fori(0, B) as b:
                for t in range(TB):
                    if t >= 2:
                        dve.wait_ge(tp_full, ONE + b * TP_N + t // 2 - 1)
                    rows(xrow[:, t % 4, :], b * TB + t).then_inc(row_full, 1)
                if not FANCY:
                    for n in range(4):
                        dve.wait_ge(sc_free, ONE + b * SC_N + n + 2)
                        split(b, n, qf[:, n % 2, :])
                else:
                    dve.wait_ge(tp_free, ONE + b * TP_N + TP_ROWS + 1)
                    for n in range(4):
                        c, which = n // 2, n % 2
                        convolve(b, which)
                        dve.drain().then_inc(conv_full, 1)
                        f = 2 * n
                        dve.wait_ge(sc_full, b * SC_N + f + 1)
                        nc.vector.scalar_tensor_tensor(out=qf[:, 0, :], in0=sc[:, f % 2, :],
                                                       scalar=(0.25 if which == 0 else 1.0),
                                                       in1=gain[:, c, :], op0=ALU.mult, op1=ALU.mult
                                                       ).then_inc(sc_free, 1)
                        dve.drain()
                        nc.vector.tensor_tensor(work[:], qf[:, 0, :], cos_t[:], ALU.mult)
                        dve.wait_ge(sc_full, b * SC_N + f + 2)
                        nc.vector.tensor_tensor(rest[:], sc[:, (f + 1) % 2, :], sin_t[:], ALU.mult)
                        dve.drain().then_inc(sc_free, 1)
                        nc.vector.tensor_tensor(qf[:, 1, :], work[:], rest[:], ALU.add)
                        dve.drain()
                        split(b, n, qf[:, 1, :])
                    convolve(b, 2)
                    dve.drain().then_inc(conv_full, 1)



HEADS = B * NH


def slots(eng, lead, unroll, total, emit):
    n = (HEADS - lead) // unroll
    for s in range(lead):
        emit(s, lambda f, s=s: f(s))
    with eng.Fori(0, n) as i:
        for s in range(lead, lead + unroll):
            emit(s, lambda f, s=s: i * (f(s + unroll) - f(s)) + f(s))
    for s in range(lead + n * unroll, total):
        emit(s, lambda f, s=s: f(s))


def live(h):
    return 0 <= h < HEADS


def load_pair(sp, qk_dram, which, dst, at_pair, sem):
    for j, i in enumerate((Q_PART, K_PART)[which]):
        sp.dma_start(dst[j * HD:(j + 1) * HD],
                     qk_dram[which, i, bass.ds(at_pair * 2 * HD, 2 * HD), :].rearrange("(h r) t -> r h t", r=HD)
                     ).then_inc(sem, 16)


def store_pair(sp, o_dram, o, at_pair, sem):
    out_dram, sum_dram = o_dram
    sp.dma_start(sum_dram[bass.ds(at_pair * 2, 2), :].rearrange("(a h) t -> a h t", a=1), o[HD:VH]).then_inc(sem, 16)
    for h in range(2):
        sp.dma_start(out_dram[bass.ds(at_pair * 2 * HD + h * HD, HD), :], o[0:HD, h, :]).then_inc(sem, 16)


def softmax_heads(core, name, qk_dram, v_dram, o_dram, *, causal):
    nc = core.nc
    LEAD, UNROLL, PAIRS = 2, 6, 3
    TOTAL = HEADS + LEAD
    MROW = QK_ROWS
    with Stage(core, name) as st:
        qs = st.sb("qs", [QK_ROWS + 3, 2 * PAIRS, S], BF16)
        ks = st.sb("ks", [QK_ROWS + 3, 2 * PAIRS, S], BF16)
        v = st.sb("v", [P, PAIRS, 2, TB * VH])
        pt = st.sb("pt", [P, 4, 512])
        o = st.sb("o", [VH, 2 * PAIRS, S])
        nmax = st.sb("nmax", [P, 2, TB])
        mrest = st.sb("mrest", [P, TB])
        mpart = st.sb("mpart", [P, 2, TB, P], BF16)
        sc = st.ps("sc", [P, 2, S])
        sct = st.ps("sct", [P, 2, 512])
        ov = st.ps("ov", [VH, 2, 512])

        qk_in = [st.sem(f"qk_in{i}") for i in range(PAIRS)]
        full, free = [st.sem("full0"), st.sem("full1")], [st.sem("free0"), st.sem("free1")]
        mpart_full, mrow_full = st.sem("mpart_full"), st.sem("mrow_full")
        sct_full, pt_full, pt_used = st.sem("sct_full"), st.sem("pt_full"), st.sem("pt_used")
        ov_free = st.sem("ov_free")
        o_out = [st.sem(f"o_out{i}") for i in range(PAIRS)]
        const = st.sem("const")
        block = st.block()

        MID = 4
        fills = []
        for s in range(TOTAL):
            for t in range(TB):
                if live(s):
                    fills.append(("max", s, t))
                if t == MID - 1 and live(s - 1):
                    fills.append(("row", s - 1))
        place = {f: n for n, f in enumerate(fills)}

        def before(key):
            return place[key] // 2

        halves = [0, 1] if causal else [1, 0]
        chunks = []
        for half in halves:
            lo, hi = 4 * half, 4 * half + 4
            for kb in (range(0, hi) if causal else range(TB - 1, lo - 1, -1)):
                q0, q1 = (max(kb, lo), hi) if causal else (lo, min(kb + 1, hi))
                chunks.append((kb, q0, q1 - q0))
        HALF_AT = 4
        assert chunks[0][2] == chunks[HALF_AT][2] == 4
        NCH = len(chunks)
        tile_of = [round((j + 1) * TB / (NCH + 1)) for j in range(NCH)]
        ROW_AT = sum(t < MID for t in tile_of)

        @block.sync
        def _(sp):
            for sem in o_out:
                sp.sem_inc(sem, ONE)

            def emit(p, at):
                slot = p % PAIRS
                if p >= PAIRS:
                    sp.wait_ge(ov_free, at(lambda p: ONE + 4 * (p - PAIRS) + 4))
                    store_pair(sp, o_dram, o[:, 2 * slot:2 * slot + 2, :], at(lambda p: p - PAIRS), o_out[slot])
                if p < HEADS // 2:
                    load_pair(sp, qk_dram, 0, qs[:, 2 * slot:2 * slot + 2, :], at(lambda p: p), qk_in[slot])
                    load_pair(sp, qk_dram, 1, ks[:, 2 * slot:2 * slot + 2, :], at(lambda p: p), qk_in[slot])
                    sp.dma_start(v[:, slot], v_dram[bass.ds(at(lambda p: p) * 2, 2), :, :].rearrange("h p e -> p h e")
                                 ).then_inc(qk_in[slot], 16)

            pairs(sp, PAIRS, PAIRS, emit)
            for slot in range(PAIRS):
                sp.wait_ge(o_out[slot], ONE + 48 * len(range(slot, HEADS // 2, PAIRS)))

        @block.gpsimd
        def _(pool):
            nc.gpsimd.memset(mpart[:], 0.0).then_inc(const, 1)
            pool.drain()
            nc.gpsimd.memset(ks[MROW:MROW + 3, :, :], 1.0).then_inc(const, 1)

        @block.tensor
        def _(pe):
            pe.sem_inc(pt_used, ONE + 3)
            pe.wait_ge(const, 2)

            def emit(s, at):
                def maxima(t):
                    n = place["max", s, t]
                    pe.wait_ge(free[n % 2], at(lambda s: ONE + before(("max", s, t))))
                    k0, k1 = (0, t + 1) if causal else (t, TB)
                    w, diag = (k1 - k0) * P, (t - k0) * P
                    for lo in range(0, w, 512):
                        hi = min(w, lo + 512)
                        has = lo <= diag < hi
                        last = nc.tensor.matmul(sc[:, n % 2, lo:hi], qs[0:QK_ROWS, s % 6, t * P:(t + 1) * P],
                                                ks[0:QK_ROWS, s % 6, k0 * P + lo:k0 * P + hi], start=True, stop=not has)
                        if has:
                            last = nc.tensor.matmul(sc[:, n % 2, diag:diag + P], core.ident_bf[:],
                                                    (core.above if causal else core.below)[:], start=False, stop=True)
                    last.then_inc(full[n % 2], 1)

                def maximum_row():
                    n = place["row", s - 1]
                    pe.wait_ge(free[n % 2], at(lambda s: ONE + before(("row", s - 1))))
                    pe.wait_ge(mpart_full, at(lambda s: s))
                    for t in range(TB):
                        last = nc.tensor.matmul(sc[:, n % 2, t * P:(t + 1) * P], mpart[:, (s - 1) % 2, t, :],
                                                core.ident_bf[:], start=True, stop=True)
                    last.then_inc(full[n % 2], 1)

                def transposed(j):
                    kb, q, nb = chunks[j]
                    h = (s - 2) % 6
                    if j >= 2:
                        pe.wait_ge(pt_full, at(lambda s: (s - 2) * NCH + j - 1))
                    has = q <= kb < q + nb
                    last = nc.tensor.matmul(sct[:, j % 2, 0:nb * P], ks[:, h, kb * P:(kb + 1) * P],
                                            qs[:, h, q * P:(q + nb) * P], start=True, stop=not has)
                    if has:
                        d = (kb - q) * P
                        last = nc.tensor.matmul(sct[:, j % 2, d:d + P], core.ident_bf[:],
                                                (core.below if causal else core.above)[:], start=False, stop=True)
                    last.then_inc(sct_full, 1)

                def values(j):
                    kb, q, nb = chunks[j]
                    h, half = s - 2, chunks[j][1] // 4
                    first = j in (0, HALF_AT)
                    if first:
                        pe.wait_ge(ov_free, at(lambda s: ONE + 2 * (s - 2) - (j == 0)) if s > 2 else ONE)
                    pe.wait_ge(pt_full, at(lambda s: (s - 2) * NCH + j + 1))
                    last = nc.tensor.matmul(ov[:, half, (q % 4) * P:(q % 4 + nb) * P],
                                            v[:, h // 2 % PAIRS, h % 2, kb * VH:(kb + 1) * VH], pt[:, j % 4, 0:nb * P],
                                            start=first, stop=j in (HALF_AT - 1, NCH - 1))
                    last.then_inc(pt_used, 1)

                if live(s) and s % 2 == 0:
                    pe.wait_ge(qk_in[s // 2 % PAIRS], at(lambda s: (s // 2 // PAIRS + 1) * 13 * 16))
                if live(s - 2):
                    pe.wait_ge(mrow_full, at(lambda s: s - 1))
                for t in range(TB + 1):
                    if t < TB and live(s):
                        maxima(t)
                    if t == MID - 1 and live(s - 1):
                        maximum_row()
                    if live(s - 2):
                        for j in (j for j in range(NCH) if tile_of[j] == t):
                            transposed(j)
                            if j >= 2:
                                values(j - 2)
                if live(s - 2):
                    values(NCH - 2)
                    values(NCH - 1)

            slots(pe, LEAD, UNROLL, TOTAL, emit)

        @block.scalar
        def _(act):
            def emit(s, at):
                def half_out(which, h, head):
                    half = halves[which]
                    done = (HALF_AT, NCH)[which]
                    act.wait_ge(pt_used, at(lambda s: ONE + 3 + head(s) * NCH + done))
                    if which == 0:
                        act.wait_ge(o_out[h // 2 % PAIRS], at(lambda s: ONE + head(s) // 2 // PAIRS * 48))
                    nc.scalar.activation(o[:, h % 6, half * 512:(half + 1) * 512], ov[:, half, :],
                                         ACT.Copy).then_inc(ov_free, 1)

                for j in range(NCH):
                    if j == ROW_AT and live(s - 1):
                        n = place["row", s - 1]
                        act.wait_ge(full[n % 2], at(lambda s: before(("row", s - 1)) + 1))
                        nc.scalar.activation(qs[MROW:MROW + 3, (s - 1) % 6, :], sc[MROW:MROW + 3, n % 2, :],
                                             ACT.Copy).then_inc(free[n % 2], 1)
                        act.drain().then_inc(mrow_full, 1)
                    if j == 2 and live(s - 3):
                        half_out(1, s - 3, lambda s: s - 3)
                    if j == HALF_AT + 3 and live(s - 2):
                        half_out(0, s - 2, lambda s: s - 2)
                    if live(s - 2):
                        act.wait_ge(sct_full, at(lambda s: (s - 2) * NCH + j + 1))
                        act.wait_ge(pt_used, at(lambda s: ONE + (s - 2) * NCH + j))
                        nb = chunks[j][2]
                        nc.scalar.activation(pt[:, j % 4, 0:nb * P], sct[:, j % 2, 0:nb * P], ACT.Exp).then_inc(pt_full, 1)

            act.sem_inc(ov_free, ONE)
            slots(act, 3, UNROLL, HEADS + 3, emit)

        @block.vector
        def _(dve):
            dve.sem_inc(free[0], ONE)
            dve.sem_inc(free[1], ONE)
            dve.wait_ge(const, 2)

            def emit(s, at):
                for t in range(TB):
                    if live(s):
                        n = place["max", s, t]
                        k0, k1 = (0, t + 1) if causal else (t, TB)
                        dve.wait_ge(full[n % 2], at(lambda s: before(("max", s, t)) + 1))
                        nc.vector.tensor_reduce(nmax[:, s % 2, t:t + 1], sc[:, n % 2, 0:(k1 - k0) * P], AX.X, ALU.max,
                                                negate=True).then_inc(free[n % 2], 1)
                if live(s):
                    cols = [mpart[:, s % 2, :, MROW + i] for i in range(3)]
                    dve.drain()
                    nc.vector.tensor_copy(cols[0], nmax[:, s % 2, :])
                    dve.drain()
                    nc.vector.tensor_tensor(mrest[:], nmax[:, s % 2, :], cols[0], ALU.subtract)
                    dve.drain()
                    nc.vector.tensor_copy(cols[1], mrest[:])
                    dve.drain()
                    nc.vector.tensor_tensor(cols[2], mrest[:], cols[1], ALU.subtract).then_inc(mpart_full, 1)

            slots(dve, LEAD, UNROLL, TOTAL, emit)


def pairs(eng, lead, unroll, emit):
    n = (HEADS // 2 - lead) // unroll
    for p in range(lead):
        emit(p, lambda f, p=p: f(p))
    with eng.Fori(0, n) as i:
        for p in range(lead, lead + unroll):
            emit(p, lambda f, p=p: i * (f(p + unroll) - f(p)) + f(p))
    for p in range(lead + n * unroll, HEADS // 2 + lead):
        emit(p, lambda f, p=p: f(p))


def project_out(core, name, wout_dram, o_dram, *, target, out_bias=None):
    nc = core.nc
    out_dram, sum_dram = o_dram
    with Stage(core, name) as st:
        wout = st.sb("wout", [P, DC, D])
        ot = st.sb("ot", [P, 2, DC, S])
        inverse = st.sb("inverse", [P, 2, DC, S])
        half_sums = st.sb("half_sums", [P, S // 2])
        if out_bias is not None:
            bo = st.sb("bo", [1, D])
        y = st.ps("y", [P, 4, 512])
        w_in = st.sem("w_in")
        o_in = [st.sem("o_in0"), st.sem("o_in1")]
        ot_full, y_full, y_used = st.sem("ot_full"), st.sem("y_full"), st.sem("y_used")
        sums_in, inverse_full, inverse_out = st.sem("sums_in"), st.sem("inverse_full"), st.sem("inverse_out")
        block = st.block()

        @block.sync
        def _(sp):
            by_half = sum_dram.rearrange("h (a t) -> (h a) t", a=2)
            sp.dma_start(half_sums[:], by_half).then_inc(sums_in, 16)
            sp.dma_start(wout[:], wout_dram.rearrange("(c p) n -> p c n", p=P)).then_inc(w_in, 16)
            if out_bias is not None:
                sp.dma_start(bo[:], out_bias.rearrange("(a n) -> a n", a=1)).then_inc(w_in, 16)
            sp.wait_ge(inverse_full, 1)
            sp.dma_start(by_half, half_sums[:]).then_inc(inverse_out, 16)
            sp.wait_ge(inverse_out, 16)
            for b in range(B):
                if b >= 2:
                    sp.wait_ge(y_full, (b - 1) * TB // 2)
                sp.dma_start(ot[:, b % 2], out_dram[b * D:(b + 1) * D, :].rearrange("(c p) t -> p c t", p=P)
                             ).then_inc(o_in[b % 2], 16)
                for c in range(DC):
                    for h in range(HC):
                        sp.dma_start(inverse[h * HD:(h + 1) * HD, b % 2, c, :],
                                     sum_dram[b * NH + c * HC + h, :].partition_broadcast(HD)).then_inc(o_in[b % 2], 16)

        @block.vector
        def _(dve):
            def normalise(b):
                dve.wait_ge(o_in[b % 2], (b // 2 + 1) * 16 * (1 + NH))
                for c in range(DC):
                    nc.vector.tensor_tensor(ot[:, b % 2, c, :], ot[:, b % 2, c, :], inverse[:, b % 2, c, :], ALU.mult)
                dve.drain().then_inc(ot_full, 1)

            dve.wait_ge(sums_in, 16)
            nc.vector.reciprocal(half_sums[:], half_sums[:]).then_inc(inverse_full, 1)
            normalise(0)
            for b in range(B):
                if b + 1 < B:
                    normalise(b + 1)
                for i in range(b * TB // 2, (b + 1) * TB // 2):
                    dve.wait_ge(y_full, i + 1)
                    tv = target[:, 2 * i:2 * i + 2, :]
                    nc.vector.tensor_tensor(tv, y[:, i % 4, :].rearrange("p (t d) -> p t d", t=2), tv,
                                            ALU.add).then_inc(y_used, 1)

        @block.tensor
        def _(pe):
            pe.wait_ge(w_in, 16 * (1 + (out_bias is not None)))
            for b in range(B):
                pe.wait_ge(ot_full, b + 1)
                for k in range(TB // 2):
                    i = b * TB // 2 + k
                    if i >= 4:
                        pe.wait_ge(y_used, i - 3)
                    for t in range(2):
                        dst = y[:, i % 4, t * D:(t + 1) * D]
                        for c in range(DC):
                            last = nc.tensor.matmul(dst, ot[:, b % 2, c, (2 * k + t) * P:(2 * k + t + 1) * P], wout[:, c, :],
                                                    start=(c == 0), stop=(c == DC - 1 and out_bias is None))
                        if out_bias is not None:
                            last = nc.tensor.matmul(dst, core.ones[:], bo[:], start=False, stop=True)
                    last.then_inc(y_full, 1)



LO, HI = TOPK - 8, TOPK
AIM = (LO + HI) // 2
ROUNDS = 4
SPAN = 64.0
BUSY = TB - 1


def sampled(t):
    return 0, t * P, max(1, t // 2)


def topk_heads(core, name, qk_dram, v_dram, o_dram, tables):
    nc = core.nc
    LEAD, UNROLL, PAIRS = 4, 4, 2
    TOTAL = HEADS + LEAD
    OFF = [P * t * (t + 1) // 2 for t in range(TB + 1)]
    order = list(range(1, TB)) + [0]
    with Stage(core, name) as st:
        qs = st.sb("qs", [QK_ROWS, 2 * PAIRS, S], BF16)
        ks = st.sb("ks", [QK_ROWS, 2 * PAIRS, S], BF16)
        v = st.sb("v", [P, PAIRS, 2, TB * VH])
        scores = st.sb("scores", [P, 4, OFF[TB]])
        e = st.sb("e", [P, OFF[TB]])
        pt = st.sb("pt", [P, 4, 512])
        o = st.sb("o", [VH, 2 * PAIRS, S])
        rest = st.sb("rest", [P, 2, S])
        rest0 = st.sb("rest0", [P, P])
        top8 = st.sb("top8", [P, 8])
        top0 = st.sb("top0", [P, 2, 8])
        largest = st.sb("largest", [P, 4, TB])
        nmax = st.sb("nmax", [P, 4, TB])
        kth = st.sb("kth", [P, TB])
        minus_one = st.sb("minus_one", [P, TB])
        tab = st.sb("tab", [P, 4, BUSY])
        minus_half, half = st.sb("minus_half", [P, BUSY]), st.sb("half", [P, BUSY])
        above = st.sb("above", [P, OFF[TB] - P], BF16)
        signs = st.sb("signs", [P, OFF[TB] - P], BF16)
        stats = st.sb("stats", [P, 4, BUSY, 6])
        at_now = st.sb("at_now", [P, 4, 2, BUSY])
        bracket = st.sb("bracket", [P, 4, 2, 2, BUSY])
        reach = st.sb("reach", [P, 4, 2, 2, BUSY])
        signed = st.sb("signed", [P, 4, BUSY])
        count = st.sb("count", [P, 4, BUSY])
        below = st.sb("below", [P, 4, BUSY, 9])
        rank = st.sb("rank", [P, 9])
        picked = st.sb("picked", [P, BUSY, 9])
        side = st.sb("side", [P, 2, 1, BUSY])
        diff = st.sb("diff", [P, 2, 2, BUSY])
        gap = st.sb("gap", [P, 2, BUSY])
        step = st.sb("step", [P, 2, BUSY])
        far = st.sb("far", [P, BUSY])
        bad = st.sb("bad", [P, TB])
        bad_head = st.sb("bad_head", [1, TB], mybir.dt.int32)
        ones_col = st.sb("ones_col", [P, 1])
        sc = st.ps("sc", [P, 2, S])
        tp = st.ps("tp", [P, 2, 512])
        ov = st.ps("ov", [VH, 2, 512])

        qk_in = [st.sem(f"qk_in{i}") for i in range(PAIRS)]
        v_in = [st.sem(f"v_in{i}") for i in range(PAIRS)]
        tab_in, ones_set = st.sem("tab_in"), st.sem("ones_set")
        sc_full, sc_free = st.sem("sc_full"), st.sem("sc_free")
        head_full, nmax_full = st.sem("head_full"), st.sem("nmax_full")
        guessed = [st.sem(f"guessed{r}") for r in range(ROUNDS + 1)]
        counted = [st.sem(f"counted{r}") for r in range(ROUNDS)]
        bad_full = st.sem("bad_full")
        e_full, e_cut = st.sem("e_full"), st.sem("e_cut")
        tp_full, tp_free, pt_used, ov_free = (st.sem(n) for n in ("tp_full", "tp_free", "pt_used", "ov_free"))
        o_out = [st.sem(f"o_out{i}") for i in range(PAIRS)]
        block = st.block()

        fills = []
        for s in range(HEADS + 3):
            fills += [("tile", s, t) for t in range(TB) if live(s)] + [("bad", s - 3)] * live(s - 3)
        place = {f: n for n, f in enumerate(fills)}

        chunks = [(t, k, min(4, t + 1 - k)) for t in order for k in range(0, t + 1, 4)]
        NCH = len(chunks)
        chunks_of = [[j for j, c in enumerate(chunks) if c[0] == t] for t in order]
        done_at = {1: chunks_of[TB - 2][-1], 0: chunks_of[TB - 1][-1]}

        @block.sync
        def _(sp):
            sp.dma_start(tab[:], tables["quantiles"].rearrange("a p t -> p a t")).then_inc(tab_in, 16)
            sp.dma_start(rank[:], tables["ranks"].partition_broadcast(P)).then_inc(tab_in, 16)
            for sem in o_out:
                sp.sem_inc(sem, ONE)

            def emit(p, at):
                slot = p % PAIRS
                if p < HEADS // 2:
                    if p >= PAIRS:
                        sp.wait_ge(sc_full, at(lambda p: place["tile", 2 * (p - PAIRS) + 1, TB - 1] + 1))
                    load_pair(sp, qk_dram, 0, qs[:, 2 * slot:2 * slot + 2, :], at(lambda p: p), qk_in[slot])
                    load_pair(sp, qk_dram, 1, ks[:, 2 * slot:2 * slot + 2, :], at(lambda p: p), qk_in[slot])
                if p >= PAIRS + 1:
                    sp.wait_ge(ov_free, at(lambda p: ONE + 4 * (p - PAIRS - 1) + 4))
                    old = (p - PAIRS - 1) % PAIRS
                    store_pair(sp, o_dram, o[:, 2 * old:2 * old + 2, :], at(lambda p: p - PAIRS - 1), o_out[old])
                if 1 <= p <= HEADS // 2:
                    sp.dma_start(v[:, (p - 1) % PAIRS],
                                 v_dram[bass.ds(at(lambda p: p - 1) * 2, 2), :, :].rearrange("h p e -> p h e")
                                 ).then_inc(v_in[(p - 1) % PAIRS], 16)

            pairs(sp, PAIRS + 1, PAIRS, emit)
            for slot in range(PAIRS):
                sp.wait_ge(o_out[slot], ONE + 48 * (HEADS // 2 // PAIRS))

        @block.tensor
        def _(pe):
            pe.sem_inc(pt_used, ONE + 3)
            pe.sem_inc(tp_full, ONE)
            pe.wait_ge(ones_set, 1)

            def emit(s, at):
                h = s - 4

                def score_tile(t):
                    if t == 0 and s % 2 == 0:
                        pe.wait_ge(qk_in[s // 2 % PAIRS], at(lambda s: (s // 2 // PAIRS + 1) * 12 * 16))
                    n = place["tile", s, t]
                    pe.wait_ge(sc_free, at(lambda s: ONE + place["tile", s, t]))
                    w, diag = (t + 1) * P, t * P
                    for lo in range(0, w, 512):
                        hi = min(w, lo + 512)
                        has = lo <= diag < hi
                        last = nc.tensor.matmul(sc[:, n % 2, lo:hi], qs[:, s % 4, t * P:(t + 1) * P],
                                                ks[:, s % 4, lo:hi], start=True, stop=not has)
                        if has:
                            last = nc.tensor.matmul(sc[:, n % 2, diag:diag + P], core.ident_bf[:], core.above[:],
                                                    start=False, stop=True)
                    last.then_inc(sc_full, 1)

                def transposes(i):
                    pe.wait_ge(e_cut, at(lambda s: (s - 4) * TB + i + 1))
                    for j in chunks_of[i]:
                        t, k0, nb = chunks[j]
                        pe.wait_ge(tp_free, at(lambda s: ONE + (s - 4) * NCH + j))
                        for m in range(nb):
                            k = OFF[t] + (k0 + m) * P
                            last = nc.tensor.transpose(tp[:, j % 2, m * P:(m + 1) * P], e[:, k:k + P], core.ident[:])
                        last.then_inc(tp_full, 1)

                def values(i):
                    if i == 0 and h % 2 == 0:
                        pe.wait_ge(v_in[h // 2 % PAIRS], at(lambda s: ((s - 4) // 2 // PAIRS + 1) * 16))
                    for j in chunks_of[i]:
                        t, k0, nb = chunks[j]
                        half = t // 4
                        if i == 0 or (i == 3 and k0 == 0):
                            pe.wait_ge(ov_free, at(lambda s: ONE + 2 * (s - 4) - (i == 3 and s > 4)))
                        pe.wait_ge(tp_free, at(lambda s: ONE + (s - 4) * NCH + j + 2))
                        for m in range(nb):
                            kb = k0 + m
                            last = nc.tensor.matmul(ov[:, half, (t % 4) * P:(t % 4 + 1) * P],
                                                    v[:, h // 2 % PAIRS, h % 2, kb * VH:(kb + 1) * VH],
                                                    pt[:, j % 4, m * P:(m + 1) * P], start=(kb == 0), stop=(kb == t))
                        last.then_inc(pt_used, 1)

                if live(s):
                    for t in range(TB):
                        score_tile(t)
                if live(h):
                    for i in range(TB):
                        transposes(i)
                        if i:
                            values(i - 1)
                    values(TB - 1)
                if live(s - 3):
                    n = place["bad", s - 3]
                    pe.wait_ge(sc_free, at(lambda s: ONE + place["bad", s - 3]))
                    pe.wait_ge(bad_full, at(lambda s: s - 2))
                    nc.tensor.matmul(sc[0:1, n % 2, 0:TB], ones_col[:], bad[:], start=True, stop=True).then_inc(sc_full, 1)

            slots(pe, LEAD, UNROLL, TOTAL, emit)

        @block.scalar
        def _(act):
            act.sem_inc(tp_free, ONE + 1)
            act.sem_inc(ov_free, ONE)

            def emit(s, at):
                def counts(r, h, head):
                    def tile(i):
                        if i == 0:
                            act.drain()
                            act.wait_ge(guessed[r], at(lambda s: head(s) + 1))
                        t = i + 1
                        last = nc.scalar.activation(signs[:, OFF[t] - P:OFF[t + 1] - P], scores[:, h % 4, OFF[t]:OFF[t + 1]],
                                                    ACT.Sign, bias=at_now[:, h % 4, 0, i:i + 1], scale=-1.0,
                                                    accum_out=signed[:, h % 4, i:i + 1])
                        if i == BUSY - 1:
                            last.then_inc(counted[r], 1)
                    return [(tile, i) for i in range(BUSY)] if live(h) else []

                def exponentials(i):
                    t = order[i]
                    if i == 0:
                        act.wait_ge(nmax_full, at(lambda s: s - 2))
                    if s > 3:
                        act.wait_ge(tp_full, at(lambda s: ONE + (s - 4) * NCH + chunks_of[i][-1] + 1))
                    nc.scalar.activation(e[:, OFF[t]:OFF[t + 1]], scores[:, (s - 3) % 4, OFF[t]:OFF[t + 1]],
                                         ACT.Exp, bias=nmax[:, (s - 3) % 4, t:t + 1]).then_inc(e_full, 1)

                def copy(j):
                    nb = chunks[j][2]
                    act.wait_ge(tp_full, at(lambda s: ONE + (s - 4) * NCH + j + 1))
                    act.wait_ge(pt_used, at(lambda s: ONE + (s - 4) * NCH + j))
                    nc.scalar.activation(pt[:, j % 4, 0:nb * P], tp[:, j % 2, 0:nb * P], ACT.Copy).then_inc(tp_free, 1)

                def half_out(half):
                    h = s - 4
                    act.wait_ge(pt_used, at(lambda s: ONE + 3 + (s - 4) * NCH + done_at[half] + 1))
                    if half == 1:
                        act.wait_ge(o_out[h // 2 % PAIRS], at(lambda s: ONE + (s - 4) // 2 // PAIRS * 48))
                    nc.scalar.activation(o[:, h % 4, half * 512:(half + 1) * 512], ov[:, half, :],
                                         ACT.Copy).then_inc(ov_free, 1)

                def run(steps):
                    for f, i in steps:
                        f(i)

                run(counts(0, s - 1, lambda s: s - 1))
                c2 = counts(2, s - 2, lambda s: s - 2)
                for j in range(NCH):
                    if live(s - 4):
                        copy(j)
                    run(c2[j * BUSY // NCH:(j + 1) * BUSY // NCH])
                c1 = counts(1, s - 1, lambda s: s - 1)
                run(c1[:1])
                if live(s - 4):
                    half_out(1)
                    half_out(0)
                run(c1[1:])
                for i in range(TB):
                    if live(s - 3):
                        exponentials(i)
                run(counts(3, s - 2, lambda s: s - 2))

            slots(act, LEAD, UNROLL, TOTAL, emit)

        @block.gpsimd
        def _(pool):
            g = nc.gpsimd
            g.memset(minus_one[:], -1.0)
            g.memset(minus_half[:], -0.5)
            g.memset(half[:], 0.5)
            for i, sign in enumerate((1.0, -1.0)):
                g.memset(reach[:, :, i, 1, :], sign * SPAN)
            g.memset(ones_col[:], 1.0)
            pool.drain().then_inc(ones_set, 1)
            pool.wait_ge(tab_in, 32)

            def emit(s, at):
                def correct(r, h, head):
                    if not live(h):
                        return
                    h4 = h % 4
                    now, br = at_now[:, h4], bracket[:, h4]
                    pool.wait_ge(counted[r], at(lambda s: head(s) + 1))
                    g.tensor_tensor(now[:, 1, :], signed[:, h4, :], minus_half[:], ALU.mult)
                    pool.drain()
                    g.tensor_tensor(now[:, 1, :], now[:, 1, :], tab[:, 2, :], ALU.add)
                    pool.drain()
                    both = now.rearrange("p (a b) t -> p a b t", a=1).to_broadcast([P, 2, 2, BUSY])
                    g.tensor_scalar(side[:, 0, 0, :], now[:, 1, :], 0.0, None, ALU.is_ge)
                    g.tensor_scalar(side[:, 1, 0, :], now[:, 1, :], 0.0, None, ALU.is_lt)
                    if r == 0:
                        g.tensor_tensor(br, both, reach[:, h4], ALU.add)
                        pool.drain()
                    g.tensor_tensor(diff[:], both, br, ALU.subtract)
                    pool.drain()
                    g.tensor_tensor(diff[:], diff[:], side[:].to_broadcast([P, 2, 2, BUSY]), ALU.mult)
                    pool.drain()
                    g.tensor_tensor(br, br, diff[:], ALU.add)
                    pool.drain()
                    g.tensor_tensor(gap[:], br[:, 0], br[:, 1], ALU.subtract)
                    g.tensor_tensor(step[:, 1, :], now[:, 1, :], now[:, 1, :], ALU.mult)
                    pool.drain()
                    g.tensor_tensor(step[:, 0, :], gap[:, 1, :], minus_one[:, 0:BUSY], ALU.pow)
                    g.tensor_scalar(step[:, 1, :], step[:, 1, :], (HI - AIM + 0.25) ** 2, None, ALU.is_gt)
                    pool.drain()
                    g.tensor_tensor(step[:, 0, :], step[:, 0, :], br[:, 0, 1, :], ALU.mult)
                    pool.drain()
                    g.tensor_tensor(step[:, 0, :], step[:, 0, :], gap[:, 0, :], ALU.mult)
                    pool.drain()
                    g.tensor_tensor(step[:, 0, :], br[:, 0, 0, :], step[:, 0, :], ALU.subtract)
                    pool.drain()
                    g.tensor_tensor(step[:, 0, :], step[:, 0, :], now[:, 0, :], ALU.subtract)
                    pool.drain()
                    g.tensor_tensor(step[:, 0, :], step[:, 0, :], step[:, 1, :], ALU.mult)
                    pool.drain()
                    g.tensor_tensor(now[:, 0, :], now[:, 0, :], step[:, 0, :], ALU.add)
                    pool.drain()
                    if r == ROUNDS - 1:
                        g.tensor_copy(below[:, h4, :, 8], now[:, 0, :]).then_inc(guessed[r + 1], 1)
                    else:
                        pool.drain().then_inc(guessed[r + 1], 1)

                if live(s):
                    pool.wait_ge(head_full, at(lambda s: s + 1))
                    g.tensor_tensor(nmax[:, s % 4, :], largest[:, s % 4, :], minus_one[:], ALU.mult).then_inc(nmax_full, 1)
                    h4 = s % 4
                    now, part = at_now[:, h4], stats[:, s % 4]
                    g.tensor_tensor(now[:, 0, :], part[:, :, 1], part[:, :, 4], ALU.add)
                    g.tensor_tensor(step[:, 0, :], part[:, :, 2], part[:, :, 5], ALU.add)
                    pool.drain()
                    g.tensor_scalar(now[:, 0, :], now[:, 0, :], 0.5, None, ALU.mult)
                    g.tensor_tensor(step[:, 0, :], step[:, 0, :], tab[:, 3, :], ALU.mult)
                    pool.drain()
                    spread = step[:, 1, :]
                    g.tensor_tensor(spread, step[:, 0, :], half[:], ALU.pow)
                    pool.drain()
                    g.tensor_tensor(step[:, 0, :], spread, tab[:, 0, :], ALU.mult)
                    g.tensor_tensor(reach[:, h4, 1, 0, :], spread, tab[:, 1, :], ALU.mult)
                    pool.drain()
                    g.tensor_tensor(now[:, 0, :], now[:, 0, :], step[:, 0, :], ALU.add)
                    g.tensor_scalar(reach[:, h4, 0, 0, :], reach[:, h4, 1, 0, :], -1.0, None, ALU.mult)
                    pool.drain().then_inc(guessed[0], 1)
                correct(0, s - 1, lambda s: s - 1)
                correct(2, s - 2, lambda s: s - 2)
                correct(1, s - 1, lambda s: s - 1)
                correct(3, s - 2, lambda s: s - 2)

            slots(pool, LEAD, UNROLL, TOTAL, emit)

        @block.vector
        def _(dve):
            dve.sem_inc(sc_free, ONE + 1)

            def emit(s, at):
                if live(s):
                    dve.drain()
                    for t in range(TB):
                        n = place["tile", s, t]
                        dve.wait_ge(sc_full, at(lambda s: place["tile", s, t] + 1))
                        nc.vector.tensor_scalar(scores[:, s % 4, OFF[t]:OFF[t + 1]], sc[:, n % 2, 0:(t + 1) * P], 0.0,
                                                None, ALU.add, ALU.max,
                                                accum_out=largest[:, s % 4, t:t + 1]).then_inc(sc_free, 1)
                    dve.drain()
                    for i in range(BUSY):
                        lo, hi, by = sampled(i + 1)
                        nc.vector.bn_stats(stats[:, s % 4, i, :], scores[:, s % 4, OFF[i + 1] + lo:OFF[i + 1] + hi:by])
                    dve.drain().then_inc(head_full, 1)
                if not live(s - 3):
                    return
                h4 = (s - 3) % 4

                def tile(t):
                    return scores[:, h4, OFF[t]:OFF[t + 1]]

                SMALL = P + 1 - TOPK
                R0 = (SMALL + 7) // 8

                def first_tile_max(r):
                    nc.vector.max(top0[:, r % 2, :], rest0[:])

                def first_tile_next(r):
                    if r < R0 - 1:
                        nc.vector.match_replace(rest0[:], top0[:, r % 2, :], rest0[:], GONE)
                    else:
                        k = (SMALL - 1) % 8
                        nc.vector.tensor_scalar(kth[:, 0:1], top0[:, r % 2, k:k + 1], -1.0, None, ALU.mult)

                nc.vector.tensor_scalar(rest0[:], tile(0), -1.0, None, ALU.mult)
                dve.wait_ge(guessed[ROUNDS], at(lambda s: s - 2))
                for i in range(BUSY):
                    t = i + 1
                    nc.vector.tensor_scalar(above[:, OFF[t] - P:OFF[t + 1] - P], tile(t), below[:, h4, i, 8:9], 0.0,
                                            ALU.is_ge, ALU.add, accum_out=count[:, h4, i:i + 1])
                dve.drain()
                nc.vector.tensor_scalar(far[:], count[:, h4, :], float(-AIM), None, ALU.add)
                first_tile_max(0)
                dve.drain()
                nc.vector.tensor_tensor(far[:], far[:], far[:], ALU.mult)
                first_tile_next(0)
                dve.drain()
                nc.vector.tensor_scalar(bad[:, 0:BUSY], far[:], (HI - AIM + 0.25) ** 2, 0.0, ALU.is_gt, ALU.add,
                                        accum_out=bad[:, BUSY:TB])
                first_tile_max(1)
                dve.drain().then_inc(bad_full, 1)
                for i in range(BUSY + 1):
                    if i < BUSY:
                        t = i + 1
                        nc.vector.scalar_tensor_tensor(out=rest[:, i % 2, 0:(t + 1) * P], in0=above[:, OFF[t] - P:OFF[t + 1] - P],
                                                       scalar=GONE, in1=tile(t), op0=ALU.mult, op1=ALU.add)
                    if i:
                        nc.vector.max(below[:, h4, i - 1, 0:8], rest[:, (i - 1) % 2, 0:(i + 1) * P])
                    r = 1 + i // 2
                    if r < R0:
                        if i % 2:
                            first_tile_max(r)
                        else:
                            first_tile_next(r)
                    if i == 2:
                        n = place["bad", s - 3]
                        dve.wait_ge(sc_full, at(lambda s: place["bad", s - 3] + 1))
                        nc.vector.tensor_copy(bad_head[:], sc[0:1, n % 2, 0:TB]).then_inc(sc_free, 1)
                    dve.drain()
                for i in range(BUSY):
                    nc.vector.scalar_tensor_tensor(out=picked[:, i, :], in0=rank[:], scalar=count[:, h4, i:i + 1],
                                                   in1=below[:, h4, i, :], op0=ALU.is_equal, op1=ALU.mult,
                                                   accum_out=kth[:, i + 1:i + 2])
                dve.drain()
                any_bad = dve.value_load(bad_head[0:1, BUSY:TB], min_val=0, max_val=P * BUSY)
                with dve.If(any_bad > 0):
                    for t in range(1, TB):
                        tile_bad = dve.value_load(bad_head[0:1, t - 1:t], min_val=0, max_val=P)
                        with dve.If(tile_bad > 0):
                            work = rest[:, 0, 0:(t + 1) * P]
                            nc.vector.tensor_copy(work, tile(t))
                            dve.drain()
                            with dve.Fori(0, (TOPK - 1) // 8):
                                nc.vector.max(top8[:], work)
                                dve.drain()
                                nc.vector.match_replace(work, top8[:], work, GONE)
                                dve.drain()
                            nc.vector.max(top8[:], work)
                            dve.drain()
                            k = (TOPK - 1) % 8
                            nc.vector.tensor_copy(kth[:, t:t + 1], top8[:, k:k + 1])
                            dve.drain()
                for i in range(TB):
                    t = order[i]
                    dve.wait_ge(e_full, at(lambda s: (s - 3) * TB + i + 1))
                    nc.vector.scalar_tensor_tensor(out=e[:, OFF[t]:OFF[t + 1]], in0=tile(t), scalar=kth[:, t:t + 1],
                                                   in1=e[:, OFF[t]:OFF[t + 1]],
                                                   op0=ALU.is_ge, op1=ALU.mult).then_inc(e_cut, 1)

            slots(dve, LEAD, UNROLL, TOTAL, emit)



def mlp_gated_by_top2(core, name, xn, rinv, norm_dram, gate_dram, up_dram, down_dram):
    nc = core.nc
    ED, NE = 1024, 8
    BLK = 512
    BT = BLK // P
    NB = B * S // BLK
    EC = ED // P
    with Stage(core, name) as st:
        up_w = st.sb("up_w", [P, DC, ED])
        down_w = st.sb("down_w", [P, EC, D])
        gate_w = st.sb("gate_w", [P, DC, NE])
        n2 = st.sb("n2", [P, DC])
        xrow = st.sb("xrow", [P, BT, D])
        xt = st.sb("xt", [P, DC, BLK])
        h = st.sb("h", [P, EC, BLK])
        gp = st.sb("gp", [P, BT, NE])
        gm, gs, top2, w = (st.sb(n, [P, BT]) for n in ("gm", "gs", "top2", "w"))
        best = st.sb("best", [P, BT, 8])
        up = st.ps("up", [P, 4, 512])
        dn = st.ps("dn", [P, 4, 512])
        w_in = st.sem("w_in")
        row_full, tr_full, lg_full = st.sem("row_full"), st.sem("tr_full"), st.sem("lg_full")
        shifted, exp_full = st.sem("shifted"), st.sem("exp_full")
        up_full = st.sem("up_full")
        up_free = [st.sem(f"up_free{i}") for i in range(4)]
        dn_full, dn_used = st.sem("dn_full"), st.sem("dn_used")
        block = st.block()
        DN = BT + 3
        UPS = EC // 4

        @block.sync
        def _(sp):
            sp.dma_start(gate_w[:], gate_dram.rearrange("(c p) n -> p c n", p=P)).then_inc(w_in, 16)
            sp.dma_start(n2[:], norm_dram).then_inc(w_in, 16)
            sp.dma_start(up_w[:], up_dram.rearrange("(c p) n -> p c n", p=P)).then_inc(w_in, 16)
            sp.dma_start(down_w[:], down_dram.rearrange("(c p) n -> p c n", p=P)).then_inc(w_in, 16)

        @block.tensor
        def _(pe):
            pe.sem_inc(tr_full, ONE)
            pe.wait_ge(w_in, 64)
            with pe.Fori(0, NB) as k:
                pe.wait_ge(dn_used, ONE + k * DN)
                for t in range(BT):
                    pe.wait_ge(row_full, k * BT + t + 1)
                    for c in range(DC):
                        o = (c * 2 + t % 2) * P
                        last = nc.tensor.transpose(dn[:, t // 2, o:o + P], xrow[:, t, c * P:(c + 1) * P], core.ident[:])
                last.then_inc(tr_full, 1)
                pe.wait_ge(dn_used, ONE + k * DN + 2)
                for t in range(BT):
                    for c in range(DC):
                        last = nc.tensor.matmul(dn[:, 2, t * NE:(t + 1) * NE], xt[:, c, t * P:(t + 1) * P],
                                                gate_w[:, c, :], start=(c == 0), stop=(c == DC - 1))
                last.then_inc(lg_full, 1)
                for u in range(EC):
                    pe.wait_ge(up_free[u % 4], ONE + k * UPS + u // 4)
                    for c in range(DC):
                        last = nc.tensor.matmul(up[:, u % 4, :], up_w[:, c, u * P:(u + 1) * P], xt[:, c, :],
                                                start=(c == 0), stop=(c == DC - 1))
                    last.then_inc(up_full, 1)
                for i in range(4):
                    pe.wait_ge(up_free[i], ONE + (k + 1) * UPS)
                pe.wait_ge(dn_used, ONE + k * DN + 3)
                for t in range(BT):
                    for m in range(EC):
                        last = nc.tensor.matmul(dn[:, t, 0:D], h[:, m, t * P:(t + 1) * P], down_w[:, m, :],
                                                start=(m == 0), stop=(m == EC - 1))
                    last.then_inc(dn_full, 1)

        @block.scalar
        def _(act):
            act.sem_inc(dn_used, ONE)
            act.sem_inc(up_free[0], ONE)
            act.sem_inc(up_free[1], ONE)
            act.sem_inc(up_free[2], ONE)
            act.sem_inc(up_free[3], ONE)
            act.wait_ge(w_in, 64)
            with act.Fori(0, NB) as k:
                act.wait_ge(tr_full, ONE + k + 1)
                for n in range(BT // 2):
                    for c in range(DC):
                        last = nc.scalar.activation(xt[:, c, n * 2 * P:(n + 1) * 2 * P], dn[:, n, c * 2 * P:(c + 1) * 2 * P],
                                                    ACT.Identity, scale=n2[:, c:c + 1])
                    last.then_inc(dn_used, 1)
                act.wait_ge(shifted, k + 1)
                nc.scalar.activation(gp[:], gp[:], ACT.Exp).then_inc(exp_full, 1)
                for u in range(EC):
                    act.wait_ge(up_full, k * EC + u + 1)
                    nc.scalar.activation(h[:, u, :], up[:, u % 4, :], ACT.Silu).then_inc(up_free[u % 4], 1)

        @block.vector
        def _(dve):
            def over_experts(v):
                return v[:].rearrange("p (t a) -> p t a", a=1).to_broadcast([P, BT, NE])

            with dve.Fori(0, NB) as k:
                for t in range(BT):
                    dve.wait_ge(tr_full, ONE + k)
                    nc.vector.tensor_scalar(xrow[:, t, :], xn[:, bass.ds(k * BT + t, 1), :].rearrange("p a d -> p (a d)"),
                                            rinv[:, bass.ds(k * BT + t, 1)], None, ALU.mult).then_inc(row_full, 1)
                dve.wait_ge(lg_full, k + 1)
                lg = dn[:, 2, 0:BT * NE].rearrange("p (t e) -> p t e", e=NE)
                nc.vector.tensor_reduce(gm[:], lg, AX.X, ALU.max)
                dve.drain()
                nc.vector.tensor_tensor(gp[:], lg, over_experts(gm), ALU.subtract)
                dve.drain().then_inc(shifted, 1)
                dve.wait_ge(exp_full, k + 1)
                nc.vector.tensor_reduce(gs[:], gp[:], AX.X, ALU.add).then_inc(dn_used, 1)
                dve.drain()
                nc.vector.reciprocal(gs[:], gs[:])
                dve.drain()
                nc.vector.tensor_tensor(gp[:], gp[:], over_experts(gs), ALU.mult)
                dve.drain()
                for t in range(BT):
                    nc.vector.max(best[:, t, :], gp[:, t, :])
                dve.drain()
                nc.vector.tensor_reduce(top2[:], best[:, :, 0:2], AX.X, ALU.add)
                dve.drain()
                nc.vector.tensor_scalar(w[:], top2[:], 1e-9, None, ALU.add)
                dve.drain()
                nc.vector.reciprocal(w[:], w[:])
                dve.drain()
                nc.vector.tensor_tensor(w[:], w[:], top2[:], ALU.mult)
                dve.drain()
                for t in range(BT):
                    nv = xn[:, bass.ds(k * BT + t, 1), :].rearrange("p a d -> p (a d)")
                    xv = core.x[:, bass.ds(k * BT + t, 1), :].rearrange("p a d -> p (a d)")
                    dve.wait_ge(dn_full, k * BT + t + 1)
                    nc.vector.scalar_tensor_tensor(out=nv, in0=dn[:, t, 0:D], scalar=w[:, t:t + 1], in1=nv,
                                                   op0=ALU.mult, op1=ALU.add).then_inc(dn_used, 1)
                    dve.drain()
                    nc.vector.tensor_tensor(xv, xv, nv, ALU.add)



def build(nc, a, out, upto=99):
    ctx = ExitStack()
    with ctx:
        core = Core(nc, ctx)
        qk_dram = nc.dram_tensor("qk", [2, 3, B * D, S], BF16, kind="Internal").ap()
        v_dram = nc.dram_tensor("v_rows", [HEADS, P, TB * VH], F32, kind="Internal").ap()
        o_dram = (nc.dram_tensor("o_transposed", [B * D, S], F32, kind="Internal").ap(),
                  nc.dram_tensor("o_sums", [HEADS, S], F32, kind="Internal").ap())
        load_and_constants(core, a["x"])

        def layernormed(dst, at):
            return nc.vector.tensor_scalar(dst, core.x[:, bass.ds(at, 1), :].rearrange("p a d -> p (a d)"),
                                           core.mean_var[:, bass.ds(at, 1), 0], core.rstd[:, bass.ds(at, 1)],
                                           ALU.subtract, ALU.mult)

        def l0_ffn(name):
            layernorm_statistics(core, name + "_stat")
            moe_shared_and_routed(core, name, a["router"], a["router_bias"], a["sw1"], a["sw3"], a["sw2"], a["ew1"], a["ew2"])

        def l1_ffn(name):
            layernorm_statistics(core, name + "_stat")
            with Stage(core, name + "_rows") as st:
                xn = st.sb("xn", [P, NT, D])
                rinv = st.sb("rinv", [P, NT])
                layernorm_rows(core, name + "_ln", xn)
                rms_statistics(core, name + "_rms1", xn, rinv)

                def rms_rows(dst, at):
                    return nc.vector.tensor_scalar(dst, xn[:, bass.ds(at, 1), :].rearrange("p a d -> p (a d)"),
                                                   rinv[:, bass.ds(at, 1)], None, ALU.mult)

                project_qkv(core, name + "_qkv", a["f_qkv"], qk_dram, v_dram, rows=rms_rows, col_scale=a["n1"])
                softmax_heads(core, name + "_heads", qk_dram, v_dram, o_dram, causal=True)
                project_out(core, name + "_out", a["f_o"], o_dram, target=xn)
                rms_statistics(core, name + "_rms2", xn, rinv)
                mlp_gated_by_top2(core, name + "_mlp", xn, rinv, a["n2"], a["gate"], a["up"], a["down"])

        stages = [
            lambda: (layernorm_statistics(core, "s1"), holographic(core, a["holo_wt"], a["holo_wout"], a["dft"])),
            lambda: l0_ffn("ffn1"),
            lambda: (layernorm_statistics(core, "s3"), delta_memory(core, a["kvq"])),
            lambda: l0_ffn("ffn2"),
            lambda: (layernorm_statistics(core, "s5"),
                     project_qkv(core, "attn_a_qkv", a["a_qkv"], qk_dram, v_dram, rows=layernormed,
                                 bias=(a["a_bqk"], a["a_bv"])),
                     softmax_heads(core, "attn_a_heads", qk_dram, v_dram, o_dram, causal=False),
                     project_out(core, "attn_a_out", a["a_out"], o_dram, target=core.x, out_bias=a["a_bout"])),
            lambda: l1_ffn("ffn3"),
            lambda: (layernorm_statistics(core, "s7"),
                     project_qkv(core, "attn_b_qkv", a["b_qkv"], qk_dram, v_dram, rows=layernormed,
                                 fancy=dict(taps=[a["tq"], a["tk"], a["tv"]], cos=a["cos"], sin=a["sin"],
                                            swap=a["swap"], gamma=a["gamma"], phase=a["phase"], theta=a["theta"])),
                     topk_heads(core, "attn_b_heads", qk_dram, v_dram, o_dram,
                                dict(quantiles=a["quantiles"], ranks=a["ranks"])),
                     project_out(core, "attn_b_out", a["b_proj"], o_dram, target=core.x, out_bias=a["b_bias"])),
            lambda: l1_ffn("ffn4"),
        ]
        for s in ([stages[i] for i in upto] if isinstance(upto, (list, tuple)) else stages[:upto]):
            s()
        store(core, out)


def shape_tables(np):
    n = np.arange(32)
    ang = 2 * np.pi * ((n[:, None] * n[None, :]) % 32) / 32
    eye = np.eye(4)
    fwd = [np.kron(eye, np.cos(ang)), np.kron(eye, -np.sin(ang))]
    dft = np.stack(fwd + [m / 32 for m in fwd]).astype(np.float32)
    inv_freq = np.float32(1.0) / np.power(np.float32(10000.0), np.arange(0, HD, 2, dtype=np.float32) / np.float32(HD))
    freqs = (np.arange(S, dtype=np.float32)[None, :] * inv_freq.astype(np.float32)[:, None]).astype(np.float32)
    r = np.arange(P)
    cos = np.cos(freqs.astype(np.float64))[(r % HD) // 2].astype(np.float32)
    sin = (np.sin(freqs.astype(np.float64))[(r % HD) // 2] * np.where(r % 2, 1.0, -1.0)[:, None]).astype(np.float32)
    swap = np.zeros((P, P), np.float32)
    swap[r, r ^ 1] = 1.0
    def quantile(p):
        lo, hi = -8.0, 8.0
        for _ in range(50):
            mid = (lo + hi) / 2
            lo, hi = (mid, hi) if 0.5 * (1 + erf(mid / sqrt(2))) < p else (lo, mid)
        return lo

    tabs = np.zeros((4, P, BUSY), np.float32)
    for t in range(1, TB):
        lo, hi, by = sampled(t)
        for row in range(P):
            n = t * P + row + 1
            z = quantile(1 - AIM / n)
            density = exp(-z * z / 2) / sqrt(2 * pi)
            tabs[:, row, t - 1] = (z, SPAN / (n * density), (t + 1) * P / 2 - AIM, 1.0 / len(range(lo, hi, by)))
    ranks = np.array([TOPK - 1 - k for k in range(8)] + [TOPK], np.float32)
    return {"quantiles": tabs, "ranks": ranks, "dft": dft, "cos": cos, "sin": sin, "swap": swap}


def layout(inputs, np):
    def arr(k):
        return np.asarray(inputs[k])

    def columns(v):
        return np.ascontiguousarray(v.reshape(-1, P).T)

    c = np.ascontiguousarray
    f = {
        "x": arr("L0_attn_a_x").reshape(B * S, D),
        "holo_wt": c(arr("L0_attn_a_w_qkv").T), "holo_wout": arr("L0_attn_a_w_out"),
        "router": c(arr("L0_ffn_router_w").T), "router_bias": arr("L0_ffn_router_bias"),
        "sw1": arr("L0_ffn_sw1"), "sw3": arr("L0_ffn_sw3"), "sw2": arr("L0_ffn_sw2"),
        "ew1": arr("L0_ffn_ew1"), "ew2": arr("L0_ffn_ew2"),
        "kvq": c(np.concatenate([arr("L0_attn_b_W_k").T, arr("L0_attn_b_W_v").T, arr("L0_attn_b_W_q").T], axis=1)),
        "a_qkv": arr("L1_attn_a_w_qkv"), "a_bqk": columns(arr("L1_attn_a_b_qkv")[0:2 * D]),
        "a_bv": arr("L1_attn_a_b_qkv")[2 * D:3 * D].reshape(1, D),
        "a_out": arr("L1_attn_a_w_out"), "a_bout": arr("L1_attn_a_b_out"),
        "b_qkv": c(arr("L1_attn_b_qkv_w").T), "b_proj": c(arr("L1_attn_b_proj_w").T), "b_bias": arr("L1_attn_b_proj_b"),
        "tq": arr("L1_attn_b_kernel_q"), "tk": arr("L1_attn_b_kernel_k"), "tv": arr("L1_attn_b_kernel_v"),
        "gamma": columns(arr("L1_attn_b_gamma_freq")), "theta": arr("L1_attn_b_theta_freq"), "phase": columns(arr("L1_attn_b_phase")),
        "n1": columns(arr("L1_ffn_n1_w")), "f_qkv": c(arr("L1_ffn_qkv_w").T), "f_o": c(arr("L1_ffn_o_w").T),
        "n2": columns(arr("L1_ffn_n2_w")), "gate": c(arr("L1_ffn_gate_w").T), "up": c(arr("L1_ffn_up_w").T),
        "down": c(arr("L1_ffn_down_w").T),
    }
    f.update(shape_tables(np))
    return f


def kernel(**inputs):
    import numpy as np
    import concourse.bacc as bacc
    from concourse.bass_utils import run_bass_kernel_spmd as run

    arrays = layout(inputs, np)
    nc = bacc.Bacc("TRN2", target_bir_lowering=False, num_devices=1)
    args = {k: nc.dram_tensor(f"in_{k}", v.shape, mybir.dt.from_np(v.dtype), kind="ExternalInput").ap()
            for k, v in arrays.items()}
    out = nc.dram_tensor("out", (B * S, D), F32, kind="ExternalOutput").ap()
    build(nc, args, out)
    r = run(nc, [{f"in_{k}": v for k, v in arrays.items()}], core_ids=[0])
    return r.results[0]["out"].reshape(B, S, D)
```

```python
import concourse.bass as bass
from concourse import mybir
from contextlib import ExitStack
from math import erf, exp, pi, sqrt

F32 = mybir.dt.float32
BF16 = mybir.dt.bfloat16
U32 = mybir.dt.uint32
ALU = mybir.AluOpType
ACT = mybir.ActivationFunctionType
AX = mybir.AxisListType

P = 128
B, S, D = 4, 1024, 256
NT = B * S // P
TB = S // P
DC = D // P
NEG = -1.0e30
GONE = -3.0e38
NH, HD = 16, 16
HC = P // HD
TOPK = max(1, int(S * 0.1))
ONE = 1
LN_EPS, RMS_EPS = 1e-5, 1e-6

Q_PART = (0, 0, 1, 1, 0, 2)
K_PART = (0, 1, 0, 1, 2, 0)
QK_ROWS = len(Q_PART) * HD
VH = HD + 1


class Core:

    def __init__(self, nc, ctx):
        self.nc = nc
        self.numbers = sorted(nc.free_semaphores)
        self.turn = 0

        def sb(name, shape, dt=F32):
            return ctx.enter_context(nc.sbuf_tensor(name, shape, dt))

        self.x = sb("x", [P, NT, D])
        self.ident = sb("ident", [P, P])
        self.ident_bf = sb("ident_bf", [P, P], BF16)
        self.above = sb("above", [P, P], BF16)
        self.below = sb("below", [P, P], BF16)
        self.ones = sb("ones", [1, P])
        self.mean_var = sb("mean_var", [P, NT, 2])
        self.rstd = sb("rstd", [P, NT])


class Stage:

    def __init__(self, core, name):
        self.core, self.nc, self.name = core, core.nc, name
        self.ctx = ExitStack()
        self.sems = []

    def __enter__(self):
        self.ctx.__enter__()
        return self

    def __exit__(self, *a):
        done = self.ctx.__exit__(*a)
        if self.sems and a[0] is None:
            self.nc.clear_and_free_semaphores(self.sems)
        return done

    def sb(self, name, shape, dt=F32):
        return self.ctx.enter_context(self.nc.sbuf_tensor(f"{self.name}_{name}", shape, dt))

    def ps(self, name, shape, dt=F32):
        return self.ctx.enter_context(self.nc.psum_tensor(f"{self.name}_{name}", shape, dt))

    def sem(self, name):
        number = self.core.numbers[self.core.turn % len(self.core.numbers)]
        self.core.turn += 1
        self.sems.append(self.nc.alloc_semaphore(f"{self.name}_{name}", num=number))
        return self.sems[-1]

    def block(self):
        return self.ctx.enter_context(self.nc.Block())



def load_and_constants(core, x_dram):
    nc = core.nc
    with Stage(core, "start") as st:
        x_loaded, zeroed, ready = st.sem("x_loaded"), st.sem("zeroed"), st.sem("ready")
        block = st.block()

        @block.sync
        def _(sp):
            xv = x_dram.rearrange("(t p) d -> p t d", p=P)
            for b in range(B):
                sp.dma_start(core.x[:, b * TB:(b + 1) * TB, :], xv[:, b * TB:(b + 1) * TB, :]).then_inc(x_loaded, 16)
            sp.wait_ge(x_loaded, 16 * B)

        @block.gpsimd
        def _(pool):
            for t in (core.ident, core.ident_bf, core.above, core.below):
                nc.gpsimd.memset(t[:], 0.0).then_inc(zeroed, 1)
            nc.gpsimd.memset(core.ones[:], 1.0)
            pool.wait_ge(zeroed, 4)
            for t in (core.ident, core.ident_bf):
                nc.gpsimd.affine_select(out=t[:], in_=t[:], compare_op=ALU.not_equal, fill=1.0,
                                        base=0, pattern=[[-1, P]], channel_multiplier=1).then_inc(ready, 1)
            nc.gpsimd.affine_select(out=core.above[:], in_=core.above[:], compare_op=ALU.is_ge, fill=NEG,
                                    base=0, pattern=[[-1, P]], channel_multiplier=1).then_inc(ready, 1)
            nc.gpsimd.affine_select(out=core.below[:], in_=core.below[:], compare_op=ALU.is_ge, fill=NEG,
                                    base=0, pattern=[[1, P]], channel_multiplier=-1).then_inc(ready, 1)
            pool.wait_ge(ready, 4)


def store(core, out_dram):
    with Stage(core, "end") as st:
        stored = st.sem("stored")
        block = st.block()

        @block.sync
        def _(sp):
            ov = out_dram.rearrange("(t p) d -> p t d", p=P)
            for b in range(B):
                sp.dma_start(ov[:, b * TB:(b + 1) * TB, :], core.x[:, b * TB:(b + 1) * TB, :]).then_inc(stored, 16)
            sp.wait_ge(stored, 16 * B)



def load_beside(st, block, loads):
    if loads:
        loaded = st.sem("loaded")

        @block.sync
        def _(sp):
            for to, source in loads:
                sp.dma_start(to, source).then_inc(loaded, 16)
            sp.wait_ge(loaded, 16 * len(loads))


def layernorm_statistics(core, name, loads=()):
    nc = core.nc
    with Stage(core, name) as st:
        parts = st.sb("parts", [P, NT, 6])
        std = st.sb("std", [P, NT])
        var_ready, std_ready = st.sem("var_ready"), st.sem("std_ready")
        eps = st.sb("eps", [P, 1])
        block = st.block()
        load_beside(st, block, loads)

        @block.vector
        def _(dve):
            nc.vector.memset(eps[:], LN_EPS)
            for t in range(NT):
                nc.vector.bn_stats(parts[:, t, :], core.x[:, t, :])
            dve.drain()
            for t in range(NT):
                last = nc.vector.bn_aggr(core.mean_var[:, t, :], parts[:, t, :])
            last.then_inc(var_ready, 1)
            dve.wait_ge(std_ready, 1)
            nc.vector.reciprocal(core.rstd[:], std[:])

        @block.scalar
        def _(act):
            act.wait_ge(var_ready, 1)
            nc.scalar.activation(std[:], core.mean_var[:, :, 1], ACT.Sqrt, bias=eps[:]).then_inc(std_ready, 1)


def layernorm_rows(core, name, xn):
    nc = core.nc
    with Stage(core, name) as st:
        block = st.block()

        @block.vector
        def _(dve):
            for t in range(NT):
                nc.vector.tensor_scalar(xn[:, t, :], core.x[:, t, :], core.mean_var[:, t, 0:1],
                                        core.rstd[:, t:t + 1], ALU.subtract, ALU.mult)


def rms_statistics(core, name, xn, rinv, loads=()):
    nc = core.nc
    with Stage(core, name) as st:
        sums = st.sb("sums", [P, NT])
        std = st.sb("std", [P, NT])
        junk = st.sb("junk", [P, D])
        eps = st.sb("eps", [P, 1])
        sums_ready, std_ready = st.sem("sums_ready"), st.sem("std_ready")
        block = st.block()
        load_beside(st, block, loads)

        @block.vector
        def _(dve):
            nc.vector.memset(eps[:], RMS_EPS)
            for t in range(NT):
                last = nc.vector.tensor_tensor_reduce(
                    out=junk[:], in0=xn[:, t, :], in1=xn[:, t, :], scale=1.0, scalar=0.0,
                    op0=ALU.mult, op1=ALU.add, accum_out=sums[:, t:t + 1])
                dve.drain()
            dve.drain().then_inc(sums_ready, 1)
            dve.wait_ge(std_ready, 1)
            nc.vector.reciprocal(rinv[:], std[:])

        @block.scalar
        def _(act):
            act.wait_ge(sums_ready, 1)
            nc.scalar.activation(std[:], sums[:], ACT.Sqrt, bias=eps[:], scale=1.0 / D).then_inc(std_ready, 1)



def holographic(core, wt_dram, wout_dram, dft_dram, *, statistics):
    nc = core.nc
    NJ = 3 * DC
    with Stage(core, "holo") as st:
        wt = st.sb("wt", [P, NJ, D])
        wout = st.sb("wout", [P, DC, D])
        dft = st.sb("dft", [P, 4, P])
        wf = st.sb("wf", [P, DC, NJ, 2, P])
        wg = st.sb("wg", [P, DC, 2, D])
        xrow = st.sb("xrow", [P, 4, D])
        xt = st.sb("xt", [P, DC, S])
        kre, kim = st.sb("kre", [P, S]), st.sb("kim", [P, S])
        t1, t2, t3, t4 = (st.sb(f"t{i}", [P, S]) for i in range(1, 5))
        kvr, kvi = st.sb("kvr", [P, S]), st.sb("kvi", [P, S])
        ar, ai = st.sb("ar", [P, DC, S]), st.sb("ai", [P, DC, S])
        ps = st.ps("ps", [P, 4, 2, 512])

        fold_full, fold_free = st.sem("fold_full"), st.sem("fold_free")
        row_full = st.sem("row_full")
        tr_full, xt_full = st.sem("tr_full"), st.sem("xt_full")
        pr_full, k_full = st.sem("pr_full"), st.sem("k_full")
        v_used, q_used = st.sem("v_used"), st.sem("q_used")
        prod_full, a_full = st.sem("prod_full"), st.sem("a_full")
        y_full, y_used = st.sem("y_full"), st.sem("y_used")
        loads = []
        loads.append((wt[:], wt_dram.rearrange("(j p) d -> p j d", p=P)))
        loads.append((wout[:], wout_dram.rearrange("(c p) d -> p c d", p=P)))
        loads.append((dft[:], dft_dram.rearrange("a p n -> p a n")))
        statistics(loads)
        block = st.block()
        NF = NJ * DC

        @block.tensor
        def _(pe):
            pe.sem_inc(tr_full, ONE)
            pe.sem_inc(y_full, ONE)
            for j in range(NJ):
                for c in range(DC):
                    n = j * DC + c
                    if n >= 4:
                        pe.wait_ge(fold_free, n - 3)
                    for part in range(2):
                        last = nc.tensor.matmul(ps[:, n % 4, 0, part * P:part * P + P],
                                                wt[:, j, c * P:(c + 1) * P], dft[:, part, :], start=True, stop=True)
                    last.then_inc(fold_full, 1)
            for c in range(DC):
                for part in range(2):
                    n = NF + c * 2 + part
                    pe.wait_ge(fold_free, n - 3)
                    nc.tensor.matmul(ps[:, n % 4, 0, 0:D], dft[:, 2 + part, :], wout[:, c, :],
                                     start=True, stop=True).then_inc(fold_full, 1)
            pe.wait_ge(fold_free, NF + 2 * DC)
            with pe.Fori(0, B) as b:
                pe.wait_ge(y_used, ONE + b * TB)
                for t in range(TB):
                    pe.wait_ge(row_full, b * TB + t + 1)
                    for c in range(DC):
                        last = nc.tensor.transpose(ps[:, t // 2, 0, (c * 2 + t % 2) * P:(c * 2 + t % 2 + 1) * P],
                                                   xrow[:, t % 4, c * P:(c + 1) * P], core.ident[:])
                    if t % 2:
                        last.then_inc(tr_full, 1)
                pe.wait_ge(xt_full, (b + 1) * (TB // 2))

                def project(which, c, part, slot):
                    for half in range(2):
                        for d in range(DC):
                            last = nc.tensor.matmul(ps[:, slot, half, :], wf[:, d, which * DC + c, part, :],
                                                    xt[:, d, half * 512:(half + 1) * 512],
                                                    start=(d == 0), stop=(d == DC - 1))
                    last.then_inc(pr_full, 1)

                for c in range(DC):
                    if c:
                        pe.wait_ge(q_used, b * DC + c)
                    for part in range(2):
                        project(1, c, part, part)
                    if c:
                        pe.wait_ge(v_used, b * DC + c)
                    for part in range(2):
                        project(2, c, part, 2 + part)
                    pe.wait_ge(k_full, b * DC + c + 1)
                    for part in range(2):
                        project(0, c, part, part)
                pe.wait_ge(a_full, (b + 1) * DC)
                for t in range(TB):
                    slot, bank = t % 4, t // 4
                    for n in range(2 * DC):
                        c, part = n // 2, n % 2
                        a = (ar, ai)[part]
                        last = nc.tensor.matmul(ps[:, slot, bank, 0:D], a[:, c, t * P:(t + 1) * P], wg[:, c, part, :],
                                                start=(n == 0), stop=(n == 2 * DC - 1))
                    last.then_inc(y_full, 1)

        @block.scalar
        def _(act):
            for n in range(NF):
                act.wait_ge(fold_full, n + 1)
                nc.scalar.activation(wf[:, n % DC, n // DC, :, :],
                                     ps[:, n % 4, 0, 0:2 * P].rearrange("p (a f) -> p a f", a=2),
                                     ACT.Copy).then_inc(fold_free, 1)
            for n in range(NF, NF + 2 * DC):
                act.wait_ge(fold_full, n + 1)
                nc.scalar.activation(wg[:, (n - NF) // 2, (n - NF) % 2, :], ps[:, n % 4, 0, 0:D],
                                     ACT.Copy).then_inc(fold_free, 1)
            with act.Fori(0, B) as b:
                for n in range(TB // 2):
                    act.wait_ge(tr_full, ONE + b * (TB // 2) + n + 1)
                    nc.scalar.activation(xt[:, :, n * 2 * P:(n + 1) * 2 * P],
                                         ps[:, n, 0, :].rearrange("p (c t) -> p c t", c=DC),
                                         ACT.Copy).then_inc(xt_full, 1)
                for c in range(DC):
                    act.wait_ge(pr_full, b * 6 * DC + c * 6 + 2)
                    if c:
                        act.wait_ge(v_used, b * DC + c)
                    nc.scalar.activation(kre[:], ps[:, 0, :, :].rearrange("p a n -> p (a n)"), ACT.Copy)
                    nc.scalar.activation(kim[:], ps[:, 1, :, :].rearrange("p a n -> p (a n)"),
                                         ACT.Copy).then_inc(k_full, 1)

        @block.vector
        def _(dve):
            dve.sem_inc(y_used, ONE)
            def slot(i):
                return ps[:, i, :, :].rearrange("p a n -> p (a n)")

            with dve.Fori(0, B) as b:
                for t in range(TB):
                    dve.wait_ge(tr_full, ONE + b * (TB // 2) + max(0, t // 2 - 1))
                    nc.vector.tensor_scalar(xrow[:, t % 4, :], core.x[:, bass.ds(b * TB + t, 1), :].rearrange("p a d -> p (a d)"),
                                            core.mean_var[:, bass.ds(b * TB + t, 1), 0], core.rstd[:, bass.ds(b * TB + t, 1)],
                                            ALU.subtract, ALU.mult).then_inc(row_full, 1)
                for c in range(DC):
                    dve.wait_ge(k_full, b * DC + c + 1)
                    dve.wait_ge(pr_full, b * 6 * DC + c * 6 + 4)
                    nc.vector.tensor_tensor(t1[:], kre[:], slot(2), ALU.mult)
                    nc.vector.tensor_tensor(t2[:], kim[:], slot(3), ALU.mult)
                    nc.vector.tensor_tensor(t3[:], kre[:], slot(3), ALU.mult)
                    nc.vector.tensor_tensor(t4[:], kim[:], slot(2), ALU.mult)
                    dve.drain().then_inc(v_used, 1)
                    nc.vector.tensor_tensor_scan(kvr[:], t1[:], t2[:], 0.0, ALU.add, ALU.subtract)
                    nc.vector.tensor_tensor_scan(kvi[:], t3[:], t4[:], 0.0, ALU.add, ALU.add)
                    dve.drain()
                    dve.wait_ge(pr_full, b * 6 * DC + c * 6 + 6)
                    nc.vector.tensor_tensor(t1[:], kvr[:], slot(0), ALU.mult)
                    nc.vector.tensor_tensor(t2[:], kvi[:], slot(1), ALU.mult)
                    nc.vector.tensor_tensor(t3[:], kvi[:], slot(0), ALU.mult)
                    nc.vector.tensor_tensor(t4[:], kvr[:], slot(1), ALU.mult)
                    dve.drain().then_inc(q_used, 1)
                    if c == 0:
                        dve.wait_ge(y_full, ONE + b * TB)
                    nc.vector.tensor_tensor(ar[:, c, :], t1[:], t2[:], ALU.add)
                    nc.vector.tensor_tensor(ai[:, c, :], t3[:], t4[:], ALU.subtract)
                    dve.drain().then_inc(a_full, 1)
                for t in range(TB):
                    xv = core.x[:, bass.ds(b * TB + t, 1), :].rearrange("p a d -> p (a d)")
                    dve.wait_ge(y_full, ONE + b * TB + t + 1)
                    nc.vector.tensor_tensor(xv, ps[:, t % 4, t // 4, 0:D], xv, ALU.add).then_inc(y_used, 1)



def moe_shared_and_routed(core, name, router_dram, bias_dram, sw1, sw3, sw2, ew1, ew2, *, statistics):
    nc = core.nc
    HS, HR, NE = 512, 256, 8
    BLK = 512
    BT = BLK // P
    NB = B * S // BLK
    SC, RC = HS // P, HR // P
    NU = SC * 2 + NE * RC
    with Stage(core, name) as st:
        w1s, w3s = st.sb("w1s", [P, DC, HS]), st.sb("w3s", [P, DC, HS])
        w2s = st.sb("w2s", [P, SC, D])
        w1e = st.sb("w1e", [P, NE, DC, HR])
        w2e = st.sb("w2e", [P, NE, RC, D])
        rw = st.sb("rw", [P, DC, NE])
        rb = st.sb("rb", [P, NE])
        iota = st.sb("iota", [P, NE])
        xrow = st.sb("xrow", [P, BT, D])
        xt = st.sb("xt", [P, 2, DC, BLK])
        sil = st.sb("sil", [P, SC, BLK])
        hs = st.sb("hs", [P, SC, BLK])
        he = st.sb("he", [P, NE * RC, BLK])
        score, sel = st.sb("score", [P, BT, NE]), st.sb("sel", [P, BT, NE])
        best, best_at = st.sb("best", [P, BT, 8]), st.sb("best_at", [P, BT, 8], U32)
        best_f = st.sb("best_f", [P, BT, 8])
        hot, hot2 = st.sb("hot", [P, BT, NE]), st.sb("hot2", [P, BT, NE])
        chosen, denom, inv, big, half = (st.sb(n, [P, BT, NE] if n == "chosen" else [P, BT])
                                         for n in ("chosen", "denom", "inv", "big", "half"))
        comb = st.sb("comb", [P, BT, NE])
        acc = st.sb("acc", [P, BT, D])
        up = st.ps("up", [P, 4, 512])
        dn = st.ps("dn", [P, 4, 512])

        io = st.sem("iota")
        row_full, tr_full = st.sem("row_full"), st.sem("tr_full")
        lg_full = st.sem("lg_full")
        up_full = st.sem("up_full")
        up_free = [st.sem(f"up_free{i}") for i in range(4)]
        dn_full, dn_used, gated = st.sem("dn_full"), st.sem("dn_used"), st.sem("gated")
        loads = []
        loads.append((rw[:], router_dram.rearrange("(c p) n -> p c n", p=P)))
        loads.append((rb[:], bias_dram.partition_broadcast(P)))
        loads.append((w1s[:], sw1.rearrange("(c p) n -> p c n", p=P)))
        loads.append((w3s[:], sw3.rearrange("(c p) n -> p c n", p=P)))
        loads.append((w2s[:], sw2.rearrange("(c p) n -> p c n", p=P)))
        for e in range(NE):
            loads.append((w1e[:, e], ew1[e].rearrange("(c p) n -> p c n", p=P)))
            loads.append((w2e[:, e], ew2[e].rearrange("(c p) n -> p c n", p=P)))
        statistics(loads)
        block = st.block()
        DN = BT * (1 + NE // 2)

        def blocks(eng, emit):
            with eng.Fori(0, NB // 2 - 1) as i:
                emit(i * 2, 0, True)
                emit(i * 2 + 1, 1, True)
            emit(NB - 2, 0, True)
            emit(NB - 1, 1, False)

        def dn_before(k):
            return ONE + 3 + k * (DN + 3)
        UPS = NU // 4

        @block.gpsimd
        def _(pool):
            nc.gpsimd.iota(iota[:], pattern=[[1, NE]], base=0, channel_multiplier=0,
                           allow_small_or_imprecise_dtypes=True).then_inc(io, 1)

        @block.tensor
        def _(pe):
            pe.sem_inc(tr_full, ONE)

            def prepare(k, parity, before):
                pe.wait_ge(dn_used, before)
                for t in range(BT):
                    pe.wait_ge(row_full, k * BT + t + 1)
                    for c in range(DC):
                        o = (c * 2 + t % 2) * P
                        last = nc.tensor.transpose(dn[:, t // 2, o:o + P], xrow[:, t, c * P:(c + 1) * P],
                                                   core.ident[:])
                last.then_inc(tr_full, 1)
                pe.wait_ge(dn_used, before + 2)
                for t in range(BT):
                    for c in range(DC):
                        last = nc.tensor.matmul(dn[:, 2, t * NE:(t + 1) * NE], xt[:, parity, c, t * P:(t + 1) * P],
                                                rw[:, c, :], start=(c == 0), stop=(c == DC - 1))
                last.then_inc(lg_full, 1)

            def emit(k, parity, has_next):
                for u in range(NU):
                    if u < 2 * SC:
                        w, m = ((w1s, w3s)[u % 2], u // 2)
                        lhs = [w[:, c, m * P:(m + 1) * P] for c in range(DC)]
                    else:
                        e, m = (u - 2 * SC) // RC, (u - 2 * SC) % RC
                        lhs = [w1e[:, e, c, m * P:(m + 1) * P] for c in range(DC)]
                    pe.wait_ge(up_free[u % 4], ONE + k * UPS + u // 4)
                    for c in range(DC):
                        last = nc.tensor.matmul(up[:, u % 4, :], lhs[c], xt[:, parity, c, :],
                                                start=(c == 0), stop=(c == DC - 1))
                    last.then_inc(up_full, 1)
                if has_next:
                    prepare(k + 1, 1 - parity, dn_before(k))
                n = 0
                for t in range(BT):
                    if t == 0:
                        for i in range(4):
                            pe.wait_ge(up_free[i], ONE + (k + 1) * UPS)
                    for g in range(1 + NE // 2):
                        pe.wait_ge(dn_used, dn_before(k) + 3 * has_next + max(0, n - 3))
                        if g == 0:
                            for m in range(SC):
                                last = nc.tensor.matmul(dn[:, n % 4, 0:D], hs[:, m, t * P:(t + 1) * P],
                                                        w2s[:, m, :], start=(m == 0), stop=(m == SC - 1))
                        else:
                            for e in (2 * g - 2, 2 * g - 1):
                                for m in range(RC):
                                    o = (e % 2) * D
                                    last = nc.tensor.matmul(dn[:, n % 4, o:o + D],
                                                            he[:, e * RC + m, t * P:(t + 1) * P],
                                                            w2e[:, e, m, :], start=(m == 0), stop=(m == RC - 1))
                        last.then_inc(dn_full, 1)
                        n += 1

            prepare(0, 0, ONE)
            blocks(pe, emit)

        @block.scalar
        def _(act):
            act.sem_inc(dn_used, ONE)
            act.sem_inc(up_free[0], ONE)
            act.sem_inc(up_free[2], ONE)

            def prepare(k, parity):
                act.wait_ge(tr_full, ONE + k + 1)
                for n in range(BT // 2):
                    nc.scalar.activation(xt[:, parity, :, n * 2 * P:(n + 1) * 2 * P],
                                         dn[:, n, :].rearrange("p (c t) -> p c t", c=DC), ACT.Copy).then_inc(dn_used, 1)
                act.wait_ge(lg_full, k + 1)
                act.wait_ge(gated, ONE + k)
                nc.scalar.activation(score[:], dn[:, 2, 0:BT * NE].rearrange("p (t e) -> p t e", e=NE),
                                     ACT.Sigmoid).then_inc(dn_used, 1)

            def emit(k, parity, has_next):
                for u in range(0, 2 * SC, 2):
                    act.wait_ge(up_full, k * NU + u + 1)
                    nc.scalar.activation(sil[:, u // 2, :], up[:, u % 4, :], ACT.Silu).then_inc(up_free[u % 4], 1)
                for u in range(2 * SC, NU):
                    act.wait_ge(up_full, k * NU + u + 1)
                    nc.scalar.activation(he[:, u - 2 * SC, :], up[:, u % 4, :], ACT.Gelu).then_inc(up_free[u % 4], 1)
                if has_next:
                    prepare(k + 1, 1 - parity)

            prepare(0, 0)
            blocks(act, emit)

        @block.vector
        def _(dve):
            dve.sem_inc(up_free[1], ONE)
            dve.sem_inc(up_free[3], ONE)
            dve.wait_ge(io, 1)
            dve.sem_inc(gated, ONE)

            def rows(k):
                dve.wait_ge(tr_full, ONE + k)
                for t in range(BT):
                    nc.vector.tensor_scalar(xrow[:, t, :], core.x[:, bass.ds(k * BT + t, 1), :].rearrange("p a d -> p (a d)"),
                                            core.mean_var[:, bass.ds(k * BT + t, 1), 0], core.rstd[:, bass.ds(k * BT + t, 1)],
                                            ALU.subtract, ALU.mult).then_inc(row_full, 1)

            def gates(k, before):
                dve.wait_ge(dn_used, before + 3)
                rb_b = rb[:].rearrange("p (a e) -> p a e", a=1).to_broadcast([P, BT, NE])
                io_b = iota[:].rearrange("p (a e) -> p a e", a=1).to_broadcast([P, BT, NE])
                nc.vector.tensor_tensor(sel[:], score[:], rb_b, ALU.add)
                dve.drain()
                for t in range(BT):
                    nc.vector.max(best[:, t, :], sel[:, t, :])
                dve.drain()
                for t in range(BT):
                    nc.vector.max_index(best_at[:, t, :], best[:, t, :], sel[:, t, :])
                dve.drain()
                nc.vector.tensor_copy(best_f[:], best_at[:])
                dve.drain()
                nc.vector.tensor_tensor(hot[:], io_b, best_f[:, :, 0:1].to_broadcast([P, BT, NE]), ALU.is_equal)
                nc.vector.tensor_tensor(hot2[:], io_b, best_f[:, :, 1:2].to_broadcast([P, BT, NE]), ALU.is_equal)
                dve.drain()
                nc.vector.tensor_tensor(hot[:], hot[:], hot2[:], ALU.add)
                dve.drain()
                nc.vector.tensor_tensor(chosen[:], hot[:], score[:], ALU.mult)
                dve.drain()
                nc.vector.tensor_reduce(denom[:], chosen[:], AX.X, ALU.add)
                dve.drain()
                nc.vector.tensor_scalar(inv[:], denom[:], 1e-9, None, ALU.add)
                nc.vector.tensor_scalar(big[:], denom[:], 1e-9, None, ALU.is_gt)
                dve.drain()
                nc.vector.reciprocal(inv[:], inv[:])
                nc.vector.tensor_scalar(half[:], big[:], -0.5, 0.5, ALU.mult, ALU.add)
                dve.drain()
                nc.vector.tensor_tensor(inv[:], inv[:], big[:], ALU.mult)
                dve.drain()

                def over_experts(v):
                    return v[:].rearrange("p (t a) -> p t a", a=1).to_broadcast([P, BT, NE])

                nc.vector.tensor_tensor(chosen[:], chosen[:], over_experts(inv), ALU.mult)
                nc.vector.tensor_tensor(hot[:], hot[:], over_experts(half), ALU.mult)
                dve.drain()
                nc.vector.tensor_tensor(comb[:], chosen[:], hot[:], ALU.add)
                dve.drain().then_inc(gated, 1)

            def emit(k, parity, has_next):
                if has_next:
                    rows(k + 1)
                for m in range(SC):
                    dve.wait_ge(up_free[(2 * m) % 4], ONE + k * UPS + m // 2 + 1)
                    dve.wait_ge(up_full, k * NU + 2 * m + 2)
                    nc.vector.tensor_tensor(hs[:, m, :], sil[:, m, :], up[:, (2 * m + 1) % 4, :],
                                            ALU.mult).then_inc(up_free[(2 * m + 1) % 4], 1)
                n = 0
                for t in range(BT):
                    xv = core.x[:, bass.ds(k * BT + t, 1), :].rearrange("p a d -> p (a d)")
                    for g in range(1 + NE // 2):
                        if g:
                            dve.drain()
                        dve.wait_ge(dn_full, k * DN + n + 1)
                        if g == 0:
                            last = nc.vector.tensor_copy(acc[:, t, :], dn[:, n % 4, 0:D])
                        else:
                            for e in (2 * g - 2, 2 * g - 1):
                                o = (e % 2) * D
                                if e % 2:
                                    dve.drain()
                                last = nc.vector.scalar_tensor_tensor(out=acc[:, t, :], in0=dn[:, n % 4, o:o + D],
                                                                      scalar=comb[:, t, e:e + 1], in1=acc[:, t, :],
                                                                      op0=ALU.mult, op1=ALU.add)
                        last.then_inc(dn_used, 1)
                        n += 1
                    dve.drain()
                    nc.vector.tensor_tensor(xv, acc[:, t, :], xv, ALU.add)
                if has_next:
                    gates(k + 1, dn_before(k))

            rows(0)
            gates(0, ONE)
            blocks(dve, emit)



def delta_memory(core, wkvq_dram, *, statistics):
    with Stage(core, "delta_kvq") as st:
        kvq = st.sb("kvq", [P, NT, 3, D])
        delta_projections(core, wkvq_dram, kvq, statistics)
        delta_recurrence(core, kvq)


NBK, BK = 32, 8


def delta_projections(core, wkvq_dram, kvq, statistics):
    nc = core.nc
    UN = 4
    with Stage(core, "delta") as st:
        w = st.sb("w", [P, DC, 3 * D])
        xrow = st.sb("xrow", [P, UN, D])
        xt = st.sb("xt", [P, 2, DC, P])
        sq = st.sb("sq", [P, 2, D])
        norm = st.sb("norm", [P, NT * NBK])
        tr = st.ps("tr", [P, 2, 512])
        pj = st.ps("pj", [P, 2, 1024])
        row_full, tr_full, xt_full = (st.sem(n) for n in ("row_full", "tr_full", "xt_full"))
        pj_full, pj_used, sq_full, sq_used = (st.sem(n) for n in ("pj_full", "pj_used", "sq_full", "sq_used"))
        ss_full, root_full = st.sem("ss_full"), st.sem("root_full")

        loads = []
        loads.append((w[:], wkvq_dram.rearrange("(c p) n -> p c n", p=P)))
        statistics(loads)
        block = st.block()

        @block.tensor
        def _(pe):
            pe.sem_inc(tr_full, ONE)
            with pe.Fori(0, NT // UN) as i:
                def transposes(j):
                    pe.wait_ge(row_full, i * UN + j + 1)
                    if j >= 2:
                        pe.wait_ge(xt_full, i * UN + j - 1)
                    for c in range(DC):
                        last = nc.tensor.transpose(tr[:, j % 2, c * P:(c + 1) * P], xrow[:, j, c * P:(c + 1) * P],
                                                   core.ident[:])
                    last.then_inc(tr_full, 1)

                transposes(0)
                transposes(1)
                for j in range(UN):
                    pe.wait_ge(xt_full, i * UN + j + 1)
                    pe.wait_ge(pj_used, ONE + i * UN + j)
                    for lo, hi in ((0, 512), (512, 768)):
                        for c in range(DC):
                            last = nc.tensor.matmul(pj[:, j % 2, lo:hi], xt[:, j % 2, c, :], w[:, c, lo:hi],
                                                    start=(c == 0), stop=(c == DC - 1))
                    last.then_inc(pj_full, 1)
                    if j + 2 < UN:
                        transposes(j + 2)

        @block.scalar
        def _(act):
            act.sem_inc(pj_used, ONE + 1)
            with act.Fori(0, NT // UN) as i:
                def copy_rows(j):
                    act.wait_ge(tr_full, ONE + i * UN + j + 1)
                    nc.scalar.activation(xt[:, j % 2], tr[:, j % 2, 0:DC * P].rearrange("p (c t) -> p c t", c=DC),
                                         ACT.Copy).then_inc(xt_full, 1)

                copy_rows(0)
                copy_rows(1)
                for j in range(UN):
                    act.wait_ge(pj_full, i * UN + j + 1)
                    act.wait_ge(sq_used, ONE + i * UN + j)
                    nc.scalar.activation(sq[:, j % 2, :], pj[:, j % 2, 0:D], ACT.Square).then_inc(sq_full, 1)
                    nc.scalar.activation(kvq[:, bass.ds(i * UN + j, 1)].rearrange("p a b d -> p (a b d)"),
                                         pj[:, j % 2, 0:3 * D], ACT.Copy).then_inc(pj_used, 1)
                    if j + 2 < UN:
                        copy_rows(j + 2)
            act.wait_ge(ss_full, 1)
            nc.scalar.activation(norm[:], norm[:], ACT.Sqrt).then_inc(root_full, 1)

        @block.vector
        def _(dve):
            dve.sem_inc(sq_used, ONE + 1)

            def row(at, j):
                nc.vector.tensor_scalar(xrow[:, j, :], core.x[:, bass.ds(at, 1), :].rearrange("p a d -> p (a d)"),
                                        core.mean_var[:, bass.ds(at, 1), 0], core.rstd[:, bass.ds(at, 1)],
                                        ALU.subtract, ALU.mult).then_inc(row_full, 1)

            with dve.Fori(0, NT // UN) as i:
                dve.wait_ge(tr_full, ONE + i * UN)
                for j in range(UN):
                    row(i * UN + j, j)
                for j in range(UN):
                    dve.wait_ge(sq_full, i * UN + j + 1)
                    nc.vector.tensor_reduce(norm[:, bass.ds((i * UN + j) * NBK, NBK)],
                                            sq[:, j % 2, :].rearrange("p (n e) -> p n e", e=BK), AX.X,
                                            ALU.add).then_inc(sq_used, 1)
            dve.drain().then_inc(ss_full, 1)
            dve.wait_ge(root_full, 1)
            nc.vector.tensor_scalar(norm[:], norm[:], 1e-6, None, ALU.add)
            dve.drain()
            nc.vector.reciprocal(norm[:], norm[:])
            dve.drain()
            for t in range(NT):
                k = kvq[:, t, 0, :].rearrange("p (n e) -> p n e", e=BK)
                r = norm[:, t * NBK:(t + 1) * NBK].rearrange("p (n a) -> p n a", a=1).to_broadcast([P, NBK, BK])
                nc.vector.tensor_tensor(k, k, r, ALU.mult)


def delta_recurrence(core, kvq):
    nc = core.nc
    with Stage(core, "recur") as s2:
        state = s2.sb("state", [P, 2, NBK, BK, BK])
        prod = s2.sb("prod", [P, 2, NBK, BK, BK])
        ret = s2.sb("ret", [P, 2, NBK, BK])
        pre_full, tanh_full = s2.sem("pre_full"), s2.sem("tanh_full")
        sq_done, silu_done = s2.sem("sq_done"), s2.sem("silu_done")
        block2 = s2.block()
        full = [P, NBK, BK, BK]

        @block2.scalar
        def _(act):
            with act.Fori(0, TB // 2) as i:
                for t in range(B):
                    for s in range(2):
                        act.wait_ge(pre_full, i * (2 * B) + (2 * t + s + 1))
                        nc.scalar.activation(state[:, s], prod[:, s], ACT.Tanh).then_inc(tanh_full, 1)
            act.wait_ge(sq_done, 1)
            for t in range(NT):
                nc.scalar.activation(kvq[:, t, 2, :], kvq[:, t, 1, :], ACT.Silu).then_inc(silu_done, 1)

        @block2.vector
        def _(dve):
            with dve.Fori(0, TB // 2) as i:
                def rows_of(t, s, which):
                    return kvq[:, bass.ds(i * 2 + (t * TB + s), 1), which, :]

                def by_j(t, s, which):
                    return rows_of(t, s, which).rearrange("p a (n o e) -> p (a n) o e", e=BK, o=1).to_broadcast(full)

                def before_tanh(t, s):
                    pr, rt = prod[:, s], ret[:, s]
                    if t == 0:
                        v_e = rows_of(t, s, 1).rearrange("p a (n e o) -> p (a n) e o", e=BK, o=1)
                        nc.vector.tensor_tensor(pr, v_e.to_broadcast(full), by_j(t, s, 0), ALU.mult).then_inc(pre_full, 1)
                        return
                    v_i = rows_of(t, s, 1).rearrange("p a (n e) -> p (a n) e", e=BK)
                    nc.vector.tensor_tensor(pr, state[:, s], by_j(t, s, 0), ALU.mult)
                    dve.drain()
                    nc.vector.tensor_reduce(rt, pr, AX.X, ALU.add)
                    dve.drain()
                    nc.vector.tensor_tensor(rt, v_i, rt, ALU.subtract)
                    dve.drain()
                    d_i = rt.rearrange("p n (e o) -> p n e o", o=1).to_broadcast(full)
                    nc.vector.tensor_tensor(pr, d_i, by_j(t, s, 0), ALU.mult)
                    dve.drain()
                    nc.vector.tensor_tensor(pr, pr, state[:, s], ALU.add).then_inc(pre_full, 1)

                def after_tanh(t, s):
                    dve.wait_ge(tanh_full, i * (2 * B) + (2 * t + s + 1))
                    nc.vector.tensor_tensor(prod[:, s], state[:, s], by_j(t, s, 2), ALU.mult)
                    dve.drain()
                    v_i = rows_of(t, s, 1).rearrange("p a (n e) -> p (a n) e", e=BK)
                    nc.vector.tensor_reduce(v_i, prod[:, s], AX.X, ALU.add)
                    dve.drain()

                for t in range(B):
                    for s in range(2):
                        before_tanh(t, s)
                    for s in range(2):
                        after_tanh(t, s)
            dve.drain().then_inc(sq_done, 1)
            for t in range(NT):
                dve.wait_ge(silu_done, t + 1)
                nc.vector.tensor_tensor(kvq[:, t, 0, :], kvq[:, t, 1, :], kvq[:, t, 2, :], ALU.mult)
            dve.drain()
            for t in range(NT):
                nc.vector.tensor_tensor(core.x[:, t, :], core.x[:, t, :], kvq[:, t, 0, :], ALU.add)



def project_qkv(core, name, wqkv_dram, qk_dram, v_dram, *, statistics, rows, bias=None, col_scale=None, fancy=None):
    nc = core.nc
    FANCY = fancy is not None
    with Stage(core, name) as st:
        wqkv = st.sb("wqkv", [P, DC, 3 * D])
        xrow = st.sb("xrow", [P, 4, D])
        PAD = 3 if FANCY else 0
        xt = st.sb("xt", [P, DC, PAD + S])
        qf = st.sb("qf", [P, 2, S])
        rest = st.sb("rest", [P, S])
        part = st.sb("part", [P, 2, 3, S], BF16)
        vt = st.sb("vt", [P, NH, TB, VH])
        if bias is not None:
            bqk = st.sb("bqk", [P, 2 * DC])
            bqk4 = st.sb("bqk4", [P, 2 * DC])
            bv = st.sb("bv", [1, D])
        if col_scale is not None:
            cs = st.sb("cs", [P, DC])
        if FANCY:
            conv = st.sb("conv", [P, 3, DC, S])
            taps = st.sb("taps", [P, 3, 4])
            swap = st.sb("swap", [P, P])
            cos_t, sin_t = st.sb("cos", [P, S]), st.sb("sin", [P, S])
            gain = st.sb("gain", [P, DC, S])
            freq, phase = st.sb("freq", [P, DC]), st.sb("phase", [P, DC])
            theta = st.sb("theta", [P, 1])
            work = st.sb("work", [P, 2, S])
            angle, turns = st.sb("angle", [P, S]), st.sb("turns", [P, S])
            hp = st.sb("hp", [P, 1])
        sc = st.ps("sc", [P, 2, 1024])
        if FANCY:
            sw = st.ps("sw", [P, 1024])
        tp = st.ps("tp", [P, 2, 512])

        row_full = st.sem("row_full")
        sc_full, sc_free = st.sem("sc_full"), st.sem("sc_free")
        tp_full, tp_free = st.sem("tp_full"), st.sem("tp_free")
        part_full = st.sem("part_full")
        part_out = [st.sem("part_out0"), st.sem("part_out1")]
        v_full, v_out, ones_set = st.sem("v_full"), st.sem("v_out"), st.sem("ones_set")
        qf_full = st.sem("qf_full")
        if FANCY:
            conv_full, gain_phase, gain_sin, pos_full, sw_full, sw_free = (
                st.sem(n) for n in ("conv_full", "gain_phase", "gain_sin", "pos_full", "sw_full", "sw_free"))
        loads = []
        loads.append((wqkv[:], wqkv_dram.rearrange("(c p) n -> p c n", p=P)))
        if bias is not None:
            loads.append((bqk[:], bias[0]))
            loads.append((bv[:], bias[1]))
        if col_scale is not None:
            loads.append((cs[:], col_scale))
        if FANCY:
            for i, kern in enumerate(fancy["taps"]):
                loads.append((taps[:, i, :], kern.partition_broadcast(P)))
            loads.append((cos_t[:], fancy["cos"]))
            loads.append((sin_t[:], fancy["sin"]))
            loads.append((swap[:], fancy["swap"]))
            loads.append((freq[:], fancy["gamma"]))
            loads.append((phase[:], fancy["phase"]))
            loads.append((theta[:], fancy["theta"].partition_broadcast(P)))
        statistics(loads)
        block = st.block()

        SC_N = 4
        TP_ROWS = TB // 2
        TP_N = 2 * TP_ROWS

        def part_slot_free(eng, b, n):
            eng.wait_ge(part_out[n % 2], ONE + b * 96 + n // 2 * 48)

        @block.sync
        def _(sp):
            for sem in part_out + [v_out]:
                sp.sem_inc(sem, ONE)
            with sp.Fori(0, B) as b:
                for n in range(4):
                    c, which = n // 2, n % 2
                    sp.wait_ge(part_full, ONE + 1 + b * 4 + n + 1)
                    for i in range(3):
                        sp.dma_start(qk_dram[which, i, bass.ds(b * D + c * P, P), :],
                                     part[:, n % 2, i, :]).then_inc(part_out[n % 2], 16)
                sp.wait_ge(v_full, b + 1)
                sp.dma_start(v_dram[bass.ds(b * NH, NH), :, :].rearrange("h p e -> p h e"),
                             vt[:].rearrange("p h t e -> p h (t e)")).then_inc(v_out, 16)
            for sem in part_out:
                sp.wait_ge(sem, ONE + B * 96)
            sp.wait_ge(v_out, ONE + B * 16)

        @block.tensor
        def _(pe):
            pe.sem_inc(tp_full, ONE)
            with pe.Fori(0, B) as b:
                for t in range(TB):
                    n = t // 2
                    if t % 2 == 0:
                        pe.wait_ge(tp_free, ONE + b * TP_N + n)
                    pe.wait_ge(row_full, b * TB + t + 1)
                    for c in range(DC):
                        k0 = (c * 2 + t % 2) * P
                        last = nc.tensor.transpose(tp[:, n % 2, k0:k0 + P], xrow[:, t % 4, c * P:(c + 1) * P],
                                                   core.ident[:])
                    if t % 2:
                        last.then_inc(tp_full, 1)
                pe.wait_ge(tp_free, ONE + b * TP_N + TP_ROWS + 1)

                def source(which, c):
                    return conv[:, which, c, :] if FANCY else xt[:, c, :]

                def values(t):
                    n = TP_ROWS + t // 2
                    if t % 2 == 0:
                        pe.wait_ge(tp_free, ONE + b * TP_N + n)
                    dst = tp[:, n % 2, (t % 2) * D:(t % 2 + 1) * D]
                    for c in range(DC):
                        last = nc.tensor.matmul(dst, source(2, c)[:, t * P:(t + 1) * P], wqkv[:, c, 2 * D:3 * D],
                                                start=(c == 0), stop=(c == DC - 1 and bias is None))
                    if bias is not None:
                        last = nc.tensor.matmul(dst, core.ones[:], bv[:], start=False, stop=True)
                    if t % 2:
                        last.then_inc(tp_full, 1)

                def swapped(n):
                    pe.wait_ge(sc_free, ONE + b * SC_N + n + 2)
                    pe.wait_ge(sw_free, ONE + b * SC_N + n)
                    for half in range(2):
                        last = nc.tensor.matmul(sw[:, half * 512:(half + 1) * 512], swap[:],
                                                qf[:, n % 2, half * 512:(half + 1) * 512], start=True, stop=True)
                    last.then_inc(sw_full, 1)

                for n in range(4):
                    c, which = n // 2, n % 2
                    if FANCY and n < 2:
                        pe.wait_ge(conv_full, b * 3 + which + 1)
                    pe.wait_ge(sc_free, ONE + b * SC_N + n)
                    for half in range(2):
                        for d in range(DC):
                            k0 = which * D + c * P
                            last = nc.tensor.matmul(sc[:, n % 2, half * 512:(half + 1) * 512],
                                                    wqkv[:, d, k0:k0 + P],
                                                    source(which, d)[:, half * 512:(half + 1) * 512],
                                                    start=(d == 0), stop=(d == DC - 1))
                    last.then_inc(sc_full, 1)
                    if FANCY and n:
                        swapped(n - 1)
                    if not FANCY:
                        values(2 * n)
                        values(2 * n + 1)
                if FANCY:
                    swapped(3)
                    pe.wait_ge(conv_full, b * 3 + 3)
                    for t in range(TB):
                        values(t)

        @block.scalar
        def _(act):
            act.sem_inc(tp_free, ONE + 1)
            if not FANCY:
                act.sem_inc(sc_free, ONE + 1)
            act.wait_ge(ones_set, 1)
            if bias is not None:
                nc.scalar.activation(bqk4[:], bqk[:], ACT.Copy, scale=0.25)
                act.drain()
            if FANCY:
                for n in range(DC + 1):
                    act.wait_ge(gain_phase, n + 1)
                    nc.scalar.activation(work[:, 0, :], rest[:], ACT.Sin).then_inc(gain_sin, 1)
            with act.Fori(0, B) as b:
                for n in range(TP_ROWS):
                    act.wait_ge(tp_full, ONE + b * TP_N + n + 1)
                    src = tp[:, n % 2, :].rearrange("p (c t) -> p c t", c=DC)
                    if col_scale is None:
                        last = nc.scalar.activation(xt[:, :, PAD + n * 2 * P:PAD + (n + 1) * 2 * P], src, ACT.Copy)
                    else:
                        for c in range(DC):
                            last = nc.scalar.activation(xt[:, c, n * 2 * P:(n + 1) * 2 * P], src[:, c, :], ACT.Identity,
                                                        scale=cs[:, c:c + 1])
                    last.then_inc(tp_free, 1)

                def copy_values(n):
                    act.wait_ge(tp_full, ONE + b * TP_N + n + 1)
                    t = 2 * (n - TP_ROWS)
                    if t == 0:
                        act.wait_ge(v_out, ONE + b * 16)
                    nc.scalar.activation(vt[:, :, t:t + 2, 0:HD],
                                         tp[:, n % 2, :].rearrange("p (t h d) -> p h t d", t=2, h=NH),
                                         ACT.Copy).then_inc(tp_free, 1)

                for n in range(4):
                    c, which = n // 2, n % 2
                    if not FANCY:
                        act.wait_ge(sc_full, b * SC_N + n + 1)
                        act.wait_ge(part_full, ONE + b * 4 + n)
                        scale = 0.25 if which == 0 else 1.0
                        if bias is None:
                            last = nc.scalar.activation(qf[:, n % 2, :], sc[:, n % 2, :], ACT.Copy, scale=scale)
                        else:
                            bcol = (bqk4 if which == 0 else bqk)[:, which * DC + c:which * DC + c + 1]
                            last = nc.scalar.activation(qf[:, n % 2, :], sc[:, n % 2, :], ACT.Identity, bias=bcol,
                                                        scale=scale)
                        last.then_inc(sc_free, 1)
                    copy_values(TP_ROWS + n)
                act.drain().then_inc(v_full, 1)

        @block.gpsimd
        def _(pool):
            nc.gpsimd.memset(vt[:, :, :, HD:VH], 1.0).then_inc(ones_set, 1)
            if FANCY:
                nc.gpsimd.iota(qf[:, 0, :], pattern=[[1, S]], base=0, channel_multiplier=0,
                               allow_small_or_imprecise_dtypes=True).then_inc(pos_full, 1)

        @block.vector
        def _(dve):
            if FANCY:
                dve.sem_inc(sc_free, ONE + 1)
                dve.sem_inc(sw_free, ONE)
            TWO_PI = 2 * pi
            if FANCY:
                nc.vector.memset(xt[:, :, 0:PAD], 0.0)
                MAGIC = 12582912.0
                TWO_PI_MID = 4058 * 2.0 ** -21
                PI_PARTS = (6.28125, TWO_PI_MID, TWO_PI - 6.28125 - TWO_PI_MID)
                dve.wait_ge(pos_full, 1)
                for n in range(DC + 1):
                    gain_n = gain[:, n, :] if n < DC else None
                    nc.vector.tensor_scalar(hp[:], freq[:, n:n + 1] if n < DC else theta[:], TWO_PI, None, ALU.mult)
                    dve.drain()
                    nc.vector.tensor_scalar(rest[:], qf[:, 0, :], hp[:], None, ALU.mult)
                    dve.drain()
                    nc.vector.tensor_scalar(angle[:], rest[:], 0.01,
                                            phase[:, n:n + 1] if n < DC else 0.0, ALU.mult, ALU.add)
                    dve.drain()
                    nc.vector.tensor_scalar(turns[:], angle[:], 1.0 / TWO_PI, 0.25, ALU.mult, ALU.add)
                    dve.drain()
                    nc.vector.tensor_scalar(turns[:], turns[:], MAGIC, None, ALU.add)
                    dve.drain()
                    nc.vector.tensor_scalar(turns[:], turns[:], MAGIC, None, ALU.subtract)
                    dve.drain()
                    for pp in PI_PARTS:
                        nc.vector.scalar_tensor_tensor(out=angle[:], in0=turns[:], scalar=-pp, in1=angle[:],
                                                       op0=ALU.mult, op1=ALU.add)
                        dve.drain()
                    nc.vector.tensor_scalar(rest[:], angle[:], pi / 2, 3.1415925, ALU.add, ALU.min)
                    dve.drain()
                    nc.vector.tensor_scalar(rest[:], rest[:], -3.1415925, None, ALU.max).then_inc(gain_phase, 1)
                    dve.wait_ge(gain_sin, n + 1)
                    if n < DC:
                        nc.vector.tensor_scalar(gain_n, work[:, 0, :], 0.3, 0.5, ALU.mult, ALU.add)
                        dve.drain()
                    else:
                        for c in range(DC):
                            nc.vector.scalar_tensor_tensor(out=gain[:, c, :], in0=work[:, 0, :], scalar=0.2,
                                                           in1=gain[:, c, :], op0=ALU.mult, op1=ALU.add)
                        dve.drain()

            def split(b, n, src):
                part_slot_free(dve, b, n)
                p0, p1, p2 = (part[:, n % 2, i, :] for i in range(3))
                nc.vector.tensor_copy(p0, src)
                dve.drain()
                nc.vector.tensor_tensor(rest[:], src, p0, ALU.subtract)
                dve.drain()
                nc.vector.tensor_copy(p1, rest[:])
                dve.drain()
                nc.vector.tensor_tensor(p2, rest[:], p1, ALU.subtract)
                dve.drain().then_inc(part_full, 1)

            def convolve(b, i):
                for j in range(4):
                    if j == 0:
                        nc.vector.tensor_scalar(conv[:, i], xt[:, :, 0:S], taps[:, i, 0:1], None, ALU.mult)
                    else:
                        for c in range(DC):
                            nc.vector.scalar_tensor_tensor(out=conv[:, i, c, :], in0=xt[:, c, j:j + S],
                                                           scalar=taps[:, i, j:j + 1], in1=conv[:, i, c, :],
                                                           op0=ALU.mult, op1=ALU.add)
                    last = dve.drain()
                last.then_inc(conv_full, 1)

            dve.sem_inc(part_full, ONE + 1)
            with dve.Fori(0, B) as b:
                for t in range(TB):
                    if t >= 2:
                        dve.wait_ge(tp_full, ONE + b * TP_N + t // 2 - 1)
                    rows(xrow[:, t % 4, :], b * TB + t).then_inc(row_full, 1)
                if not FANCY:
                    for n in range(4):
                        dve.wait_ge(sc_free, ONE + b * SC_N + n + 2)
                        split(b, n, qf[:, n % 2, :])
                else:
                    dve.wait_ge(tp_free, ONE + b * TP_N + TP_ROWS + 1)
                    convolve(b, 0)
                    convolve(b, 1)
                    for n in range(5):
                        if n < 4:
                            c, which = n // 2, n % 2
                            dve.wait_ge(sc_full, b * SC_N + n + 1)
                            nc.vector.scalar_tensor_tensor(out=qf[:, n % 2, :], in0=sc[:, n % 2, :],
                                                           scalar=(0.25 if which == 0 else 1.0),
                                                           in1=gain[:, c, :], op0=ALU.mult, op1=ALU.mult
                                                           ).then_inc(sc_free, 1)
                            dve.drain()
                            nc.vector.tensor_tensor(work[:, n % 2, :], qf[:, n % 2, :], cos_t[:], ALU.mult)
                        if n == 0:
                            convolve(b, 2)
                        else:
                            k = n - 1
                            dve.wait_ge(sw_full, b * SC_N + k + 1)
                            nc.vector.tensor_tensor(rest[:], sw[:], sin_t[:], ALU.mult).then_inc(sw_free, 1)
                            dve.drain()
                            nc.vector.tensor_tensor(work[:, k % 2, :], work[:, k % 2, :], rest[:], ALU.add)
                            dve.drain()
                            split(b, k, work[:, k % 2, :])



HEADS = B * NH


def slots(eng, lead, unroll, total, emit):
    n = (HEADS - lead) // unroll
    for s in range(lead):
        emit(s, lambda f, s=s: f(s))
    with eng.Fori(0, n) as i:
        for s in range(lead, lead + unroll):
            emit(s, lambda f, s=s: i * (f(s + unroll) - f(s)) + f(s))
    for s in range(lead + n * unroll, total):
        emit(s, lambda f, s=s: f(s))


def live(h):
    return 0 <= h < HEADS


def load_pair(sp, qk_dram, which, dst, at_pair, sem):
    for j, i in enumerate((Q_PART, K_PART)[which]):
        sp.dma_start(dst[j * HD:(j + 1) * HD],
                     qk_dram[which, i, bass.ds(at_pair * 2 * HD, 2 * HD), :].rearrange("(h r) t -> r h t", r=HD)
                     ).then_inc(sem, 16)


def store_pair(sp, o_dram, o, at_pair, sem):
    out_dram, sum_dram = o_dram
    sp.dma_start(sum_dram[bass.ds(at_pair * 2, 2), :].rearrange("(a h) t -> a h t", a=1), o[HD:VH]).then_inc(sem, 16)
    for h in range(2):
        sp.dma_start(out_dram[bass.ds(at_pair * 2 * HD + h * HD, HD), :], o[0:HD, h, :]).then_inc(sem, 16)


def softmax_heads(core, name, qk_dram, v_dram, o_dram, *, causal):
    nc = core.nc
    LEAD, UNROLL, PAIRS = 2, 6, 3
    TOTAL = HEADS + LEAD
    MROW = QK_ROWS
    with Stage(core, name) as st:
        qs = st.sb("qs", [QK_ROWS + 3, 2 * PAIRS, S], BF16)
        ks = st.sb("ks", [QK_ROWS + 3, 2 * PAIRS, S], BF16)
        v = st.sb("v", [P, PAIRS, 2, TB * VH])
        pt = st.sb("pt", [P, 4, 512])
        o = st.sb("o", [VH, 2 * PAIRS, S])
        nmax = st.sb("nmax", [P, 2, TB])
        mrest = st.sb("mrest", [P, TB])
        mpart = st.sb("mpart", [P, 2, TB, P], BF16)
        sc = st.ps("sc", [P, 2, S])
        sct = st.ps("sct", [P, 2, 512])
        ov = st.ps("ov", [VH, 2, 512])

        qk_in = [st.sem(f"qk_in{i}") for i in range(PAIRS)]
        full, free = [st.sem("full0"), st.sem("full1")], [st.sem("free0"), st.sem("free1")]
        mpart_full, mrow_full = st.sem("mpart_full"), st.sem("mrow_full")
        sct_full, pt_full, pt_used = st.sem("sct_full"), st.sem("pt_full"), st.sem("pt_used")
        ov_free = st.sem("ov_free")
        o_out = [st.sem(f"o_out{i}") for i in range(PAIRS)]
        const = st.sem("const")
        block = st.block()

        MID = 4
        fills = []
        for s in range(TOTAL):
            for t in range(TB):
                if live(s):
                    fills.append(("max", s, t))
                if t == MID - 1 and live(s - 1):
                    fills.append(("row", s - 1))
        place = {f: n for n, f in enumerate(fills)}

        def before(key):
            return place[key] // 2

        halves = [0, 1] if causal else [1, 0]
        chunks = []
        for half in halves:
            lo, hi = 4 * half, 4 * half + 4
            for kb in (range(0, hi) if causal else range(TB - 1, lo - 1, -1)):
                q0, q1 = (max(kb, lo), hi) if causal else (lo, min(kb + 1, hi))
                chunks.append((kb, q0, q1 - q0))
        HALF_AT = 4
        assert chunks[0][2] == chunks[HALF_AT][2] == 4
        NCH = len(chunks)
        tile_of = [round((j + 1) * TB / (NCH + 1)) for j in range(NCH)]
        ROW_AT = sum(t < MID for t in tile_of)

        @block.sync
        def _(sp):
            for sem in o_out:
                sp.sem_inc(sem, ONE)

            def emit(p, at):
                slot = p % PAIRS
                if p >= PAIRS:
                    sp.wait_ge(ov_free, at(lambda p: ONE + 4 * (p - PAIRS) + 4))
                    store_pair(sp, o_dram, o[:, 2 * slot:2 * slot + 2, :], at(lambda p: p - PAIRS), o_out[slot])
                if p < HEADS // 2:
                    load_pair(sp, qk_dram, 0, qs[:, 2 * slot:2 * slot + 2, :], at(lambda p: p), qk_in[slot])
                    load_pair(sp, qk_dram, 1, ks[:, 2 * slot:2 * slot + 2, :], at(lambda p: p), qk_in[slot])
                    sp.dma_start(v[:, slot], v_dram[bass.ds(at(lambda p: p) * 2, 2), :, :].rearrange("h p e -> p h e")
                                 ).then_inc(qk_in[slot], 16)

            pairs(sp, PAIRS, PAIRS, emit)
            for slot in range(PAIRS):
                sp.wait_ge(o_out[slot], ONE + 48 * len(range(slot, HEADS // 2, PAIRS)))

        @block.gpsimd
        def _(pool):
            nc.gpsimd.memset(mpart[:], 0.0).then_inc(const, 1)
            pool.drain()
            nc.gpsimd.memset(ks[MROW:MROW + 3, :, :], 1.0).then_inc(const, 1)

        @block.tensor
        def _(pe):
            pe.sem_inc(pt_used, ONE + 3)
            pe.wait_ge(const, 2)

            def emit(s, at):
                def maxima(t):
                    n = place["max", s, t]
                    pe.wait_ge(free[n % 2], at(lambda s: ONE + before(("max", s, t))))
                    k0, k1 = (0, t + 1) if causal else (t, TB)
                    w, diag = (k1 - k0) * P, (t - k0) * P
                    for lo in range(0, w, 512):
                        hi = min(w, lo + 512)
                        has = lo <= diag < hi
                        last = nc.tensor.matmul(sc[:, n % 2, lo:hi], qs[0:QK_ROWS, s % 6, t * P:(t + 1) * P],
                                                ks[0:QK_ROWS, s % 6, k0 * P + lo:k0 * P + hi], start=True, stop=not has)
                        if has:
                            last = nc.tensor.matmul(sc[:, n % 2, diag:diag + P], core.ident_bf[:],
                                                    (core.above if causal else core.below)[:], start=False, stop=True)
                    last.then_inc(full[n % 2], 1)

                def maximum_row():
                    n = place["row", s - 1]
                    pe.wait_ge(free[n % 2], at(lambda s: ONE + before(("row", s - 1))))
                    pe.wait_ge(mpart_full, at(lambda s: s))
                    for t in range(TB):
                        last = nc.tensor.matmul(sc[:, n % 2, t * P:(t + 1) * P], mpart[:, (s - 1) % 2, t, :],
                                                core.ident_bf[:], start=True, stop=True)
                    last.then_inc(full[n % 2], 1)

                def transposed(j):
                    kb, q, nb = chunks[j]
                    h = (s - 2) % 6
                    if j >= 2:
                        pe.wait_ge(pt_full, at(lambda s: (s - 2) * NCH + j - 1))
                    has = q <= kb < q + nb
                    last = nc.tensor.matmul(sct[:, j % 2, 0:nb * P], ks[:, h, kb * P:(kb + 1) * P],
                                            qs[:, h, q * P:(q + nb) * P], start=True, stop=not has)
                    if has:
                        d = (kb - q) * P
                        last = nc.tensor.matmul(sct[:, j % 2, d:d + P], core.ident_bf[:],
                                                (core.below if causal else core.above)[:], start=False, stop=True)
                    last.then_inc(sct_full, 1)

                def values(j):
                    kb, q, nb = chunks[j]
                    h, half = s - 2, chunks[j][1] // 4
                    first = j in (0, HALF_AT)
                    if first:
                        pe.wait_ge(ov_free, at(lambda s: ONE + 2 * (s - 2) - (j == 0)) if s > 2 else ONE)
                    pe.wait_ge(pt_full, at(lambda s: (s - 2) * NCH + j + 1))
                    last = nc.tensor.matmul(ov[:, half, (q % 4) * P:(q % 4 + nb) * P],
                                            v[:, h // 2 % PAIRS, h % 2, kb * VH:(kb + 1) * VH], pt[:, j % 4, 0:nb * P],
                                            start=first, stop=j in (HALF_AT - 1, NCH - 1))
                    last.then_inc(pt_used, 1)

                if live(s) and s % 2 == 0:
                    pe.wait_ge(qk_in[s // 2 % PAIRS], at(lambda s: (s // 2 // PAIRS + 1) * 13 * 16))
                if live(s - 2):
                    pe.wait_ge(mrow_full, at(lambda s: s - 1))
                for t in range(TB + 1):
                    if t < TB and live(s):
                        maxima(t)
                    if t == MID - 1 and live(s - 1):
                        maximum_row()
                    if live(s - 2):
                        for j in (j for j in range(NCH) if tile_of[j] == t):
                            transposed(j)
                            if j >= 2:
                                values(j - 2)
                if live(s - 2):
                    values(NCH - 2)
                    values(NCH - 1)

            slots(pe, LEAD, UNROLL, TOTAL, emit)

        @block.scalar
        def _(act):
            def emit(s, at):
                def half_out(which, h, head):
                    half = halves[which]
                    done = (HALF_AT, NCH)[which]
                    act.wait_ge(pt_used, at(lambda s: ONE + 3 + head(s) * NCH + done))
                    if which == 0:
                        act.wait_ge(o_out[h // 2 % PAIRS], at(lambda s: ONE + head(s) // 2 // PAIRS * 48))
                    nc.scalar.activation(o[:, h % 6, half * 512:(half + 1) * 512], ov[:, half, :],
                                         ACT.Copy).then_inc(ov_free, 1)

                for j in range(NCH):
                    if j == ROW_AT and live(s - 1):
                        n = place["row", s - 1]
                        act.wait_ge(full[n % 2], at(lambda s: before(("row", s - 1)) + 1))
                        nc.scalar.activation(qs[MROW:MROW + 3, (s - 1) % 6, :], sc[MROW:MROW + 3, n % 2, :],
                                             ACT.Copy).then_inc(free[n % 2], 1)
                        act.drain().then_inc(mrow_full, 1)
                    if j == 2 and live(s - 3):
                        half_out(1, s - 3, lambda s: s - 3)
                    if j == HALF_AT + 3 and live(s - 2):
                        half_out(0, s - 2, lambda s: s - 2)
                    if live(s - 2):
                        act.wait_ge(sct_full, at(lambda s: (s - 2) * NCH + j + 1))
                        act.wait_ge(pt_used, at(lambda s: ONE + (s - 2) * NCH + j))
                        nb = chunks[j][2]
                        nc.scalar.activation(pt[:, j % 4, 0:nb * P], sct[:, j % 2, 0:nb * P], ACT.Exp).then_inc(pt_full, 1)

            act.sem_inc(ov_free, ONE)
            slots(act, 3, UNROLL, HEADS + 3, emit)

        @block.vector
        def _(dve):
            dve.sem_inc(free[0], ONE)
            dve.sem_inc(free[1], ONE)
            dve.wait_ge(const, 2)

            def emit(s, at):
                for t in range(TB):
                    if live(s):
                        n = place["max", s, t]
                        k0, k1 = (0, t + 1) if causal else (t, TB)
                        dve.wait_ge(full[n % 2], at(lambda s: before(("max", s, t)) + 1))
                        nc.vector.tensor_reduce(nmax[:, s % 2, t:t + 1], sc[:, n % 2, 0:(k1 - k0) * P], AX.X, ALU.max,
                                                negate=True).then_inc(free[n % 2], 1)
                if live(s):
                    cols = [mpart[:, s % 2, :, MROW + i] for i in range(3)]
                    dve.drain()
                    nc.vector.tensor_copy(cols[0], nmax[:, s % 2, :])
                    dve.drain()
                    nc.vector.tensor_tensor(mrest[:], nmax[:, s % 2, :], cols[0], ALU.subtract)
                    dve.drain()
                    nc.vector.tensor_copy(cols[1], mrest[:])
                    dve.drain()
                    nc.vector.tensor_tensor(cols[2], mrest[:], cols[1], ALU.subtract).then_inc(mpart_full, 1)

            slots(dve, LEAD, UNROLL, TOTAL, emit)


def pairs(eng, lead, unroll, emit):
    n = (HEADS // 2 - lead) // unroll
    for p in range(lead):
        emit(p, lambda f, p=p: f(p))
    with eng.Fori(0, n) as i:
        for p in range(lead, lead + unroll):
            emit(p, lambda f, p=p: i * (f(p + unroll) - f(p)) + f(p))
    for p in range(lead + n * unroll, HEADS // 2 + lead):
        emit(p, lambda f, p=p: f(p))


def project_out(core, name, wout_dram, o_dram, *, target, out_bias=None):
    nc = core.nc
    out_dram, sum_dram = o_dram
    with Stage(core, name) as st:
        wout = st.sb("wout", [P, DC, D])
        ot = st.sb("ot", [P, 2, DC, S])
        inverse = st.sb("inverse", [P, 2, DC, S])
        half_sums = st.sb("half_sums", [P, S // 2])
        if out_bias is not None:
            bo = st.sb("bo", [1, D])
        y = st.ps("y", [P, 4, 512])
        w_in = st.sem("w_in")
        o_in = [st.sem("o_in0"), st.sem("o_in1")]
        ot_full, y_full, y_used = st.sem("ot_full"), st.sem("y_full"), st.sem("y_used")
        sums_in, inverse_full, inverse_out = st.sem("sums_in"), st.sem("inverse_full"), st.sem("inverse_out")
        block = st.block()

        @block.sync
        def _(sp):
            by_half = sum_dram.rearrange("h (a t) -> (h a) t", a=2)
            sp.dma_start(half_sums[:], by_half).then_inc(sums_in, 16)
            sp.dma_start(wout[:], wout_dram.rearrange("(c p) n -> p c n", p=P)).then_inc(w_in, 16)
            if out_bias is not None:
                sp.dma_start(bo[:], out_bias.rearrange("(a n) -> a n", a=1)).then_inc(w_in, 16)
            sp.wait_ge(inverse_full, 1)
            sp.dma_start(by_half, half_sums[:]).then_inc(inverse_out, 16)
            sp.wait_ge(inverse_out, 16)
            for b in range(B):
                if b >= 2:
                    sp.wait_ge(y_full, (b - 1) * TB // 2)
                sp.dma_start(ot[:, b % 2], out_dram[b * D:(b + 1) * D, :].rearrange("(c p) t -> p c t", p=P)
                             ).then_inc(o_in[b % 2], 16)
                for c in range(DC):
                    for h in range(HC):
                        sp.dma_start(inverse[h * HD:(h + 1) * HD, b % 2, c, :],
                                     sum_dram[b * NH + c * HC + h, :].partition_broadcast(HD)).then_inc(o_in[b % 2], 16)

        @block.vector
        def _(dve):
            def normalise(b):
                dve.wait_ge(o_in[b % 2], (b // 2 + 1) * 16 * (1 + NH))
                for c in range(DC):
                    nc.vector.tensor_tensor(ot[:, b % 2, c, :], ot[:, b % 2, c, :], inverse[:, b % 2, c, :], ALU.mult)
                dve.drain().then_inc(ot_full, 1)

            dve.wait_ge(sums_in, 16)
            nc.vector.reciprocal(half_sums[:], half_sums[:]).then_inc(inverse_full, 1)
            normalise(0)
            for b in range(B):
                if b + 1 < B:
                    normalise(b + 1)
                for i in range(b * TB // 2, (b + 1) * TB // 2):
                    dve.wait_ge(y_full, i + 1)
                    tv = target[:, 2 * i:2 * i + 2, :]
                    nc.vector.tensor_tensor(tv, y[:, i % 4, :].rearrange("p (t d) -> p t d", t=2), tv,
                                            ALU.add).then_inc(y_used, 1)

        @block.tensor
        def _(pe):
            pe.wait_ge(w_in, 16 * (1 + (out_bias is not None)))
            for b in range(B):
                pe.wait_ge(ot_full, b + 1)
                for k in range(TB // 2):
                    i = b * TB // 2 + k
                    if i >= 4:
                        pe.wait_ge(y_used, i - 3)
                    for t in range(2):
                        dst = y[:, i % 4, t * D:(t + 1) * D]
                        for c in range(DC):
                            last = nc.tensor.matmul(dst, ot[:, b % 2, c, (2 * k + t) * P:(2 * k + t + 1) * P], wout[:, c, :],
                                                    start=(c == 0), stop=(c == DC - 1 and out_bias is None))
                        if out_bias is not None:
                            last = nc.tensor.matmul(dst, core.ones[:], bo[:], start=False, stop=True)
                    last.then_inc(y_full, 1)



LO, HI = TOPK - 8, TOPK
AIM = (LO + HI) // 2
ROUNDS = 4
SPAN = 1024.0
BUSY = TB - 1


def sampled(t):
    return 0, t * P, t


def topk_heads(core, name, qk_dram, v_dram, o_dram, tables):
    nc = core.nc
    LEAD, UNROLL, PAIRS = 4, 4, 2
    TOTAL = HEADS + LEAD
    OFF = [P * t * (t + 1) // 2 for t in range(TB + 1)]
    order = list(range(1, TB)) + [0]
    with Stage(core, name) as st:
        qs = st.sb("qs", [QK_ROWS, 2 * PAIRS, S], BF16)
        ks = st.sb("ks", [QK_ROWS, 2 * PAIRS, S], BF16)
        v = st.sb("v", [P, PAIRS, 2, TB * VH])
        scores = st.sb("scores", [P, 4, OFF[TB]])
        e = st.sb("e", [P, OFF[TB]])
        pt = st.sb("pt", [P, 4, 512])
        o = st.sb("o", [VH, 2 * PAIRS, S])
        rest = st.sb("rest", [P, 2, S])
        rest0 = st.sb("rest0", [P, P])
        top8 = st.sb("top8", [P, 8])
        top0 = st.sb("top0", [P, 2, 8])
        largest = st.sb("largest", [P, 4, TB])
        nmax = st.sb("nmax", [P, 4, TB])
        kth = st.sb("kth", [P, TB])
        minus_one = st.sb("minus_one", [P, TB])
        tab = st.sb("tab", [P, 4, BUSY])
        minus_half, half = st.sb("minus_half", [P, BUSY]), st.sb("half", [P, BUSY])
        above = st.sb("above", [P, OFF[TB] - P], BF16)
        signs = st.sb("signs", [P, OFF[TB] - P], BF16)
        stats = st.sb("stats", [P, 4, BUSY, 6])
        at_now = st.sb("at_now", [P, 4, 2, BUSY])
        bracket = st.sb("bracket", [P, 4, 2, 2, BUSY])
        reach = st.sb("reach", [P, 4, 2, 2, BUSY])
        signed = st.sb("signed", [P, 4, BUSY])
        count = st.sb("count", [P, 4, BUSY])
        below = st.sb("below", [P, 4, BUSY, 9])
        rank = st.sb("rank", [P, 9])
        picked = st.sb("picked", [P, BUSY, 9])
        side = st.sb("side", [P, 2, 1, BUSY])
        diff = st.sb("diff", [P, 2, 2, BUSY])
        gap = st.sb("gap", [P, 2, BUSY])
        step = st.sb("step", [P, 2, BUSY])
        far = st.sb("far", [P, BUSY])
        bad = st.sb("bad", [P, TB])
        bad_head = st.sb("bad_head", [1, TB], mybir.dt.int32)
        ones_col = st.sb("ones_col", [P, 1])
        sc = st.ps("sc", [P, 2, S])
        tp = st.ps("tp", [P, 2, 512])
        ov = st.ps("ov", [VH, 2, 512])

        qk_in = [st.sem(f"qk_in{i}") for i in range(PAIRS)]
        v_in = [st.sem(f"v_in{i}") for i in range(PAIRS)]
        tab_in, ones_set = st.sem("tab_in"), st.sem("ones_set")
        sc_full, sc_free = st.sem("sc_full"), st.sem("sc_free")
        head_full, nmax_full = st.sem("head_full"), st.sem("nmax_full")
        guessed = [st.sem(f"guessed{r}") for r in range(ROUNDS + 1)]
        counted = [st.sem(f"counted{r}") for r in range(ROUNDS)]
        bad_full = st.sem("bad_full")
        e_full, e_cut = st.sem("e_full"), st.sem("e_cut")
        tp_full, tp_free, pt_used, ov_free = (st.sem(n) for n in ("tp_full", "tp_free", "pt_used", "ov_free"))
        o_out = [st.sem(f"o_out{i}") for i in range(PAIRS)]
        block = st.block()

        fills = []
        for s in range(HEADS + 3):
            fills += [("tile", s, t) for t in range(TB) if live(s)] + [("bad", s - 3)] * live(s - 3)
        place = {f: n for n, f in enumerate(fills)}

        chunks = [(t, k, min(4, t + 1 - k)) for t in order for k in range(0, t + 1, 4)]
        NCH = len(chunks)
        chunks_of = [[j for j, c in enumerate(chunks) if c[0] == t] for t in order]
        done_at = {1: chunks_of[TB - 2][-1], 0: chunks_of[TB - 1][-1]}

        @block.sync
        def _(sp):
            sp.dma_start(tab[:], tables["quantiles"].rearrange("a p t -> p a t")).then_inc(tab_in, 16)
            sp.dma_start(rank[:], tables["ranks"].partition_broadcast(P)).then_inc(tab_in, 16)
            for sem in o_out:
                sp.sem_inc(sem, ONE)

            def emit(p, at):
                slot = p % PAIRS
                if p < HEADS // 2:
                    if p >= PAIRS:
                        sp.wait_ge(sc_full, at(lambda p: place["tile", 2 * (p - PAIRS) + 1, TB - 1] + 1))
                    load_pair(sp, qk_dram, 0, qs[:, 2 * slot:2 * slot + 2, :], at(lambda p: p), qk_in[slot])
                    load_pair(sp, qk_dram, 1, ks[:, 2 * slot:2 * slot + 2, :], at(lambda p: p), qk_in[slot])
                if p >= PAIRS + 1:
                    sp.wait_ge(ov_free, at(lambda p: ONE + 4 * (p - PAIRS - 1) + 4))
                    old = (p - PAIRS - 1) % PAIRS
                    store_pair(sp, o_dram, o[:, 2 * old:2 * old + 2, :], at(lambda p: p - PAIRS - 1), o_out[old])
                if 1 <= p <= HEADS // 2:
                    sp.dma_start(v[:, (p - 1) % PAIRS],
                                 v_dram[bass.ds(at(lambda p: p - 1) * 2, 2), :, :].rearrange("h p e -> p h e")
                                 ).then_inc(v_in[(p - 1) % PAIRS], 16)

            pairs(sp, PAIRS + 1, PAIRS, emit)
            for slot in range(PAIRS):
                sp.wait_ge(o_out[slot], ONE + 48 * (HEADS // 2 // PAIRS))

        @block.tensor
        def _(pe):
            pe.sem_inc(pt_used, ONE + 3)
            pe.sem_inc(tp_full, ONE)
            pe.wait_ge(ones_set, 1)

            def emit(s, at):
                h = s - 4

                def score_tile(t):
                    if t == 0 and s % 2 == 0:
                        pe.wait_ge(qk_in[s // 2 % PAIRS], at(lambda s: (s // 2 // PAIRS + 1) * 12 * 16))
                    n = place["tile", s, t]
                    pe.wait_ge(sc_free, at(lambda s: ONE + place["tile", s, t]))
                    w, diag = (t + 1) * P, t * P
                    for lo in range(0, w, 512):
                        hi = min(w, lo + 512)
                        has = lo <= diag < hi
                        last = nc.tensor.matmul(sc[:, n % 2, lo:hi], qs[:, s % 4, t * P:(t + 1) * P],
                                                ks[:, s % 4, lo:hi], start=True, stop=not has)
                        if has:
                            last = nc.tensor.matmul(sc[:, n % 2, diag:diag + P], core.ident_bf[:], core.above[:],
                                                    start=False, stop=True)
                    last.then_inc(sc_full, 1)

                def transposes(i):
                    pe.wait_ge(e_cut, at(lambda s: (s - 4) * TB + i + 1))
                    for j in chunks_of[i]:
                        t, k0, nb = chunks[j]
                        pe.wait_ge(tp_free, at(lambda s: ONE + (s - 4) * NCH + j))
                        for m in range(nb):
                            k = OFF[t] + (k0 + m) * P
                            last = nc.tensor.transpose(tp[:, j % 2, m * P:(m + 1) * P], e[:, k:k + P], core.ident[:])
                        last.then_inc(tp_full, 1)

                def values(i):
                    if i == 0 and h % 2 == 0:
                        pe.wait_ge(v_in[h // 2 % PAIRS], at(lambda s: ((s - 4) // 2 // PAIRS + 1) * 16))
                    for j in chunks_of[i]:
                        t, k0, nb = chunks[j]
                        half = t // 4
                        if i == 0 or (i == 3 and k0 == 0):
                            pe.wait_ge(ov_free, at(lambda s: ONE + 2 * (s - 4) - (i == 3 and s > 4)))
                        pe.wait_ge(tp_free, at(lambda s: ONE + (s - 4) * NCH + j + 2))
                        for m in range(nb):
                            kb = k0 + m
                            last = nc.tensor.matmul(ov[:, half, (t % 4) * P:(t % 4 + 1) * P],
                                                    v[:, h // 2 % PAIRS, h % 2, kb * VH:(kb + 1) * VH],
                                                    pt[:, j % 4, m * P:(m + 1) * P], start=(kb == 0), stop=(kb == t))
                        last.then_inc(pt_used, 1)

                if live(s):
                    for t in range(TB):
                        score_tile(t)
                if live(h):
                    for i in range(TB):
                        transposes(i)
                        if i:
                            values(i - 1)
                    values(TB - 1)
                if live(s - 3):
                    n = place["bad", s - 3]
                    pe.wait_ge(sc_free, at(lambda s: ONE + place["bad", s - 3]))
                    pe.wait_ge(bad_full, at(lambda s: s - 2))
                    nc.tensor.matmul(sc[0:1, n % 2, 0:TB], ones_col[:], bad[:], start=True, stop=True).then_inc(sc_full, 1)

            slots(pe, LEAD, UNROLL, TOTAL, emit)

        @block.scalar
        def _(act):
            act.sem_inc(tp_free, ONE + 1)
            act.sem_inc(ov_free, ONE)

            def emit(s, at):
                def counts(r, h, head):
                    def tile(i):
                        if i == 0:
                            act.drain()
                            act.wait_ge(guessed[r], at(lambda s: head(s) + 1))
                        t = i + 1
                        last = nc.scalar.activation(signs[:, OFF[t] - P:OFF[t + 1] - P], scores[:, h % 4, OFF[t]:OFF[t + 1]],
                                                    ACT.Sign, bias=at_now[:, h % 4, 0, i:i + 1], scale=-1.0,
                                                    accum_out=signed[:, h % 4, i:i + 1])
                        if i == BUSY - 1:
                            last.then_inc(counted[r], 1)
                    return [(tile, i) for i in range(BUSY)] if live(h) else []

                def exponentials(i):
                    t = order[i]
                    if i == 0:
                        act.wait_ge(nmax_full, at(lambda s: s - 2))
                    if s > 3:
                        act.wait_ge(tp_full, at(lambda s: ONE + (s - 4) * NCH + chunks_of[i][-1] + 1))
                    nc.scalar.activation(e[:, OFF[t]:OFF[t + 1]], scores[:, (s - 3) % 4, OFF[t]:OFF[t + 1]],
                                         ACT.Exp, bias=nmax[:, (s - 3) % 4, t:t + 1]).then_inc(e_full, 1)

                def copy(j):
                    nb = chunks[j][2]
                    act.wait_ge(tp_full, at(lambda s: ONE + (s - 4) * NCH + j + 1))
                    act.wait_ge(pt_used, at(lambda s: ONE + (s - 4) * NCH + j))
                    nc.scalar.activation(pt[:, j % 4, 0:nb * P], tp[:, j % 2, 0:nb * P], ACT.Copy).then_inc(tp_free, 1)

                def half_out(half):
                    h = s - 4
                    act.wait_ge(pt_used, at(lambda s: ONE + 3 + (s - 4) * NCH + done_at[half] + 1))
                    if half == 1:
                        act.wait_ge(o_out[h // 2 % PAIRS], at(lambda s: ONE + (s - 4) // 2 // PAIRS * 48))
                    nc.scalar.activation(o[:, h % 4, half * 512:(half + 1) * 512], ov[:, half, :],
                                         ACT.Copy).then_inc(ov_free, 1)

                def run(steps):
                    for f, i in steps:
                        f(i)

                run(counts(0, s - 1, lambda s: s - 1))
                c2 = counts(2, s - 2, lambda s: s - 2)
                for j in range(NCH):
                    if live(s - 4):
                        copy(j)
                    run(c2[j * BUSY // NCH:(j + 1) * BUSY // NCH])
                c1 = counts(1, s - 1, lambda s: s - 1)
                run(c1[:1])
                if live(s - 4):
                    half_out(1)
                    half_out(0)
                run(c1[1:])
                for i in range(TB):
                    if live(s - 3):
                        exponentials(i)
                run(counts(3, s - 2, lambda s: s - 2))

            slots(act, LEAD, UNROLL, TOTAL, emit)

        @block.gpsimd
        def _(pool):
            g = nc.gpsimd
            g.memset(minus_one[:], -1.0)
            g.memset(minus_half[:], -0.5)
            g.memset(half[:], 0.5)
            for i, sign in enumerate((1.0, -1.0)):
                g.memset(reach[:, :, i, 1, :], sign * SPAN)
            g.memset(ones_col[:], 1.0)
            pool.drain().then_inc(ones_set, 1)
            pool.wait_ge(tab_in, 32)

            def emit(s, at):
                def correct(r, h, head):
                    if not live(h):
                        return
                    h4 = h % 4
                    now, br = at_now[:, h4], bracket[:, h4]
                    pool.wait_ge(counted[r], at(lambda s: head(s) + 1))
                    g.tensor_tensor(now[:, 1, :], signed[:, h4, :], minus_half[:], ALU.mult)
                    pool.drain()
                    g.tensor_tensor(now[:, 1, :], now[:, 1, :], tab[:, 2, :], ALU.add)
                    pool.drain()
                    both = now.rearrange("p (a b) t -> p a b t", a=1).to_broadcast([P, 2, 2, BUSY])
                    g.tensor_scalar(side[:, 0, 0, :], now[:, 1, :], 0.0, None, ALU.is_ge)
                    g.tensor_scalar(side[:, 1, 0, :], now[:, 1, :], 0.0, None, ALU.is_lt)
                    if r == 0:
                        g.tensor_tensor(br, both, reach[:, h4], ALU.add)
                        pool.drain()
                    g.tensor_tensor(diff[:], both, br, ALU.subtract)
                    pool.drain()
                    g.tensor_tensor(diff[:], diff[:], side[:].to_broadcast([P, 2, 2, BUSY]), ALU.mult)
                    pool.drain()
                    g.tensor_tensor(br, br, diff[:], ALU.add)
                    pool.drain()
                    g.tensor_tensor(gap[:], br[:, 0], br[:, 1], ALU.subtract)
                    g.tensor_tensor(step[:, 1, :], now[:, 1, :], now[:, 1, :], ALU.mult)
                    pool.drain()
                    g.tensor_tensor(step[:, 0, :], gap[:, 1, :], minus_one[:, 0:BUSY], ALU.pow)
                    g.tensor_scalar(step[:, 1, :], step[:, 1, :], (HI - AIM + 0.25) ** 2, None, ALU.is_gt)
                    pool.drain()
                    g.tensor_tensor(step[:, 0, :], step[:, 0, :], br[:, 0, 1, :], ALU.mult)
                    pool.drain()
                    g.tensor_tensor(step[:, 0, :], step[:, 0, :], gap[:, 0, :], ALU.mult)
                    pool.drain()
                    g.tensor_tensor(step[:, 0, :], br[:, 0, 0, :], step[:, 0, :], ALU.subtract)
                    pool.drain()
                    g.tensor_tensor(step[:, 0, :], step[:, 0, :], now[:, 0, :], ALU.subtract)
                    pool.drain()
                    g.tensor_tensor(step[:, 0, :], step[:, 0, :], step[:, 1, :], ALU.mult)
                    pool.drain()
                    g.tensor_tensor(now[:, 0, :], now[:, 0, :], step[:, 0, :], ALU.add)
                    pool.drain()
                    if r == ROUNDS - 1:
                        g.tensor_copy(below[:, h4, :, 8], now[:, 0, :]).then_inc(guessed[r + 1], 1)
                    else:
                        pool.drain().then_inc(guessed[r + 1], 1)

                if live(s):
                    pool.wait_ge(head_full, at(lambda s: s + 1))
                    g.tensor_tensor(nmax[:, s % 4, :], largest[:, s % 4, :], minus_one[:], ALU.mult).then_inc(nmax_full, 1)
                    h4 = s % 4
                    now, part = at_now[:, h4], stats[:, s % 4]
                    g.tensor_tensor(now[:, 0, :], part[:, :, 1], part[:, :, 4], ALU.add)
                    g.tensor_tensor(step[:, 0, :], part[:, :, 2], part[:, :, 5], ALU.add)
                    pool.drain()
                    g.tensor_scalar(now[:, 0, :], now[:, 0, :], 0.5, None, ALU.mult)
                    g.tensor_tensor(step[:, 0, :], step[:, 0, :], tab[:, 3, :], ALU.mult)
                    pool.drain()
                    spread = step[:, 1, :]
                    g.tensor_tensor(spread, step[:, 0, :], half[:], ALU.pow)
                    pool.drain()
                    g.tensor_tensor(step[:, 0, :], spread, tab[:, 0, :], ALU.mult)
                    g.tensor_tensor(reach[:, h4, 1, 0, :], spread, tab[:, 1, :], ALU.mult)
                    pool.drain()
                    g.tensor_tensor(now[:, 0, :], now[:, 0, :], step[:, 0, :], ALU.add)
                    g.tensor_scalar(reach[:, h4, 0, 0, :], reach[:, h4, 1, 0, :], -1.0, None, ALU.mult)
                    pool.drain().then_inc(guessed[0], 1)
                correct(0, s - 1, lambda s: s - 1)
                correct(2, s - 2, lambda s: s - 2)
                correct(1, s - 1, lambda s: s - 1)
                correct(3, s - 2, lambda s: s - 2)

            slots(pool, LEAD, UNROLL, TOTAL, emit)

        @block.vector
        def _(dve):
            dve.sem_inc(sc_free, ONE + 1)

            def emit(s, at):
                if live(s):
                    dve.drain()
                    for t in range(TB):
                        n = place["tile", s, t]
                        dve.wait_ge(sc_full, at(lambda s: place["tile", s, t] + 1))
                        nc.vector.tensor_scalar(scores[:, s % 4, OFF[t]:OFF[t + 1]], sc[:, n % 2, 0:(t + 1) * P], 0.0,
                                                None, ALU.add, ALU.max,
                                                accum_out=largest[:, s % 4, t:t + 1]).then_inc(sc_free, 1)
                    dve.drain()
                    for i in range(BUSY):
                        lo, hi, by = sampled(i + 1)
                        nc.vector.bn_stats(stats[:, s % 4, i, :], scores[:, s % 4, OFF[i + 1] + lo:OFF[i + 1] + hi:by])
                    dve.drain().then_inc(head_full, 1)
                if not live(s - 3):
                    return
                h4 = (s - 3) % 4

                def tile(t):
                    return scores[:, h4, OFF[t]:OFF[t + 1]]

                SMALL = P + 1 - TOPK
                R0 = (SMALL + 7) // 8

                def first_tile_max(r):
                    nc.vector.max(top0[:, r % 2, :], rest0[:])

                def first_tile_next(r):
                    if r < R0 - 1:
                        nc.vector.match_replace(rest0[:], top0[:, r % 2, :], rest0[:], GONE)
                    else:
                        k = (SMALL - 1) % 8
                        nc.vector.tensor_scalar(kth[:, 0:1], top0[:, r % 2, k:k + 1], -1.0, None, ALU.mult)

                nc.vector.tensor_scalar(rest0[:], tile(0), -1.0, None, ALU.mult)
                dve.wait_ge(guessed[ROUNDS], at(lambda s: s - 2))
                for i in range(BUSY):
                    t = i + 1
                    nc.vector.tensor_scalar(above[:, OFF[t] - P:OFF[t + 1] - P], tile(t), below[:, h4, i, 8:9], 0.0,
                                            ALU.is_ge, ALU.add, accum_out=count[:, h4, i:i + 1])
                dve.drain()
                nc.vector.tensor_scalar(far[:], count[:, h4, :], float(-AIM), None, ALU.add)
                first_tile_max(0)
                dve.drain()
                nc.vector.tensor_tensor(far[:], far[:], far[:], ALU.mult)
                first_tile_next(0)
                dve.drain()
                nc.vector.tensor_scalar(bad[:, 0:BUSY], far[:], (HI - AIM + 0.25) ** 2, 0.0, ALU.is_gt, ALU.add,
                                        accum_out=bad[:, BUSY:TB])
                first_tile_max(1)
                dve.drain().then_inc(bad_full, 1)
                for i in range(BUSY + 1):
                    if i < BUSY:
                        t = i + 1
                        nc.vector.scalar_tensor_tensor(out=rest[:, i % 2, 0:(t + 1) * P], in0=above[:, OFF[t] - P:OFF[t + 1] - P],
                                                       scalar=GONE, in1=tile(t), op0=ALU.mult, op1=ALU.add)
                    if i:
                        nc.vector.max(below[:, h4, i - 1, 0:8], rest[:, (i - 1) % 2, 0:(i + 1) * P])
                    r = 1 + i // 2
                    if r < R0:
                        if i % 2:
                            first_tile_max(r)
                        else:
                            first_tile_next(r)
                    if i == 2:
                        n = place["bad", s - 3]
                        dve.wait_ge(sc_full, at(lambda s: place["bad", s - 3] + 1))
                        nc.vector.tensor_copy(bad_head[:], sc[0:1, n % 2, 0:TB]).then_inc(sc_free, 1)
                    dve.drain()
                for i in range(BUSY):
                    nc.vector.scalar_tensor_tensor(out=picked[:, i, :], in0=rank[:], scalar=count[:, h4, i:i + 1],
                                                   in1=below[:, h4, i, :], op0=ALU.is_equal, op1=ALU.mult,
                                                   accum_out=kth[:, i + 1:i + 2])
                dve.drain()
                any_bad = dve.value_load(bad_head[0:1, BUSY:TB], min_val=0, max_val=P * BUSY)
                with dve.If(any_bad > 0):
                    for t in range(1, TB):
                        tile_bad = dve.value_load(bad_head[0:1, t - 1:t], min_val=0, max_val=P)
                        with dve.If(tile_bad > 0):
                            work = rest[:, 0, 0:(t + 1) * P]
                            nc.vector.tensor_copy(work, tile(t))
                            dve.drain()
                            with dve.Fori(0, (TOPK - 1) // 8):
                                nc.vector.max(top8[:], work)
                                dve.drain()
                                nc.vector.match_replace(work, top8[:], work, GONE)
                                dve.drain()
                            nc.vector.max(top8[:], work)
                            dve.drain()
                            k = (TOPK - 1) % 8
                            nc.vector.tensor_copy(kth[:, t:t + 1], top8[:, k:k + 1])
                            dve.drain()
                for i in range(TB):
                    t = order[i]
                    dve.wait_ge(e_full, at(lambda s: (s - 3) * TB + i + 1))
                    nc.vector.scalar_tensor_tensor(out=e[:, OFF[t]:OFF[t + 1]], in0=tile(t), scalar=kth[:, t:t + 1],
                                                   in1=e[:, OFF[t]:OFF[t + 1]],
                                                   op0=ALU.is_ge, op1=ALU.mult).then_inc(e_cut, 1)

            slots(dve, LEAD, UNROLL, TOTAL, emit)



def mlp_gated_by_top2(core, name, xn, rinv, norm_dram, gate_dram, up_dram, down_dram, *, statistics):
    nc = core.nc
    ED, NE = 1024, 8
    BLK = 512
    BT = BLK // P
    NB = B * S // BLK
    EC = ED // P
    with Stage(core, name) as st:
        up_w = st.sb("up_w", [P, DC, ED])
        down_w = st.sb("down_w", [P, EC, D])
        gate_w = st.sb("gate_w", [P, DC, NE])
        n2 = st.sb("n2", [P, DC])
        xrow = st.sb("xrow", [P, BT, D])
        xt = st.sb("xt", [P, 2, DC, BLK])
        h = st.sb("h", [P, EC, BLK])
        gp = st.sb("gp", [P, BT, NE])
        gm, gs, top2, w = (st.sb(n, [P, BT]) for n in ("gm", "gs", "top2", "w"))
        best = st.sb("best", [P, BT, 8])
        up = st.ps("up", [P, 4, 512])
        dn = st.ps("dn", [P, 4, 512])
        row_full, tr_full, lg_full = st.sem("row_full"), st.sem("tr_full"), st.sem("lg_full")
        shifted, exp_full = st.sem("shifted"), st.sem("exp_full")
        up_full = st.sem("up_full")
        up_free = [st.sem(f"up_free{i}") for i in range(4)]
        dn_full, dn_used = st.sem("dn_full"), st.sem("dn_used")
        loads = []
        loads.append((gate_w[:], gate_dram.rearrange("(c p) n -> p c n", p=P)))
        loads.append((n2[:], norm_dram))
        loads.append((up_w[:], up_dram.rearrange("(c p) n -> p c n", p=P)))
        loads.append((down_w[:], down_dram.rearrange("(c p) n -> p c n", p=P)))
        statistics(loads)
        block = st.block()
        DN = BT + 3
        UPS = EC // 4

        def blocks(eng, emit):
            with eng.Fori(0, NB // 2 - 1) as i:
                emit(i * 2, 0, True)
                emit(i * 2 + 1, 1, True)
            emit(NB - 2, 0, True)
            emit(NB - 1, 1, False)

        def dn_before(k):
            return ONE + 3 + k * DN

        @block.tensor
        def _(pe):
            pe.sem_inc(tr_full, ONE)

            def prepare(k, parity, before):
                pe.wait_ge(dn_used, before)
                for t in range(BT):
                    pe.wait_ge(row_full, k * BT + t + 1)
                    for c in range(DC):
                        o = (c * 2 + t % 2) * P
                        last = nc.tensor.transpose(dn[:, t // 2, o:o + P], xrow[:, t, c * P:(c + 1) * P], core.ident[:])
                last.then_inc(tr_full, 1)
                pe.wait_ge(dn_used, before + 2)
                for t in range(BT):
                    for c in range(DC):
                        last = nc.tensor.matmul(dn[:, 2, t * NE:(t + 1) * NE], xt[:, parity, c, t * P:(t + 1) * P],
                                                gate_w[:, c, :], start=(c == 0), stop=(c == DC - 1))
                last.then_inc(lg_full, 1)

            def emit(k, parity, has_next):
                for u in range(EC):
                    pe.wait_ge(up_free[u % 4], ONE + k * UPS + u // 4)
                    for c in range(DC):
                        last = nc.tensor.matmul(up[:, u % 4, :], up_w[:, c, u * P:(u + 1) * P], xt[:, parity, c, :],
                                                start=(c == 0), stop=(c == DC - 1))
                    last.then_inc(up_full, 1)
                if has_next:
                    prepare(k + 1, 1 - parity, dn_before(k))
                for i in range(4):
                    pe.wait_ge(up_free[i], ONE + (k + 1) * UPS)
                pe.wait_ge(dn_used, dn_before(k) + 3 * has_next)
                for t in range(BT):
                    for m in range(EC):
                        last = nc.tensor.matmul(dn[:, t, 0:D], h[:, m, t * P:(t + 1) * P], down_w[:, m, :],
                                                start=(m == 0), stop=(m == EC - 1))
                    last.then_inc(dn_full, 1)

            prepare(0, 0, ONE)
            blocks(pe, emit)

        @block.scalar
        def _(act):
            act.sem_inc(dn_used, ONE)
            for i in range(4):
                act.sem_inc(up_free[i], ONE)

            def prepare(k, parity):
                act.wait_ge(tr_full, ONE + k + 1)
                for n in range(BT // 2):
                    for c in range(DC):
                        last = nc.scalar.activation(xt[:, parity, c, n * 2 * P:(n + 1) * 2 * P],
                                                    dn[:, n, c * 2 * P:(c + 1) * 2 * P],
                                                    ACT.Identity, scale=n2[:, c:c + 1])
                    last.then_inc(dn_used, 1)
                act.wait_ge(shifted, k + 1)
                nc.scalar.activation(gp[:], gp[:], ACT.Exp).then_inc(exp_full, 1)

            def emit(k, parity, has_next):
                for u in range(EC):
                    act.wait_ge(up_full, k * EC + u + 1)
                    nc.scalar.activation(h[:, u, :], up[:, u % 4, :], ACT.Silu).then_inc(up_free[u % 4], 1)
                if has_next:
                    prepare(k + 1, 1 - parity)

            prepare(0, 0)
            blocks(act, emit)

        @block.vector
        def _(dve):
            def over_experts(v):
                return v[:].rearrange("p (t a) -> p t a", a=1).to_broadcast([P, BT, NE])

            def rows(k):
                dve.wait_ge(tr_full, ONE + k)
                for t in range(BT):
                    nc.vector.tensor_scalar(xrow[:, t, :], xn[:, bass.ds(k * BT + t, 1), :].rearrange("p a d -> p (a d)"),
                                            rinv[:, bass.ds(k * BT + t, 1)], None, ALU.mult).then_inc(row_full, 1)

            def shift(k):
                dve.wait_ge(lg_full, k + 1)
                lg = dn[:, 2, 0:BT * NE].rearrange("p (t e) -> p t e", e=NE)
                nc.vector.tensor_reduce(gm[:], lg, AX.X, ALU.max)
                dve.drain()
                nc.vector.tensor_tensor(gp[:], lg, over_experts(gm), ALU.subtract).then_inc(dn_used, 1)
                dve.drain().then_inc(shifted, 1)

            def gates(k):
                dve.wait_ge(exp_full, k + 1)
                nc.vector.tensor_reduce(gs[:], gp[:], AX.X, ALU.add)
                dve.drain()
                nc.vector.reciprocal(gs[:], gs[:])
                dve.drain()
                nc.vector.tensor_tensor(gp[:], gp[:], over_experts(gs), ALU.mult)
                dve.drain()
                for t in range(BT):
                    nc.vector.max(best[:, t, :], gp[:, t, :])
                dve.drain()
                nc.vector.tensor_reduce(top2[:], best[:, :, 0:2], AX.X, ALU.add)
                dve.drain()
                nc.vector.tensor_scalar(w[:], top2[:], 1e-9, None, ALU.add)
                dve.drain()
                nc.vector.reciprocal(w[:], w[:])
                dve.drain()
                nc.vector.tensor_tensor(w[:], w[:], top2[:], ALU.mult)
                dve.drain()

            def emit(k, parity, has_next):
                if has_next:
                    rows(k + 1)
                    shift(k + 1)
                for t in range(BT):
                    nv = xn[:, bass.ds(k * BT + t, 1), :].rearrange("p a d -> p (a d)")
                    xv = core.x[:, bass.ds(k * BT + t, 1), :].rearrange("p a d -> p (a d)")
                    dve.wait_ge(dn_full, k * BT + t + 1)
                    nc.vector.scalar_tensor_tensor(out=nv, in0=dn[:, t, 0:D], scalar=w[:, t:t + 1], in1=nv,
                                                   op0=ALU.mult, op1=ALU.add).then_inc(dn_used, 1)
                    dve.drain()
                    nc.vector.tensor_tensor(xv, xv, nv, ALU.add)
                if has_next:
                    dve.drain()
                    gates(k + 1)

            rows(0)
            shift(0)
            gates(0)
            blocks(dve, emit)



def build(nc, a, out, upto=99):
    ctx = ExitStack()
    with ctx:
        core = Core(nc, ctx)
        qk_dram = nc.dram_tensor("qk", [2, 3, B * D, S], BF16, kind="Internal").ap()
        v_dram = nc.dram_tensor("v_rows", [HEADS, P, TB * VH], F32, kind="Internal").ap()
        o_dram = (nc.dram_tensor("o_transposed", [B * D, S], F32, kind="Internal").ap(),
                  nc.dram_tensor("o_sums", [HEADS, S], F32, kind="Internal").ap())
        load_and_constants(core, a["x"])

        def layernormed(dst, at):
            return nc.vector.tensor_scalar(dst, core.x[:, bass.ds(at, 1), :].rearrange("p a d -> p (a d)"),
                                           core.mean_var[:, bass.ds(at, 1), 0], core.rstd[:, bass.ds(at, 1)],
                                           ALU.subtract, ALU.mult)

        def of_rows(name):
            return lambda loads: layernorm_statistics(core, name + "_stat", loads)

        def l0_ffn(name):
            moe_shared_and_routed(core, name, a["router"], a["router_bias"], a["sw1"], a["sw3"], a["sw2"], a["ew1"], a["ew2"],
                                  statistics=of_rows(name))

        def l1_ffn(name):
            layernorm_statistics(core, name + "_stat")
            with Stage(core, name + "_rows") as st:
                xn = st.sb("xn", [P, NT, D])
                rinv = st.sb("rinv", [P, NT])
                layernorm_rows(core, name + "_ln", xn)

                def rms_rows(dst, at):
                    return nc.vector.tensor_scalar(dst, xn[:, bass.ds(at, 1), :].rearrange("p a d -> p (a d)"),
                                                   rinv[:, bass.ds(at, 1)], None, ALU.mult)

                project_qkv(core, name + "_qkv", a["f_qkv"], qk_dram, v_dram, rows=rms_rows, col_scale=a["n1"],
                            statistics=lambda loads: rms_statistics(core, name + "_rms1", xn, rinv, loads))
                softmax_heads(core, name + "_heads", qk_dram, v_dram, o_dram, causal=True)
                project_out(core, name + "_out", a["f_o"], o_dram, target=xn)
                mlp_gated_by_top2(core, name + "_mlp", xn, rinv, a["n2"], a["gate"], a["up"], a["down"],
                                  statistics=lambda loads: rms_statistics(core, name + "_rms2", xn, rinv, loads))

        stages = [
            lambda: holographic(core, a["holo_wt"], a["holo_wout"], a["dft"], statistics=of_rows("holo")),
            lambda: l0_ffn("ffn1"),
            lambda: delta_memory(core, a["kvq"], statistics=of_rows("delta")),
            lambda: l0_ffn("ffn2"),
            lambda: (project_qkv(core, "attn_a_qkv", a["a_qkv"], qk_dram, v_dram, rows=layernormed,
                                 statistics=of_rows("attn_a"), bias=(a["a_bqk"], a["a_bv"])),
                     softmax_heads(core, "attn_a_heads", qk_dram, v_dram, o_dram, causal=False),
                     project_out(core, "attn_a_out", a["a_out"], o_dram, target=core.x, out_bias=a["a_bout"])),
            lambda: l1_ffn("ffn3"),
            lambda: (project_qkv(core, "attn_b_qkv", a["b_qkv"], qk_dram, v_dram, rows=layernormed,
                                 statistics=of_rows("attn_b"),
                                 fancy=dict(taps=[a["tq"], a["tk"], a["tv"]], cos=a["cos"], sin=a["sin"],
                                            swap=a["swap"], gamma=a["gamma"], phase=a["phase"], theta=a["theta"])),
                     topk_heads(core, "attn_b_heads", qk_dram, v_dram, o_dram,
                                dict(quantiles=a["quantiles"], ranks=a["ranks"])),
                     project_out(core, "attn_b_out", a["b_proj"], o_dram, target=core.x, out_bias=a["b_bias"])),
            lambda: l1_ffn("ffn4"),
        ]
        for s in ([stages[i] for i in upto] if isinstance(upto, (list, tuple)) else stages[:upto]):
            s()
        store(core, out)


def shape_tables(np):
    n = np.arange(32)
    ang = 2 * np.pi * ((n[:, None] * n[None, :]) % 32) / 32
    eye = np.eye(4)
    fwd = [np.kron(eye, np.cos(ang)), np.kron(eye, -np.sin(ang))]
    dft = np.stack(fwd + [m / 32 for m in fwd]).astype(np.float32)
    inv_freq = np.float32(1.0) / np.power(np.float32(10000.0), np.arange(0, HD, 2, dtype=np.float32) / np.float32(HD))
    freqs = (np.arange(S, dtype=np.float32)[None, :] * inv_freq.astype(np.float32)[:, None]).astype(np.float32)
    r = np.arange(P)
    cos = np.cos(freqs.astype(np.float64))[(r % HD) // 2].astype(np.float32)
    sin = (np.sin(freqs.astype(np.float64))[(r % HD) // 2] * np.where(r % 2, 1.0, -1.0)[:, None]).astype(np.float32)
    swap = np.zeros((P, P), np.float32)
    swap[r, r ^ 1] = 1.0
    def quantile(p):
        lo, hi = -8.0, 8.0
        for _ in range(50):
            mid = (lo + hi) / 2
            lo, hi = (mid, hi) if 0.5 * (1 + erf(mid / sqrt(2))) < p else (lo, mid)
        return lo

    tabs = np.zeros((4, P, BUSY), np.float32)
    for t in range(1, TB):
        lo, hi, by = sampled(t)
        for row in range(P):
            n = t * P + row + 1
            z = quantile(1 - AIM / n)
            density = exp(-z * z / 2) / sqrt(2 * pi)
            tabs[:, row, t - 1] = (z, SPAN / (n * density), (t + 1) * P / 2 - AIM, 1.0 / len(range(lo, hi, by)))
    ranks = np.array([TOPK - 1 - k for k in range(8)] + [TOPK], np.float32)
    return {"quantiles": tabs, "ranks": ranks, "dft": dft, "cos": cos, "sin": sin, "swap": swap}


def layout(inputs, np):
    def arr(k):
        return np.asarray(inputs[k])

    def columns(v):
        return np.ascontiguousarray(v.reshape(-1, P).T)

    c = np.ascontiguousarray
    f = {
        "x": arr("L0_attn_a_x").reshape(B * S, D),
        "holo_wt": c(arr("L0_attn_a_w_qkv").T), "holo_wout": arr("L0_attn_a_w_out"),
        "router": c(arr("L0_ffn_router_w").T), "router_bias": arr("L0_ffn_router_bias"),
        "sw1": arr("L0_ffn_sw1"), "sw3": arr("L0_ffn_sw3"), "sw2": arr("L0_ffn_sw2"),
        "ew1": arr("L0_ffn_ew1"), "ew2": arr("L0_ffn_ew2"),
        "kvq": c(np.concatenate([arr("L0_attn_b_W_k").T, arr("L0_attn_b_W_v").T, arr("L0_attn_b_W_q").T], axis=1)),
        "a_qkv": arr("L1_attn_a_w_qkv"), "a_bqk": columns(arr("L1_attn_a_b_qkv")[0:2 * D]),
        "a_bv": arr("L1_attn_a_b_qkv")[2 * D:3 * D].reshape(1, D),
        "a_out": arr("L1_attn_a_w_out"), "a_bout": arr("L1_attn_a_b_out"),
        "b_qkv": c(arr("L1_attn_b_qkv_w").T), "b_proj": c(arr("L1_attn_b_proj_w").T), "b_bias": arr("L1_attn_b_proj_b"),
        "tq": arr("L1_attn_b_kernel_q"), "tk": arr("L1_attn_b_kernel_k"), "tv": arr("L1_attn_b_kernel_v"),
        "gamma": columns(arr("L1_attn_b_gamma_freq")), "theta": arr("L1_attn_b_theta_freq"), "phase": columns(arr("L1_attn_b_phase")),
        "n1": columns(arr("L1_ffn_n1_w")), "f_qkv": c(arr("L1_ffn_qkv_w").T), "f_o": c(arr("L1_ffn_o_w").T),
        "n2": columns(arr("L1_ffn_n2_w")), "gate": c(arr("L1_ffn_gate_w").T), "up": c(arr("L1_ffn_up_w").T),
        "down": c(arr("L1_ffn_down_w").T),
    }
    f.update(shape_tables(np))
    return f


def kernel(**inputs):
    import numpy as np
    import concourse.bacc as bacc
    from concourse.bass_utils import run_bass_kernel_spmd as run

    arrays = layout(inputs, np)
    nc = bacc.Bacc("TRN2", target_bir_lowering=False, num_devices=1)
    args = {k: nc.dram_tensor(f"in_{k}", v.shape, mybir.dt.from_np(v.dtype), kind="ExternalInput").ap()
            for k, v in arrays.items()}
    out = nc.dram_tensor("out", (B * S, D), F32, kind="ExternalOutput").ap()
    build(nc, args, out)
    r = run(nc, [{f"in_{k}": v for k, v in arrays.items()}], core_ids=[0])
    return r.results[0]["out"].reshape(B, S, D)
```
